# Optimizing a Trainium2 kernel written in Bass

```python
import numpy as np
import jax
import jax.numpy as jnp

def _softmax(x, axis=-1):
    return jax.nn.softmax(x, axis=axis)

def _gelu(x):
    return jax.nn.gelu(x, approximate=True)

def _silu(x):
    return jax.nn.silu(x)

def _sigmoid(x):
    return jax.nn.sigmoid(x)

def _layernorm(x, axis=-1, eps=1e-05):
    m = jnp.mean(x, axis=axis, keepdims=True)
    v = jnp.var(x, axis=axis, keepdims=True)
    return (x - m) / jnp.sqrt(v + eps)

def _scatter_add(tgt, idx, src, axis=0):
    return tgt.at[idx].add(src)

def _segment_sum(src, seg, n):
    return jax.ops.segment_sum(src, seg, n)
kernel_name = 'mk_adj_preln_d4_adj_r2_3fbf34'

def setup_inputs(seed: int=0):
    np.random.seed(seed)
    _w = jnp.asarray

    def _rec_inputs():
        import jax
        import jax.numpy as jnp
        _gk = jax.random.key(seed)
        x = -0.0005207 + 1.001 * jax.random.normal(jax.random.fold_in(_gk, 1), (8, 1024, 64), jnp.float32)
        _a = jax.random.bernoulli(jax.random.fold_in(_gk, 2), 0.00390625, (8, 1024, 1024))
        _a = jnp.logical_or(_a, jnp.swapaxes(_a, -1, -2))
        _a = jnp.logical_or(_a, jnp.eye(1024, dtype=bool))
        adj = _a.astype(jnp.int32)
        return (x, adj)
    x, adj = _rec_inputs()

    def _L0_gnn_setup():
        import jax, jax.numpy as jnp
        import numpy as np
        B, N, F_IN, F_OUT = (16, 1024, 64, 64)
        NEG = -1000000000.0
        key = jax.random.key(seed)
        k1, k2, k3, k4, k5 = jax.random.split(key, 5)
        x = jax.random.normal(k1, (B, N, F_IN), dtype=jnp.float32)
        adj = jax.random.randint(k2, (B, N, N), 0, 2, dtype=jnp.int32)
        W_q = jax.random.normal(k3, (F_IN, F_OUT), dtype=jnp.float32)
        W_k = jax.random.normal(k4, (F_IN, F_OUT), dtype=jnp.float32)
        W_v = jax.random.normal(k5, (F_IN, F_OUT), dtype=jnp.float32)
        return {'x': x, 'adj': adj, 'W_q': W_q, 'W_k': W_k, 'W_v': W_v}
    _L0_gnn_all = _L0_gnn_setup()
    _L0_gnn_in = {k: v for k, v in _L0_gnn_all.items() if k in ('W_q', 'W_k', 'W_v')}
    del _L0_gnn_all

    def _L1_gnn_setup():
        import jax, jax.numpy as jnp
        import numpy as np
        import math
        B, N, D, O, H = (2, 1536, 64, 64, 4)
        key = jax.random.key(seed)
        ks = jax.random.split(key, 8)
        x = jax.random.normal(ks[0], (B, N, D), dtype=jnp.float32)
        edge_index = jax.random.randint(ks[1], (B, N, N), 0, 2, dtype=jnp.int32)
        s = 1.0 / math.sqrt(D)
        Wv = jax.random.uniform(ks[2], (H, D, O), jnp.float32, -s, s)
        bv = jax.random.uniform(ks[3], (H, O), jnp.float32, -s, s)
        Wq = jax.random.uniform(ks[4], (H, D, O), jnp.float32, -s, s)
        bq = jax.random.uniform(ks[5], (H, O), jnp.float32, -s, s)
        Wk = jax.random.uniform(ks[6], (H, D, O), jnp.float32, -s, s)
        bk = jax.random.uniform(ks[7], (H, O), jnp.float32, -s, s)
        return {'x': x, 'edge_index': edge_index, 'Wv': Wv, 'bv': bv, 'Wq': Wq, 'bq': bq, 'Wk': Wk, 'bk': bk}
    _L1_gnn_all = _L1_gnn_setup()
    _L1_gnn_in = {k: v for k, v in _L1_gnn_all.items() if k in ('Wv', 'bv', 'Wq', 'bq', 'Wk', 'bk')}
    del _L1_gnn_all

    def _L2_gnn_setup():
        import jax, jax.numpy as jnp
        import numpy as np
        ALPHA = 0.2
        NEG_INF = -9000000000000000.0
        key = jax.random.key(seed)
        ks = jax.random.split(key, 6)
        B, N, F_IN, F_OUT = (4, 512, 64, 64)
        h = jax.random.normal(ks[0], (B, N, F_IN), dtype=jnp.float32)
        adj = jax.random.randint(ks[1], (B, N, N), 0, 2, dtype=jnp.int32)
        lin_w = jax.random.normal(ks[2], (F_OUT, F_IN), dtype=jnp.float32) * (1.0 / np.sqrt(F_IN))
        lin_b = jax.random.normal(ks[3], (F_OUT,), dtype=jnp.float32) * 0.02
        W_w = jax.random.normal(ks[4], (F_OUT, 2 * F_OUT), dtype=jnp.float32) * (1.0 / np.sqrt(2 * F_OUT))
        a = jax.random.normal(ks[5], (F_OUT, 1), dtype=jnp.float32) * (1.414 / np.sqrt(F_OUT))
        return {'h': h, 'adj': adj, 'lin_w': lin_w, 'lin_b': lin_b, 'W_w': W_w, 'a': a}
    _L2_gnn_all = _L2_gnn_setup()
    _L2_gnn_in = {k: v for k, v in _L2_gnn_all.items() if k in ('lin_w', 'lin_b', 'W_w', 'a')}
    del _L2_gnn_all

    def _L3_gnn_setup():
        import jax, jax.numpy as jnp
        import numpy as np
        B, N, F_IN, F_OUT = (8, 1024, 64, 64)
        ALPHA = 0.2
        NEG_INF = -9000000000000000.0
        LN_EPS = 1e-05
        key = jax.random.key(seed)
        ks = jax.random.split(key, 6)
        h = jax.random.normal(ks[0], (B, N, F_IN), dtype=jnp.float32)
        adj = jax.random.randint(ks[1], (B, N, N), 0, 2).astype(jnp.int32)
        adj = jnp.maximum(adj, jnp.eye(N, dtype=jnp.int32)[None])
        W = jax.random.normal(ks[2], (F_IN, F_OUT), dtype=jnp.float32) * 0.1
        a = jax.random.normal(ks[3], (2 * F_OUT,), dtype=jnp.float32) * 0.1
        W_res = jax.random.normal(ks[4], (F_IN, F_OUT), dtype=jnp.float32) * 0.1
        gamma = jnp.ones((F_OUT,), dtype=jnp.float32)
        beta = jnp.zeros((F_OUT,), dtype=jnp.float32)
        return {'h': h, 'adj': adj, 'W': W, 'a': a, 'W_res': W_res, 'gamma': gamma, 'beta': beta}
    _L3_gnn_all = _L3_gnn_setup()
    _L3_gnn_in = {k: v for k, v in _L3_gnn_all.items() if k in ('W', 'a', 'W_res', 'gamma', 'beta')}
    del _L3_gnn_all
    return {'x': x, 'adj': adj, 'L0_gnn_W_q': _L0_gnn_in['W_q'], 'L0_gnn_W_k': _L0_gnn_in['W_k'], 'L0_gnn_W_v': _L0_gnn_in['W_v'], 'L1_gnn_Wv': _L1_gnn_in['Wv'], 'L1_gnn_bv': _L1_gnn_in['bv'], 'L1_gnn_Wq': _L1_gnn_in['Wq'], 'L1_gnn_bq': _L1_gnn_in['bq'], 'L1_gnn_Wk': _L1_gnn_in['Wk'], 'L1_gnn_bk': _L1_gnn_in['bk'], 'L2_gnn_lin_w': _L2_gnn_in['lin_w'], 'L2_gnn_lin_b': _L2_gnn_in['lin_b'], 'L2_gnn_W_w': _L2_gnn_in['W_w'], 'L2_gnn_a': _L2_gnn_in['a'], 'L3_gnn_W': _L3_gnn_in['W'], 'L3_gnn_a': _L3_gnn_in['a'], 'L3_gnn_W_res': _L3_gnn_in['W_res'], 'L3_gnn_gamma': _L3_gnn_in['gamma'], 'L3_gnn_beta': _L3_gnn_in['beta']}

def reference(x, adj, L0_gnn_W_q, L0_gnn_W_k, L0_gnn_W_v, L1_gnn_Wv, L1_gnn_bv, L1_gnn_Wq, L1_gnn_bq, L1_gnn_Wk, L1_gnn_bk, L2_gnn_lin_w, L2_gnn_lin_b, L2_gnn_W_w, L2_gnn_a, L3_gnn_W, L3_gnn_a, L3_gnn_W_res, L3_gnn_gamma, L3_gnn_beta):
    import jax
    import jax.numpy as jnp

    def _L0_gnn_ref(x, adj, W_q, W_k, W_v):
        import jax, jax.numpy as jnp
        import numpy as np
        B, N, F_IN, F_OUT = (16, 1024, 64, 64)
        NEG = -1000000000.0
        Q = jnp.matmul(x, W_q)
        K = jnp.matmul(x, W_k)
        V = jnp.matmul(x, W_v)
        scale = 1.0 / jnp.sqrt(jnp.asarray(F_OUT, dtype=jnp.float32))
        scores = jnp.einsum('bnd,bmd->bnm', Q, K) * scale
        scores = jnp.where(adj == 0, jnp.asarray(NEG, scores.dtype), scores)
        attn = jax.nn.softmax(scores, axis=-1)
        out = jnp.matmul(attn, V)
        return out

    def _L1_gnn_ref(x, edge_index, Wv, bv, Wq, bq, Wk, bk):
        import jax, jax.numpy as jnp
        import numpy as np
        import math
        B, N, D, O, H = (2, 1536, 64, 64, 4)
        dk = jnp.asarray(math.sqrt(x.shape[-1]), x.dtype)
        v = jnp.einsum('bnd,hdo->bhno', x, Wv) + bv[None, :, None, :]
        q = jnp.einsum('bnd,hdo->bhno', x, Wq) + bq[None, :, None, :]
        k = jnp.einsum('bnd,hdo->bhno', x, Wk) + bk[None, :, None, :]
        scores = jnp.einsum('bhno,bhmo->bhnm', q, k) / dk
        scores = jax.nn.leaky_relu(scores, 0.2)
        mask = -10000000000.0 * (1.0 - edge_index.astype(scores.dtype))
        scores = scores + mask[:, None, :, :]
        prop = jax.nn.softmax(scores, axis=-1)
        feats = jnp.einsum('bhnm,bhmo->bhno', prop, v)
        out = jnp.mean(feats, axis=1)
        return jax.nn.leaky_relu(out, 0.2)

    def _L2_gnn_ref(h, adj, lin_w, lin_b, W_w, a):
        import jax, jax.numpy as jnp
        import numpy as np
        ALPHA = 0.2
        NEG_INF = -9000000000000000.0
        F_OUT = lin_w.shape[0]
        hp = jnp.einsum('bni,oi->bno', h, lin_w) + lin_b
        W1, W2 = (W_w[:, :F_OUT], W_w[:, F_OUT:])
        u = jnp.einsum('bnf,of->bno', hp, W1)
        v = jnp.einsum('bnf,of->bno', hp, W2)
        s = u[:, :, None, :] + v[:, None, :, :]
        s = jnp.where(s > 0, s, ALPHA * s)
        e = jnp.einsum('bijf,f->bij', s, a[:, 0])
        e = jnp.where(adj > 0, e, NEG_INF)
        attention = jax.nn.softmax(e, axis=2)
        h_prime = jnp.einsum('bij,bjf->bif', attention, hp)
        return jax.nn.elu(h_prime)

    def _L3_gnn_ref(h, adj, W, a, W_res, gamma, beta):
        import jax, jax.numpy as jnp
        import numpy as np
        B, N, F_IN, F_OUT = (8, 1024, 64, 64)
        ALPHA = 0.2
        NEG_INF = -9000000000000000.0
        LN_EPS = 1e-05
        Wh = h @ W
        src = Wh @ a[:F_OUT]
        dst = Wh @ a[F_OUT:]
        e = jax.nn.leaky_relu(src[:, :, None] + dst[:, None, :], ALPHA)
        e = jnp.where(adj > 0, e, NEG_INF)
        attention = jax.nn.softmax(e, axis=-1)
        h_prime = jnp.einsum('bij,bjf->bif', attention, Wh)
        h_prime = h_prime + h @ W_res
        h_prime = jax.nn.elu(h_prime)
        mean = jnp.mean(h_prime, axis=-1, keepdims=True)
        var = jnp.var(h_prime, axis=-1, keepdims=True)
        return (h_prime - mean) * jax.lax.rsqrt(var + LN_EPS) * gamma + beta
    h = jnp.maximum(_layernorm(x, axis=-1), 0.0)
    x = x + _L0_gnn_ref(h, adj, L0_gnn_W_q, L0_gnn_W_k, L0_gnn_W_v)
    h = jnp.maximum(_layernorm(x, axis=-1), 0.0)
    x = x + _L1_gnn_ref(h, adj, L1_gnn_Wv, L1_gnn_bv, L1_gnn_Wq, L1_gnn_bq, L1_gnn_Wk, L1_gnn_bk)
    h = jnp.maximum(_layernorm(x, axis=-1), 0.0)
    x = x + _L2_gnn_ref(h, adj, L2_gnn_lin_w, L2_gnn_lin_b, L2_gnn_W_w, L2_gnn_a)
    h = jnp.maximum(_layernorm(x, axis=-1), 0.0)
    x = x + _L3_gnn_ref(h, adj, L3_gnn_W, L3_gnn_a, L3_gnn_W_res, L3_gnn_gamma, L3_gnn_beta)
    return x

_drawn_inputs = setup_inputs


def setup_inputs(seed=0):
    import zlib

    import numpy as np

    out = dict(_drawn_inputs(seed))
    spreads = {'L3_gnn_gamma': (1.0, 0.2), 'L3_gnn_beta': (0.0, 0.646)}
    factors = {'L1_gnn_Wv': 3.624,
     'L1_gnn_bv': 8.0,
     'L1_gnn_Wq': 8.0,
     'L1_gnn_bq': 28.357,
     'L1_gnn_Wk': 8.0,
     'L1_gnn_bk': 64.0,
     'L2_gnn_lin_b': 8.0,
     'L2_gnn_W_w': 4.976,
     'L2_gnn_a': 4.356,
     'L3_gnn_a': 8.0}
    for name, (base, spread) in spreads.items():
        noise = np.random.default_rng([zlib.crc32(name.encode()), seed]).standard_normal(out[name].shape)
        drawn = base * np.exp(spread * noise) if base else spread * noise
        out[name] = jnp.asarray(drawn.astype(out[name].dtype))
    for name, factor in factors.items():
        out[name] = (out[name] * factor).astype(out[name].dtype)
    return out
```

```python
from contextlib import ExitStack

import concourse.bass as bass
from concourse import mybir

F32 = mybir.dt.float32
I32 = mybir.dt.int32
F16 = mybir.dt.float16
BF16 = mybir.dt.bfloat16
U8 = mybir.dt.uint8
ALU = mybir.AluOpType
ACT = mybir.ActivationFunctionType
AX = mybir.AxisListType

P = 128
BANK = 512
LN_EPS = 1e-05
MASKED = -float(2 ** 90)
SLOPE = 0.2
EXP_BITS = 0x7F800000
HIGH_BITS = -8192
RSQRT_MAGIC = float(0x5F3759DF)
F16_TOP = float(2 ** 14)
RING = 2


def wait(eng, sem, value):
    if not isinstance(value, int) or value > 0:
        eng.wait_ge(sem, value)


def hold_waits(eng, sems):
    eng.sem_inc(sems["passed"], 1)


class Shared:

    def __init__(self, nc, ctx, B, N, D):
        def sb(name, shape, dt):
            return ctx.enter_context(nc.sbuf_tensor(name, shape, dt))

        def ps(name, shape, dt):
            return ctx.enter_context(nc.psum_tensor(name, shape, dt))

        self.nc, self.B, self.N, self.D, self.NB = nc, B, N, D, N // P
        NB = self.NB
        self.x = sb("x_res", [P, B, NB, D], F32)
        self.adj8 = sb("adj8", [P, B * NB, N], U8)
        self.bytes = sb("bytes", [P, 2, N], U8)
        self.mask = sb("mask", [P, 2, N], BF16)
        self.probs_t = sb("probs_t", [P, NB, P], F32)
        self.y = sb("y", [P, 2, NB, D], F32)
        self.centred = sb("centred", [P, NB, D], F32)
        self.square = sb("square", [P, NB, D], F32)
        self.hT = sb("hT", [P, N], F32)
        self.stat = sb("stat", [P, 8, NB], F32)
        self.turned_out = sb("turned_out", [P, P], F32)
        self.ident = sb("ident", [P, P], F32)
        self.ident16 = sb("ident16", [P, P], BF16)
        self.add_halves = sb("add_halves", [P, D], F32)
        self.rowmax = sb("rowmax", [P, 4], F32)
        self.negmax = sb("negmax", [P, 4], F32)
        self.rowsum = sb("rowsum", [P, 4], F32)
        self.rinv = sb("rinv", [P, 4], F32)
        self.scores = ps("scores", [P, 2, 2, BANK], F32)
        self.turned = ps("turned", [P, NB, P], F32)
        self.outT = ps("outT", [P, BANK], F32)
        self.fill = ps("fill", [P, BANK], F32)

    def graph(self, b):
        return self.x[:, bass.ds(b, 1), :, :].rearrange("p a t d -> p (a t) d")

    def block(self, b, i):
        return self.x[:, bass.ds(b, 1), i, :].rearrange("p a d -> p (a d)")

    def edges(self, m):
        return self.adj8[:, bass.ds(m, 1), :].rearrange("p a n -> p (a n)")



def layer_norm_mean(v, s, sems, b, done):
    nc = s.nc
    wait(v, sems["rstd_ready"], done)
    nc.vector.tensor_reduce(s.stat[:, 0, :], s.graph(b), AX.X, ALU.add)
    v.drain()
    nc.vector.tensor_scalar(s.stat[:, 1, :], s.stat[:, 0, :], 1.0 / s.D, None, ALU.mult).then_inc(sems["mean_ready"], 1)


def layer_norm_centre(g, s, sems, b, done):
    nc = s.nc
    shape = [P, s.NB, s.D]
    g.wait_ge(sems["mean_ready"], done + 1)
    wait(g, sems["y_ready"], done)
    nc.gpsimd.tensor_tensor(s.centred[:], s.graph(b), s.stat[:, 1, :].unsqueeze(2).to_broadcast(shape),
                            ALU.subtract).then_inc(sems["centred_ready"], 1)
    g.wait_ge(sems["centred_ready"], done + 1)
    nc.gpsimd.tensor_tensor(s.square[:], s.centred[:], s.centred[:], ALU.mult).then_inc(sems["square_ready"], 1)


def rsqrt_of_variance(v, s, total, out):
    nc = s.nc
    var, g0, sq, half = (s.stat[:, i, :] for i in (3, 4, 5, 6))
    nc.vector.tensor_scalar(var, total, 1.0 / s.D, LN_EPS, ALU.mult, ALU.add)
    v.drain()
    nc.vector.tensor_scalar(sq.bitcast(I32), var.bitcast(I32), 1, None, ALU.logical_shift_right)
    v.drain()
    nc.vector.tensor_scalar(g0.bitcast(I32), sq.bitcast(I32), -1.0, RSQRT_MAGIC, ALU.mult, ALU.add)
    v.drain()
    for step in range(3):
        nc.vector.tensor_tensor(sq, g0, g0, ALU.mult)
        v.drain()
        nc.vector.scalar_tensor_tensor(out=half, in0=sq, scalar=-0.5, in1=var, op0=ALU.mult, op1=ALU.mult)
        v.drain()
        last = nc.vector.scalar_tensor_tensor(out=out if step == 2 else g0, in0=half, scalar=1.5, in1=g0,
                                              op0=ALU.add, op1=ALU.mult)
        if step < 2:
            v.drain()
    return last


def layer_norm_scale(v, s, sems, b, done):
    nc = s.nc
    v.wait_ge(sems["square_ready"], done + 1)
    nc.vector.tensor_reduce(s.stat[:, 2, :], s.square[:], AX.X, ALU.add)
    v.drain()
    rsqrt_of_variance(v, s, s.stat[:, 2, :], s.stat[:, 7, :]).then_inc(sems["rstd_ready"], 1)


def layer_norm_apply(g, s, sems, b, par, done, y_free):
    g.wait_ge(sems["rstd_ready"], done + 1)
    wait(g, sems["fill_ready"], y_free)
    s.nc.gpsimd.tensor_tensor(s.y[:, par, :, :], s.centred[:],
                              s.stat[:, 7, :].unsqueeze(2).to_broadcast([P, s.NB, s.D]),
                              ALU.mult).then_inc(sems["y_ready"], 1)


def turn_y(pe, s, par, half):
    for i in range(s.NB // 2):
        last = s.nc.tensor.matmul(s.fill[0:s.D, i * P:(i + 1) * P], s.y[:, par, half * s.NB // 2 + i, :], s.ident[:],
                                  start=True, stop=True, skip_group_check=True)
    return last


def turn_probs(pe, s, sems, probs, u):
    pe.wait_ge(sems["probs_ready"], u + 1)
    wait(pe, sems["half0_copied"], u)
    wait(pe, sems["half1_copied"], u)
    for j in range(s.NB):
        last = s.nc.tensor.transpose(s.turned[:, j, :], probs[:, j * P:(j + 1) * P], s.ident[:])
    last.then_inc(sems["turned_ready"], 1)


def probs_times_values(pe, s, sems, values, u):
    pe.wait_ge(sems["half0_copied"], u + 1)
    pe.wait_ge(sems["half1_copied"], u + 1)
    wait(pe, sems["out_copied"], u)
    for j in range(s.NB):
        half = j % 2
        last = s.nc.tensor.matmul(s.outT[half * s.D:(half + 1) * s.D, 0:P], values[:, j, :], s.probs_t[:, j, :],
                                  start=(j < 2), stop=(j >= s.NB - 2))
    last.then_inc(sems["out_ready"], 1)


def turn_out(pe, s, sems, u, fills_done):
    pe.wait_ge(sems["out_copied"], u + 1)
    wait(pe, sems["fill_copied"], fills_done)
    wait(pe, sems["unit_done"], u)
    s.nc.tensor.matmul(s.fill[:, 0:s.D], s.turned_out[:], s.add_halves[:], start=True,
                       stop=True).then_inc(sems["out_turned"], 1)


def copy_half(eng, copy, s, sems, half, u):
    eng.wait_ge(sems["turned_ready"], u + 1)
    n = s.NB // 2
    copy(s.probs_t[:, half * n:(half + 1) * n, :], s.turned[:, half * n:(half + 1) * n, :]
         ).then_inc(sems[f"half{half}_copied"], 1)


def copy_out(v, s, sems, u):
    v.wait_ge(sems["out_ready"], u + 1)
    s.nc.vector.tensor_copy(s.turned_out[:], s.outT[:, 0:P]).then_inc(sems["out_copied"], 1)


def load_bytes(sp, s, sems, m, slot):
    wait(sp, sems["mask_ready"], m - 1)
    sp.dma_start(s.bytes[:, slot, :], s.edges(m)).then_inc(sems[f"bytes_in{slot}"], 16)


def load_all_bytes(sp, s, sems):
    for i in range(2):
        load_bytes(sp, s, sems, i, i)
    with sp.Fori(1, s.B * s.NB // 2) as t:
        for i in range(2):
            load_bytes(sp, s, sems, 2 * t + i, i)


def mask_from(g, s, sems, edges, slot):
    hold_waits(g, sems)
    s.nc.gpsimd.tensor_scalar(s.mask[:, slot, :], edges, -1.0, -MASKED, ALU.add, ALU.mult
                              ).then_inc(sems["mask_ready"], 1)


def masked_max(v, s, sems, logits, slot, bias_scale, out, mask):
    hold_waits(v, sems)
    s.nc.vector.tensor_tensor_reduce(out=out, in0=logits, in1=mask, scale=1.0, scalar=-3e38, op0=ALU.add,
                                     op1=ALU.max, accum_out=s.rowmax[:, slot:slot + 1])
    v.drain()
    s.nc.vector.tensor_scalar(s.negmax[:, slot:slot + 1], s.rowmax[:, slot:slot + 1], bias_scale, None,
                              ALU.mult).then_inc(sems["logits_ready"], 1)


def exponentials(a, s, sems, logits, probs, slot, u, scale, buffers=2):
    a.wait_ge(sems["logits_ready"], u + 1)
    wait(a, sems["turned_ready"], u + 1 - buffers)
    s.nc.scalar.activation(probs, logits, ACT.Exp, bias=s.negmax[:, slot:slot + 1], scale=scale,
                           accum_out=s.rowsum[:, slot:slot + 1]).then_inc(sems["probs_ready"], 1)


UNIT_SEMS = ["scores_ready", "logits_ready", "probs_ready", "turned_ready", "half0_copied", "half1_copied",
             "out_ready", "out_copied", "out_turned", "unit_done", "mask_ready", "bytes_in0", "bytes_in1",
             "mean_ready", "centred_ready", "square_ready", "rstd_ready", "y_ready",
             "fill_ready", "high_ready", "fill_copied", "weights_in", "weights_ready", "passed"]


def make_sems(nc, ctx, layer, more=()):
    return {n: ctx.enter_context(nc.semaphore(f"{layer}_{n}")) for n in UNIT_SEMS + list(more)}



def dot_layer(nc, s, layer, heads, w_dram, b_dram, adj_dram=None, x_dram=None):
    B, N, D, NB, H = s.B, s.N, s.D, s.NB, heads
    U = NB * H
    leaky = H > 1
    QK = 2 * H
    K = 2 + 2 * QK + H
    LOADS = 2 if adj_dram is not None else 1
    with ExitStack() as ctx:
        def sb(name, shape, dt):
            return ctx.enter_context(nc.sbuf_tensor(f"{layer}_{name}", shape, dt))

        sems = make_sems(nc, ctx, layer, ["adj_packed", "bytes_stored0", "bytes_stored1", "x_in", "relu_ready", "bound_ready", "zeros_ready"]
                         + [f"adj_in{i}" for i in range(LOADS)])
        wqk = sb("wqk", [P, QK, 2, D], F32)
        wv = sb("wv", [P, H, D], F32)
        wabs = sb("wabs", [P, QK, D], F32)
        ones = sb("ones", [P, P], F32)
        bound = sb("bound", [P, 12], F32)
        q2 = sb("q2", [P, 2, H, N], F16)
        kh = sb("kh", [P, 2, H, N], F16)
        kl = sb("kl", [P, 2, H, N], F16)
        values = sb("values", [P, 2, NB, H, D], F32)
        logits = sb("logits", [P, 2, N], F32)
        probs = sb("probs", [P, 2, N], F32)
        relu4 = sb("relu4", [P, 2, N], F32) if leaky else None
        acc = sb("acc", [P, D], F32)
        leaked = sb("leaked", [P, D], F32)
        adj32 = sb("adj32", [P, 2, N], I32) if adj_dram is not None else None
        exp_scale, neg_scale = bound[:, 6:7], bound[:, 7:8]
        scores = [s.scores[:, i, :, :].rearrange("p a b -> p (a b)") for i in range(2)]
        WEIGHT_LOADS = 3 * H * (2 if b_dram else 1) + QK * (2 if b_dram else 1)
        block = ctx.enter_context(nc.Block())

        def fills_before(n):
            return min(K, n)

        @block.sync
        def _(sp):
            sp.wait_ge(sems["zeros_ready"], 1)
            for o in range(2):
                for h in range(H):
                    p = 2 * h + o
                    for twice in range(2):
                        sp.dma_start(wqk[0:D, p, twice, :], w_dram[o][h]).then_inc(sems["weights_in"], 16)
                        if b_dram:
                            sp.dma_start(wqk[D:D + 1, p, twice, :], b_dram[o][h]).then_inc(sems["weights_in"], 16)
            for h in range(H):
                sp.dma_start(wv[0:D, h, :], w_dram[2][h]).then_inc(sems["weights_in"], 16)
                if b_dram:
                    sp.dma_start(wv[D:D + 1, h, :], b_dram[2][h]).then_inc(sems["weights_in"], 16)
            if adj_dram is not None:
                for b in range(B):
                    sp.dma_start(s.x[:, b, :, :], x_dram[b].rearrange("(t p) d -> p t d", p=P)
                                 ).then_inc(sems["x_in"], 16)
                rows = adj_dram.rearrange("b n m -> (b n) m")

                def load(m, i):
                    sp.dma_start(adj32[:, i, :], rows[bass.ds(m * P, P), :]).then_inc(sems[f"adj_in{i}"], 16)

                def store_bytes(m, i):
                    sp.wait_ge(sems["adj_packed"], m + 1)
                    sp.dma_start(s.edges(m), s.bytes[:, i, :]).then_inc(sems[f"bytes_stored{i}"], 16)

                for i in range(2):
                    load(i, i)
                with sp.Fori(1, B * NB // 2) as t:
                    for i in range(2):
                        store_bytes(2 * t + i - 2, i)
                        sp.wait_ge(sems["mask_ready"], 2 * t + i - 1)
                        load(2 * t + i, i)
                for i in range(2):
                    store_bytes(B * NB - 2 + i, i)
                for i in range(2):
                    sp.wait_ge(sems[f"bytes_stored{i}"], 16 * B * NB // 2)
            else:
                load_all_bytes(sp, s, sems)

        @block.gpsimd
        def _(g):
            def mask(pair, i):
                m = 2 * pair + i
                if adj_dram is not None:
                    g.wait_ge(sems[f"adj_in{i}"], 16 * pair + 16)
                    wait(g, sems[f"bytes_stored{i}"], 16 * pair)
                    hold_waits(g, sems)
                    nc.gpsimd.tensor_scalar(s.bytes[:, i, :], adj32[:, i, :], 1.0, 0.0, ALU.mult, ALU.add
                                            ).then_inc(sems["adj_packed"], 1)
                else:
                    g.wait_ge(sems[f"bytes_in{i}"], 16 * pair + 16)
                if leaky:
                    wait(g, sems["scores_ready"], (m - 1) * H)
                else:
                    wait(g, sems["logits_ready"], m - 1)
                mask_from(g, s, sems, s.bytes[:, i, :] if adj_dram is None else adj32[:, i, :], i)

            def graph(b, par, norm):
                if norm:
                    layer_norm_centre(g, s, sems, b + 2, b + 2)
                for n in range(NB):
                    if norm and n == 3:
                        layer_norm_apply(g, s, sems, b + 2, par, b + 2, b * K + 2)
                    if norm or par == 0 or n + 2 < NB:
                        mask(b * (NB // 2) + n // 2 + 1, n % 2)

            if adj_dram is not None:
                g.wait_ge(sems["x_in"], 16 * B)
            for b in range(2):
                layer_norm_centre(g, s, sems, b, b)
                layer_norm_apply(g, s, sems, b, b, b, 0)
            mask(0, 0)
            mask(0, 1)
            with g.Fori(0, B // 2 - 1) as t:
                for par in range(2):
                    graph(2 * t + par, par, True)
            graph(B - 2, 0, False)
            graph(B - 1, 1, False)

        @block.tensor
        def _(pe):
            def fill(b, par, k, units):
                wait(pe, sems["fill_copied"], b * K + k)
                wait(pe, sems["unit_done"], units)
                if k < 2:
                    pe.wait_ge(sems["y_ready"], b + 1)
                    last = turn_y(pe, s, par, k)
                elif k < 2 + 2 * QK:
                    p, half = divmod(k - 2, 2)
                    last = nc.tensor.matmul(s.fill[:], wqk[:, p, :, :].rearrange("p a d -> p (a d)"),
                                            s.hT[:, half * BANK:(half + 1) * BANK], start=True, stop=True)
                else:
                    v = k - 2 - 2 * QK
                    each = NB // H
                    for i in range(each):
                        j = v * each + i
                        last = nc.tensor.matmul(s.fill[:, i * H * D:(i + 1) * H * D], s.hT[:, j * P:(j + 1) * P],
                                                wv[:].rearrange("p h d -> p (h d)"), start=True, stop=True,
                                                skip_group_check=True)
                last.then_inc(sems["fill_ready"], 1)

            def score(b, par, n, u):
                i, h = n // H, n % H
                wait(pe, sems["logits_ready"], u - 1)
                if leaky and h == 0:
                    pe.wait_ge(sems["mask_ready"], b * NB + i + 1)
                lhs = q2[:, par, h, i * P:(i + 1) * P]
                for half in range(2):
                    cols = slice(half * BANK, (half + 1) * BANK)
                    out = s.scores[:, n % 2, half, :]
                    nc.tensor.matmul(out, lhs, kh[:, par, h, cols], start=True, stop=False)
                    last = nc.tensor.matmul(out, lhs, kl[:, par, h, cols], start=False, stop=not leaky)
                    if leaky:
                        last = nc.tensor.matmul(out, s.ident16[:], s.mask[:, i % 2, cols], start=False, stop=True)
                last.then_inc(sems["scores_ready"], 1)

            def graph(b, par, project, last_graph):
                for n in range(U):
                    u = b * U + n
                    turn_probs(pe, s, sems, probs[:, n % 2, :], u)
                    if n > 0:
                        turn_out(pe, s, sems, u - 1, (b + 1) * K + (fills_before(n) if project else 0))
                    if n + 2 < U:
                        score(b, par, n + 2, u + 2)
                    elif not last_graph:
                        score(b + 1, 1 - par, n + 2 - U, u + 2)
                    if project:
                        for k in range(fills_before(n), fills_before(n + 1)):
                            fill(b + 1, 1 - par, k, u)
                    probs_times_values(pe, s, sems, values[:, par, :, n % H, :], u)
                turn_out(pe, s, sems, b * U + U - 1, (b + 1) * K + (K if project else 0))

            pe.wait_ge(sems["weights_ready"], 1)
            for p in range(2):
                nc.tensor.matmul(s.outT[:, p * H * D:(p + 1) * H * D], ones[:], wabs[:, p::2, :], start=True, stop=True,
                                 skip_group_check=True).then_inc(sems["bound_ready"], 1)
            pe.wait_ge(sems["weights_ready"], 2)
            for k in range(K):
                fill(0, 0, k, 0)
            wait(pe, sems["fill_copied"], K)
            score(0, 0, 0, 0)
            score(0, 0, 1, 1)
            with pe.Fori(0, B // 2 - 1) as t:
                for par in range(2):
                    graph(2 * t + par, par, True, False)
            graph(B - 2, 0, True, False)
            graph(B - 1, 1, False, True)

        @block.scalar
        def _(a):
            def high_part(b, par, k):
                if 2 <= k < 2 + 2 * QK:
                    p, half = divmod(k - 2, 2)
                    h, which = divmod(p, 2)
                    to = (q2, kh)[which]
                    a.wait_ge(sems["fill_ready"], b * K + k + 1)
                    nc.scalar.copy(to[:, par, h, half * BANK:(half + 1) * BANK], s.fill[:]
                                   ).then_inc(sems["high_ready"], 1)

            def relu(n, u):
                a.wait_ge(sems["scores_ready"], u + 1)
                wait(a, sems["logits_ready"], u - 1)
                nc.scalar.activation(relu4[:, n % 2, :], scores[n % 2], ACT.Relu, scale=1.0 / SLOPE - 1.0
                                     ).then_inc(sems["relu_ready"], 1)

            def graph(b, par, project, last_graph):
                for n in range(U):
                    u = b * U + n
                    copy_half(a, nc.scalar.copy, s, sems, 1, u)
                    if not (last_graph and n + 1 == U):
                        exponentials(a, s, sems, logits[:, (n + 1) % 2, :], probs[:, (n + 1) % 2, :],
                                     (n + 1) % 4, u + 1, exp_scale)
                    if project:
                        for k in range(fills_before(n), fills_before(n + 1)):
                            high_part(b + 1, 1 - par, k)
                    if leaky and not (last_graph and n + 2 >= U):
                        relu(n, u + 2)

            for k in range(K):
                high_part(0, 0, k)
            if leaky:
                relu(0, 0)
                relu(1, 1)
            exponentials(a, s, sems, logits[:, 0, :], probs[:, 0, :], 0, 0, exp_scale)
            with a.Fori(0, B // 2 - 1) as t:
                for par in range(2):
                    graph(2 * t + par, par, True, False)
            graph(B - 2, 0, True, False)
            graph(B - 1, 1, False, True)

        @block.vector
        def _(v):
            def take_fill(b, par, k):
                if k < 2:
                    v.wait_ge(sems["fill_ready"], b * K + k + 1)
                    last = nc.vector.tensor_scalar(s.hT[0:D, k * BANK:(k + 1) * BANK], s.fill[0:D, :], 0.0, None, ALU.max)
                elif k < 2 + 2 * QK:
                    p, half = divmod(k - 2, 2)
                    h, which = divmod(p, 2)
                    cols = slice(half * BANK, (half + 1) * BANK)
                    v.wait_ge(sems["high_ready"], b * 2 * QK + k - 2 + 1)
                    if which == 0:
                        low = q2[D:P, par, h, cols]
                        last = nc.vector.tensor_tensor(low, s.fill[D:P, :], low, ALU.subtract)
                    else:
                        last = nc.vector.tensor_tensor(kl[:, par, h, cols], s.fill[:], kh[:, par, h, cols], ALU.subtract)
                else:
                    v.wait_ge(sems["fill_ready"], b * K + k + 1)
                    each = NB // H
                    at = (k - 2 - 2 * QK) * each
                    last = nc.vector.tensor_copy(values[:, par, at:at + each, :, :].rearrange("p j h d -> p (j h d)"), s.fill[:])
                last.then_inc(sems["fill_copied"], 1)

            def logit(b, n, u):
                wait(v, sems["probs_ready"], u - 1)
                if leaky:
                    v.wait_ge(sems["relu_ready"], u + 1)
                    masked_max(v, s, sems, scores[n % 2], n % 4, neg_scale, logits[:, n % 2, :], relu4[:, n % 2, :])
                else:
                    v.wait_ge(sems["scores_ready"], u + 1)
                    v.wait_ge(sems["mask_ready"], u + 1)
                    masked_max(v, s, sems, scores[n % 2], n % 4, neg_scale, logits[:, n % 2, :], s.mask[:, n % 2, :])

            def finish(b, n, u):
                i, h = n // H, n % H
                slot = n % 4
                nc.vector.reciprocal(s.rinv[:, slot:slot + 1], s.rowsum[:, slot:slot + 1])
                v.drain()
                v.wait_ge(sems["out_turned"], u + 1)
                xb = s.block(b, i)
                if not leaky:
                    nc.vector.scalar_tensor_tensor(out=xb, in0=s.fill[:, 0:D], scalar=s.rinv[:, slot:slot + 1], in1=xb,
                                                   op0=ALU.mult, op1=ALU.add).then_inc(sems["unit_done"], 1)
                    return
                if h == 0:
                    nc.vector.tensor_scalar(acc[:], s.fill[:, 0:D], s.rinv[:, slot:slot + 1], None, ALU.mult
                                            ).then_inc(sems["unit_done"], 1)
                else:
                    nc.vector.scalar_tensor_tensor(out=acc[:], in0=s.fill[:, 0:D], scalar=s.rinv[:, slot:slot + 1],
                                                   in1=acc[:], op0=ALU.mult, op1=ALU.add).then_inc(sems["unit_done"], 1)
                if h == H - 1:
                    v.drain()
                    nc.vector.scalar_tensor_tensor(out=leaked[:], in0=acc[:], scalar=SLOPE, in1=acc[:], op0=ALU.mult, op1=ALU.max)
                    v.drain()
                    nc.vector.scalar_tensor_tensor(out=xb, in0=leaked[:], scalar=1.0 / H, in1=xb, op0=ALU.mult, op1=ALU.add)

            def graph(b, par, project, last_graph, norm=True):
                for n in range(U):
                    u = b * U + n
                    copy_half(v, nc.vector.tensor_copy, s, sems, 0, u)
                    if n > 0:
                        finish(b, n - 1, u - 1)
                    if not last_graph or n + 1 < U:
                        logit(b, (n + 1) % U, u + 1)
                    if project:
                        for k in range(fills_before(n), fills_before(n + 1)):
                            take_fill(b + 1, 1 - par, k)
                    if norm and n == 0:
                        layer_norm_mean(v, s, sems, b + 2, b + 2)
                    if norm and n == 2:
                        layer_norm_scale(v, s, sems, b + 2, b + 2)
                    copy_out(v, s, sems, u)
                finish(b, U - 1, b * U + U - 1)

            nc.vector.memset(wqk[D:P, :, :, :], 0.0)
            nc.vector.memset(wv[D:P, :, :], 0.0).then_inc(sems["zeros_ready"], 1)
            if adj_dram is not None:
                v.wait_ge(sems["x_in"], 16 * B)
                nc.vector.memset(s.hT[D:P, :], 0.0)
                v.drain()
                nc.vector.memset(s.hT[D:D + 1, :], 1.0)
            nc.vector.memset(ones[:], 0.0)
            v.drain()
            nc.vector.memset(ones[0:D, :], float(D) ** 0.5)
            v.drain()
            nc.vector.memset(ones[D:D + 1, :], 1.0)
            v.wait_ge(sems["weights_in"], 16 * WEIGHT_LOADS)
            nc.vector.scalar_tensor_tensor(out=wabs[:], in0=wqk[:, :, 0, :], scalar=-1.0, in1=wqk[:, :, 0, :],
                                           op0=ALU.mult, op1=ALU.max).then_inc(sems["weights_ready"], 1)
            v.wait_ge(sems["bound_ready"], 2)
            for p in range(2):
                nc.vector.tensor_reduce(bound[:, p:p + 1], s.outT[:, p * H * D:(p + 1) * H * D], AX.X, ALU.max)
            v.drain()
            nc.vector.tensor_scalar(bound[:, 2:4], bound[:, 0:2], 1e-20, None, ALU.max)
            v.drain()
            nc.vector.tensor_scalar(bound[:, 0:2].bitcast(I32), bound[:, 2:4].bitcast(I32), EXP_BITS, None, ALU.bitwise_and)
            v.drain()
            nc.vector.reciprocal(bound[:, 2:4], bound[:, 0:2])
            v.drain()
            nc.vector.tensor_scalar(bound[:, 4:6], bound[:, 2:4], F16_TOP, None, ALU.mult)
            nc.vector.tensor_scalar(bound[:, 8:9], bound[:, 0:1], bound[:, 1:2],
                                    (SLOPE if leaky else 1.0) * float(D) ** -0.5 / F16_TOP ** 2, ALU.mult, ALU.mult)
            v.drain()
            nc.vector.tensor_copy(exp_scale, bound[:, 8:9])
            nc.vector.tensor_scalar(neg_scale, bound[:, 8:9], -1.0, None, ALU.mult)
            for o in range(2):
                last = nc.vector.tensor_scalar(wqk[:, o::2, :, :], wqk[:, o::2, :, :], bound[:, 4 + o:5 + o], None, ALU.mult)
            last.then_inc(sems["weights_ready"], 1)
            for b in range(2):
                layer_norm_mean(v, s, sems, b, b)
                layer_norm_scale(v, s, sems, b, b)
            for k in range(K):
                take_fill(0, 0, k)
            logit(0, 0, 0)
            with v.Fori(0, B // 2 - 1) as t:
                for par in range(2):
                    graph(2 * t + par, par, True, False)
            graph(B - 2, 0, True, False, norm=False)
            graph(B - 1, 1, False, True, norm=False)



def elu_parts(v, s, sems, z, low, high):
    s.nc.vector.tensor_scalar(low[:], z, 0.0, None, ALU.min)
    s.nc.vector.tensor_scalar(high[:], z, 0.0, -1.0, ALU.max, ALU.add).then_inc(sems["elu_parts"], 1)


def elu_exp(a, s, sems, low, b):
    a.wait_ge(sems["elu_parts"], b + 1)
    s.nc.scalar.activation(low[:], low[:], ACT.Exp).then_inc(sems["elu_exp"], 1)



def additive_layer(nc, s, lin_w, lin_b, W_w, a_w):
    B, N, D, NB = s.B, s.N, s.D, s.NB
    K = 9
    G, ROWS = 4, 32
    SETS = ROWS // 2
    PAIRS = P // 2
    WIN = 2 * ROWS - 2
    with ExitStack() as ctx:
        def sb(name, shape, dt):
            return ctx.enter_context(nc.sbuf_tensor(f"l2_{name}", shape, dt))

        sems = make_sems(nc, ctx, "l2", ["vector_sets", "scalar_sets", "set_summed", "coded", "elu_parts", "elu_exp",
                                         "raw_turned", "x_added"])
        raw = sb("raw", [D, 3, D], F32)
        lwT = sb("lwT", [P, D], F32)
        w1 = sb("w1", [P, 2, D], F32)
        w2 = sb("w2", [P, 2, D], F32)
        acol = sb("acol", [P, 4], F32)
        ones = sb("ones", [P, P], F32)
        hpT = sb("hpT", [P, N], F32)
        w = sb("w", [P, 2, N], F32)
        r = sb("r", [P, 2, N // 2], F32)
        w_code = sb("w_code", [P, 2, N], F32)
        r_code = sb("r_code", [P, 2, N // 2], F32)
        scaled = sb("scaled", [P, N], F32)
        cut = sb("cut", [P, N], F32)
        rng = sb("rng", [P, 12], F32)
        signs = sb("signs", [P, WIN], F32)
        signs_code = sb("signs_code", [P, 2, WIN], BF16)
        quarter = sb("quarter", [P, 2, P], BF16)
        ring = sb("ring", [P, RING, G, N], F32)
        values = sb("values", [P, 2, NB, D], F32)
        logits = sb("logits", [P, N], F32)
        probs = sb("probs", [P, N], F32)
        z = sb("z", [P, NB, D], F32)
        low = sb("low", [P, NB, D], F32)
        high = sb("high", [P, NB, D], F32)
        scores = [s.scores[:, i, :, :].rearrange("p a b -> p (a b)") for i in range(2)]
        block = ctx.enter_context(nc.Block())

        def parts(t):
            return t.bitcast(F16).rearrange("p (n two) -> p n two", two=2)

        def on_scalar(k):
            return {(k // 2) % G} if k % 2 == 0 else {(k // 2) % G, (k // 2 + 2) % G}

        TURN, MULTIPLY, TURN_OUT = 3, 6, 9
        MAX, COPY, COPY_OUT, FINISH = 1, 5, 8, 11
        EXP = 2
        FILL_AT = {0: 0, 2: 1, 4: 2, 6: 3, 11: 4, 13: 5}
        TAKE_AT = {k + 2: i for k, i in FILL_AT.items()}
        FILLS = {1: (0, 6), NB - 2: (6, K)}

        def fills_of(n, project):
            first, end = FILLS.get(n, (0, 0))
            return (first, end - first) if project else (0, 0)

        @block.sync
        def _(sp):
            sp.wait_ge(sems["weights_ready"], 1)
            for dst, src in ((raw[:, 0, :], lin_w), (raw[:, 1, :], W_w[:, 0:D]), (raw[:, 2, :], W_w[:, D:2 * D]),
                             (acol[0:D, 0:1], a_w), (acol[D:P, 0:1], a_w),
                             (lwT[D:D + 1, :], lin_b.rearrange("(a d) -> a d", a=1))):
                sp.dma_start(dst, src).then_inc(sems["weights_in"], 16)
            load_all_bytes(sp, s, sems)

        @block.gpsimd
        def _(g):
            def mask(pair, i):
                g.wait_ge(sems[f"bytes_in{i}"], 16 * pair + 16)
                wait(g, sems["logits_ready"], 2 * pair + i - 1)
                mask_from(g, s, sems, s.bytes[:, i, :], i)

            def elu_add(b):
                g.wait_ge(sems["elu_exp"], b + 1)
                nc.gpsimd.tensor_tensor(high[:], high[:], low[:], ALU.add).then_inc(sems["x_added"], 1)
                g.wait_ge(sems["x_added"], 2 * b + 1)
                nc.gpsimd.tensor_tensor(s.graph(b), s.graph(b), high[:], ALU.add).then_inc(sems["x_added"], 1)

            def graph(b, par, norm, project):
                for n in range(2, NB):
                    mask(b * (NB // 2) + n // 2, n % 2)
                    if norm and n == NB - 1:
                        layer_norm_centre(g, s, sems, b + 2, b + 2)
                        layer_norm_apply(g, s, sems, b + 2, par, b + 2, b * K + 2)
                if project:
                    mask((b + 1) * (NB // 2), 0)
                    mask((b + 1) * (NB // 2), 1)
                elu_add(b)

            for b in range(2):
                layer_norm_centre(g, s, sems, b, b)
                layer_norm_apply(g, s, sems, b, b, b, 0)
            mask(0, 0)
            mask(0, 1)
            with g.Fori(0, B // 2 - 1) as t:
                for par in range(2):
                    graph(2 * t + par, par, True, True)
            graph(B - 2, 0, False, True)
            graph(B - 1, 1, False, False)

        @block.tensor
        def _(pe):
            def fill(b, par, k, units):
                wait(pe, sems["fill_copied"], b * K + k)
                wait(pe, sems["unit_done"], units)
                both = [slice(h * BANK, (h + 1) * BANK) for h in range(2)]
                if k < 2:
                    pe.wait_ge(sems["y_ready"], b + 1)
                    last = turn_y(pe, s, par, k)
                elif k < 4:
                    last = nc.tensor.matmul(s.fill[0:D, :], lwT[:], s.hT[:, both[k - 2]], start=True, stop=True)
                elif k < 8:
                    lhs = (w2 if k < 6 else w1)[:].rearrange("p a d -> p (a d)")
                    last = nc.tensor.matmul(s.fill[:], lhs, hpT[:, both[k % 2]], start=True, stop=True)
                else:
                    for j in range(NB):
                        last = nc.tensor.matmul(s.fill[:, j * D:(j + 1) * D], s.hT[:, j * P:(j + 1) * P], lwT[:],
                                                start=True, stop=True, skip_group_check=True)
                last.then_inc(sems["fill_ready"], 1)

            def run(b, par, n, u, buf, fills, issued, before=True):
                first, count = fills
                wait(pe, sems["logits_ready"], u - 1)
                pe.wait_ge(sems["coded"], b + 1)
                for half in range(2):
                    for part in range(2):
                        nc.tensor.matmul(s.scores[:, buf, half, :], quarter[:, par, :],
                                         parts(w_code[:, par, half * BANK:(half + 1) * BANK])[:, :, part],
                                         start=(part == 0), stop=False, skip_group_check=True)
                for k in range(SETS):
                    pe.wait_ge(sems["vector_sets"], SETS * u + k + 1)
                    pe.wait_ge(sems["scalar_sets"], SETS * u + k + 1)
                    window = slice(WIN - ROWS - 2 * k, WIN - 2 * k)
                    for half in range(2):
                        cols = slice(half * BANK, (half + 1) * BANK)
                        for part in range(2):
                            for g in range(G):
                                out = s.scores[g * ROWS:(g + 1) * ROWS, buf, half, :]
                                if g in on_scalar(k):
                                    if part == 0:
                                        last = nc.tensor.matmul(out, signs[:, window], ring[:, k % RING, g, cols],
                                                                start=False, stop=(k == SETS - 1), skip_group_check=True)
                                else:
                                    last = nc.tensor.matmul(out, signs_code[:, par, window],
                                                            parts(ring[:, k % RING, g, cols])[:, :, part], start=False,
                                                            stop=(k == SETS - 1 and part == 1), skip_group_check=True)
                    last.then_inc(sems["set_summed"], 1)
                    if k in FILL_AT and FILL_AT[k] < count:
                        fill(b + 1, 1 - par, first + FILL_AT[k], u if k > TURN_OUT else u - 1)
                        issued += 1
                    if not before:
                        continue
                    prev = par if not (isinstance(n, int) and n == 0) else 1 - par
                    if k == TURN:
                        turn_probs(pe, s, sems, probs, u - 1)
                    if k == MULTIPLY:
                        probs_times_values(pe, s, sems, values[:, prev, :, :], u - 1)
                    if k == TURN_OUT:
                        turn_out(pe, s, sems, u - 1, issued)
                return issued

            def graph(b, par, project, last_graph):
                done = (b + 1) * K
                done = run(b, par, 1, b * NB + 1, 1, fills_of(1, project), done)
                with pe.Fori(0, (NB - 4) // 2) as t:
                    for i in range(2):
                        run(b, par, 2 * t + 2 + i, b * NB + 2 * t + 2 + i, i, (0, 0), done)
                done = run(b, par, NB - 2, b * NB + NB - 2, 0, fills_of(NB - 2, project), done)
                done = run(b, par, NB - 1, b * NB + NB - 1, 1, (0, 0), done)
                if not last_graph:
                    run(b + 1, 1 - par, 0, (b + 1) * NB, 0, (0, 0), done)

            pe.wait_ge(sems["weights_ready"], 2)
            for i in range(3):
                last = nc.tensor.transpose(s.fill[0:D, i * D:(i + 1) * D], raw[:, i, :], s.ident[0:D, 0:D])
            last.then_inc(sems["raw_turned"], 1)
            pe.wait_ge(sems["weights_ready"], 3)
            for k in range(K):
                fill(0, 0, k, 0)
            run(0, 0, 0, 0, 0, (0, 0), K, before=False)
            with pe.Fori(0, B // 2 - 1) as t:
                for par in range(2):
                    graph(2 * t + par, par, True, False)
            graph(B - 2, 0, True, False)
            graph(B - 1, 1, False, True)
            last = B * NB - 1
            turn_probs(pe, s, sems, probs, last)
            probs_times_values(pe, s, sems, values[:, 1, :, :], last)
            turn_out(pe, s, sems, last, B * K)

        @block.scalar
        def _(a):
            def run(b, par, n, u, buf, before=True):
                slot = 1 - buf
                a.wait_ge(sems["fill_copied"], (b + 1) * K)
                for k in range(SETS):
                    wait(a, sems["set_summed"], SETS * u + k - RING + 1)
                    for g in sorted(on_scalar(k)):
                        last = nc.scalar.activation(ring[:, k % RING, g, :], w[:, par, :], ACT.Relu,
                                                    bias=r[:, par, bass.ds(n * PAIRS + g * SETS + k, 1)])
                    last.then_inc(sems["scalar_sets"], 1)
                    if not before:
                        continue
                    if k == EXP:
                        exponentials(a, s, sems, logits[:], probs[:], slot, u - 1, 1.0, buffers=1)
                    if k == COPY:
                        copy_half(a, nc.scalar.copy, s, sems, 1, u - 1)
                    if k == FINISH + 2 and isinstance(n, int) and n == 0:
                        elu_exp(a, s, sems, low, b - 1)

            def graph(b, par, last_graph):
                run(b, par, 1, b * NB + 1, 1)
                with a.Fori(0, (NB - 4) // 2) as t:
                    for i in range(2):
                        run(b, par, 2 * t + 2 + i, b * NB + 2 * t + 2 + i, i)
                for n in (NB - 2, NB - 1):
                    run(b, par, n, b * NB + n, n % 2)
                if not last_graph:
                    run(b + 1, 1 - par, 0, (b + 1) * NB, 0)

            run(0, 0, 0, 0, 0, before=False)
            with a.Fori(0, B // 2 - 1) as t:
                for par in range(2):
                    graph(2 * t + par, par, False)
            graph(B - 2, 0, False)
            graph(B - 1, 1, True)
            exponentials(a, s, sems, logits[:], probs[:], 1, B * NB - 1, 1.0, buffers=1)
            copy_half(a, nc.scalar.copy, s, sems, 1, B * NB - 1)
            elu_exp(a, s, sems, low, B - 1)

        @block.vector
        def _(v):
            def take_fill(b, par, k):
                v.wait_ge(sems["fill_ready"], b * K + k + 1)
                half = slice((k % 2) * BANK, (k % 2 + 1) * BANK)
                if k < 2:
                    last = nc.vector.tensor_scalar(s.hT[0:D, half], s.fill[0:D, :], 0.0, None, ALU.max)
                elif k < 4:
                    last = nc.vector.tensor_copy(hpT[0:D, half], s.fill[0:D, :])
                elif k < 6:
                    last = nc.vector.tensor_scalar(w[:, par, half], s.fill[:], acol[:, 2:3], None, ALU.mult)
                elif k < 8:
                    pairs = slice((k % 2) * BANK // 2, (k % 2 + 1) * BANK // 2)
                    for odd in range(2):
                        rows = slice(odd * D, (odd + 1) * D)
                        last = nc.vector.tensor_scalar(r[rows, par, pairs],
                                                       s.fill[rows, :].rearrange("p (n two) -> p n two", two=2)[:, :, odd],
                                                       acol[rows, 2:3], None, ALU.mult)
                else:
                    last = nc.vector.tensor_copy(values[:, par, :, :].rearrange("p j d -> p (j d)"), s.fill[:])
                last.then_inc(sems["fill_copied"], 1)

            def find_range(par):
                for i, t in enumerate((w[:, par, :], r[:, par, :])):
                    nc.vector.tensor_reduce(rng[:, 2 * i:2 * i + 1], t, AX.X, ALU.max)
                    nc.vector.tensor_reduce(rng[:, 2 * i + 1:2 * i + 2], t, AX.X, ALU.min)
                v.drain()
                nc.vector.scalar_tensor_tensor(out=rng[:, 4:6], in0=rng[:, 1:4:2], scalar=-1.0, in1=rng[:, 0:4:2],
                                               op0=ALU.mult, op1=ALU.max)
                v.drain()
                nc.vector.tensor_scalar(rng[:, 6:7], rng[:, 4:5], rng[:, 5:6], 1e-30, ALU.max, ALU.max)
                v.drain()
                nc.vector.tensor_scalar(rng[:, 7:8].bitcast(I32), rng[:, 6:7].bitcast(I32), EXP_BITS, None, ALU.bitwise_and)
                v.drain()
                nc.vector.reciprocal(rng[:, 8:9], rng[:, 7:8])
                v.drain()
                nc.vector.tensor_scalar(rng[:, 9:10], rng[:, 8:9], F16_TOP, None, ALU.mult)
                nc.vector.tensor_scalar(rng[:, 10:11], rng[:, 8:9], -F16_TOP, None, ALU.mult)
                nc.vector.tensor_scalar(rng[:, 11:12], rng[:, 7:8], 1.0 / F16_TOP, None, ALU.mult)
                v.drain()

            def code(src, dst, scale):
                n = src.shape[-1]
                nc.vector.tensor_scalar(scaled[:, 0:n], src, scale, None, ALU.mult)
                v.drain()
                nc.vector.tensor_scalar(cut[:, 0:n].bitcast(I32), scaled[:, 0:n].bitcast(I32), HIGH_BITS, None, ALU.bitwise_and)
                v.drain()
                nc.vector.tensor_copy(parts(dst)[:, :, 1], cut[:, 0:n])
                nc.vector.tensor_tensor(parts(dst)[:, :, 0], scaled[:, 0:n], cut[:, 0:n], ALU.subtract)
                v.drain()

            def code_signs(par):
                for odd in range(2):
                    rows = slice(odd * D, (odd + 1) * D)
                    nc.vector.tensor_scalar(signs_code[rows, par, ROWS - 2 + odd:ROWS - 1 + odd], acol[rows, 1:2],
                                            rng[rows, 11:12], None, ALU.mult)
                nc.vector.tensor_scalar(quarter[:, par, :], ones[:], acol[:, 3:4], rng[:, 11:12], ALU.mult, ALU.mult
                                        ).then_inc(sems["coded"], 1)

            def run(b, par, n, u, buf, fills, before=True, norm=False, encode=False):
                first, count = fills
                for k in range(SETS):
                    wait(v, sems["set_summed"], SETS * u + k - RING + 1)
                    for g in range(G):
                        if g not in on_scalar(k):
                            last = nc.vector.tensor_scalar(ring[:, k % RING, g, :], w_code[:, par, :],
                                                           r_code[:, par, bass.ds(n * PAIRS + g * SETS + k, 1)], None,
                                                           ALU.max)
                    last.then_inc(sems["vector_sets"], 1)
                    if k in TAKE_AT and TAKE_AT[k] < count:
                        take_fill(b + 1, 1 - par, first + TAKE_AT[k])
                    if norm and k == 2:
                        layer_norm_mean(v, s, sems, b + 2, b + 2)
                    if norm and k == 6:
                        layer_norm_scale(v, s, sems, b + 2, b + 2)
                    if encode and k == 3:
                        find_range(1 - par)
                    if encode and k == 7:
                        code(w[:, 1 - par, :], w_code[:, 1 - par, :], rng[:, 9:10])
                    if encode and k == 10:
                        code(r[:, 1 - par, :], r_code[:, 1 - par, :], rng[:, 10:11])
                    if encode and k == 13:
                        code_signs(1 - par)
                    if not before:
                        continue
                    if k == MAX:
                        logit(1 - buf, u - 1)
                    if k == COPY:
                        copy_half(v, nc.vector.tensor_copy, s, sems, 0, u - 1)
                    if k == COPY_OUT:
                        copy_out(v, s, sems, u - 1)
                    if k == FINISH:
                        at_start = isinstance(n, int) and n == 0
                        finish(NB - 1 if at_start else n - 1, 1 - buf, u - 1)
                        if at_start:
                            batch_end(b - 1)

            def batch_end(b):
                v.drain()
                wait(v, sems["x_added"], 2 * b)
                elu_parts(v, s, sems, z[:], low, high)

            def logit(buf, u):
                v.wait_ge(sems["set_summed"], SETS * (u + 1))
                v.wait_ge(sems["mask_ready"], u + 1)
                wait(v, sems["probs_ready"], u)
                masked_max(v, s, sems, scores[buf], buf, -1.0, logits[:], s.mask[:, buf, :])

            def finish(n, slot, u):
                nc.vector.reciprocal(s.rinv[:, slot:slot + 1], s.rowsum[:, slot:slot + 1])
                v.drain()
                v.wait_ge(sems["out_turned"], u + 1)
                nc.vector.tensor_scalar(z[:, bass.ds(n, 1), :].rearrange("p a d -> p (a d)"), s.fill[:, 0:D],
                                        s.rinv[:, slot:slot + 1], None, ALU.mult).then_inc(sems["unit_done"], 1)

            def graph(b, par, project, last_graph, norm):
                run(b, par, 1, b * NB + 1, 1, fills_of(1, project))
                with v.Fori(0, (NB - 4) // 2) as t:
                    for i in range(2):
                        run(b, par, 2 * t + 2 + i, b * NB + 2 * t + 2 + i, i, (0, 0))
                run(b, par, NB - 2, b * NB + NB - 2, 0, fills_of(NB - 2, project))
                run(b, par, NB - 1, b * NB + NB - 1, 1, (0, 0), norm=norm, encode=project)
                if not last_graph:
                    run(b + 1, 1 - par, 0, (b + 1) * NB, 0, (0, 0))

            nc.vector.memset(lwT[D:P, :], 0.0)
            nc.vector.memset(w1[D:P, :, :], 0.0)
            nc.vector.memset(w2[D:P, :, :], 0.0)
            nc.vector.memset(hpT[D:P, :], 0.0)
            nc.vector.memset(ones[:], 1.0)
            nc.vector.memset(signs[:], 0.0)
            nc.vector.memset(signs_code[:], 0.0).then_inc(sems["weights_ready"], 1)
            v.wait_ge(sems["weights_in"], 16 * 6)
            v.drain()
            nc.vector.tensor_scalar(acol[:, 1:2], acol[:, 0:1], 0.0, 2.0, ALU.is_ge, ALU.mult).then_inc(sems["weights_ready"], 1)
            v.drain()
            nc.vector.tensor_scalar(acol[:, 3:4], acol[:, 1:2], -1.0, None, ALU.add)
            v.drain()
            nc.vector.tensor_copy(acol[:, 1:2], acol[:, 3:4])
            nc.vector.scalar_tensor_tensor(out=acol[:, 2:3], in0=acol[:, 0:1], scalar=1.0 - SLOPE, in1=acol[:, 3:4],
                                           op0=ALU.mult, op1=ALU.mult)
            v.drain()
            nc.vector.tensor_scalar(acol[:, 3:4], acol[:, 1:2], SLOPE / (1.0 - SLOPE) / 2, None, ALU.mult)
            for odd in range(2):
                rows = slice(odd * D, (odd + 1) * D)
                nc.vector.tensor_copy(signs[rows, ROWS - 2 + odd:ROWS - 1 + odd], acol[rows, 1:2])
            v.wait_ge(sems["raw_turned"], 1)
            nc.vector.tensor_copy(lwT[0:D, :], s.fill[0:D, 0:D])
            for twice in range(2):
                nc.vector.tensor_copy(w1[0:D, twice, :], s.fill[0:D, D:2 * D])
                last = nc.vector.tensor_copy(w2[0:D, twice, :], s.fill[0:D, 2 * D:3 * D])
            last.then_inc(sems["weights_ready"], 1)
            for b in range(2):
                layer_norm_mean(v, s, sems, b, b)
                layer_norm_scale(v, s, sems, b, b)
            for k in range(K):
                take_fill(0, 0, k)
            v.drain()
            find_range(0)
            code(w[:, 0, :], w_code[:, 0, :], rng[:, 9:10])
            code(r[:, 0, :], r_code[:, 0, :], rng[:, 10:11])
            code_signs(0)
            run(0, 0, 0, 0, 0, (0, 0), before=False)
            with v.Fori(0, B // 2 - 1) as t:
                for par in range(2):
                    graph(2 * t + par, par, True, False, True)
            graph(B - 2, 0, True, False, False)
            graph(B - 1, 1, False, True, False)
            u = B * NB - 1
            logit(1, u)
            copy_half(v, nc.vector.tensor_copy, s, sems, 0, u)
            copy_out(v, s, sems, u)
            finish(NB - 1, 1, u)
            batch_end(B - 1)



def gat_layer(nc, s, w_dram, a_dram, w_res, gamma_dram, beta_dram, out):
    B, N, D, NB = s.B, s.N, s.D, s.NB
    K = 9
    with ExitStack() as ctx:
        def sb(name, shape, dt):
            return ctx.enter_context(nc.sbuf_tensor(f"l3_{name}", shape, dt))

        sems = make_sems(nc, ctx, "l3", ["leaky_ready", "elu_parts", "elu_exp", "elu_ready", "out_mean", "out_centred",
                                         "out_square", "out_rstd", "out_steps", "x_done", "stored"])
        w = sb("w", [P, D], F32)
        wres = sb("wres", [P, D], F32)
        acol = sb("acol", [P, 2], F32)
        gamma = sb("gamma", [P, D], F32)
        beta = sb("beta", [P, D], F32)
        ones = sb("ones", [P, P], F32)
        a_dst = sb("a_dst", [P, P], F32)
        whT = sb("whT", [P, N], F32)
        dst = sb("dst", [P, 2, N], F32)
        dst_slope = sb("dst_slope", [P, 2, N], F32)
        src = sb("src", [P, 2, NB], F32)
        values = sb("values", [P, 2, NB, D], F32)
        residual = sb("residual", [P, 2, NB, D], F32)
        leaky = sb("leaky", [P, 2, N], F32)
        logits = sb("logits", [P, 2, N], F32)
        probs = sb("probs", [P, 2, N], F32)
        z = sb("z", [P, 2, NB, D], F32)
        low = sb("low", [P, NB, D], F32)
        high = sb("high", [P, NB, D], F32)
        work = sb("work", [P, 4, NB, D], F32)
        total = sb("total", [P, 4, NB], F32)
        block = ctx.enter_context(nc.Block())

        def fills_before(n):
            return -(-K * n // NB)

        @block.sync
        def _(sp):
            sp.wait_ge(sems["weights_ready"], 1)
            for to, at in ((w[0:D, :], w_dram), (wres[0:D, :], w_res),
                           (acol[0:D, 0:1], a_dram[0:D].rearrange("(d a) -> d a", a=1)),
                           (acol[0:D, 1:2], a_dram[D:2 * D].rearrange("(d a) -> d a", a=1)),
                           (gamma[:], gamma_dram.partition_broadcast(P)), (beta[:], beta_dram.partition_broadcast(P))):
                sp.dma_start(to, at).then_inc(sems["weights_in"], 16)

            def store(b):
                sp.wait_ge(sems["x_done"], b + 1)
                sp.dma_start(out[bass.ds(b, 1)].rearrange("a (t p) d -> p (a t) d", p=P), s.graph(b)
                             ).then_inc(sems["stored"], 16)

            def loads(b, first):
                for n in range(first, NB):
                    load_bytes(sp, s, sems, b * NB + n, n % 2)

            load_bytes(sp, s, sems, 0, 0)
            load_bytes(sp, s, sems, 1, 1)
            loads(0, 2)
            with sp.Fori(1, B) as b:
                loads(b, 0)
                store(b - 1)
            store(B - 1)
            sp.wait_ge(sems["stored"], 16 * B)

        @block.gpsimd
        def _(g):
            shape = [P, NB, D]

            def mask(pair, i):
                g.wait_ge(sems[f"bytes_in{i}"], 16 * pair + 16)
                wait(g, sems["logits_ready"], 2 * pair + i - 1)
                mask_from(g, s, sems, s.bytes[:, i, :], i)

            def out_centre(b):
                centred, square, elu = (work[:, i, :, :] for i in range(3))
                g.wait_ge(sems["out_mean"], b + 1)
                nc.gpsimd.tensor_tensor(centred, elu, total[:, 1, :].unsqueeze(2).to_broadcast(shape), ALU.subtract
                                        ).then_inc(sems["out_centred"], 1)
                g.wait_ge(sems["out_centred"], b + 1)
                nc.gpsimd.tensor_tensor(square, centred, centred, ALU.mult).then_inc(sems["out_square"], 1)

            def out_scale(b):
                t = [work[:, i, :, :] for i in range(4)]
                g.wait_ge(sems["out_rstd"], b + 1)
                nc.gpsimd.tensor_tensor(t[3], t[0], total[:, 3, :].unsqueeze(2).to_broadcast(shape), ALU.mult
                                        ).then_inc(sems["out_steps"], 1)
                g.wait_ge(sems["out_steps"], 3 * b + 1)
                nc.gpsimd.tensor_tensor(t[1], t[3], gamma[:].unsqueeze(1).to_broadcast(shape), ALU.mult
                                        ).then_inc(sems["out_steps"], 1)
                g.wait_ge(sems["out_steps"], 3 * b + 2)
                nc.gpsimd.tensor_tensor(t[3], t[1], beta[:].unsqueeze(1).to_broadcast(shape), ALU.add
                                        ).then_inc(sems["out_steps"], 1)
                g.wait_ge(sems["out_steps"], 3 * b + 3)
                nc.gpsimd.tensor_tensor(s.graph(b), s.graph(b), t[3], ALU.add).then_inc(sems["x_done"], 1)

            def graph(b, par, norm):
                if norm:
                    layer_norm_centre(g, s, sems, b + 2, b + 2)
                for n in range(NB):
                    if norm and n == 3:
                        layer_norm_apply(g, s, sems, b + 2, par, b + 2, b * K + 2)
                    if norm or par == 0 or n + 2 < NB:
                        mask(b * (NB // 2) + n // 2 + 1, n % 2)
                out_centre(b)
                out_scale(b)

            for b in range(2):
                layer_norm_centre(g, s, sems, b, b)
                layer_norm_apply(g, s, sems, b, b, b, 0)
            mask(0, 0)
            mask(0, 1)
            with g.Fori(0, B // 2 - 1) as t:
                for par in range(2):
                    graph(2 * t + par, par, True)
            graph(B - 2, 0, False)
            graph(B - 1, 1, False)

        @block.tensor
        def _(pe):
            def fill(b, par, k, units):
                wait(pe, sems["fill_copied"], b * K + k)
                wait(pe, sems["unit_done"], units)
                cols = slice((k % 2) * BANK, (k % 2 + 1) * BANK)
                if k < 2:
                    pe.wait_ge(sems["y_ready"], b + 1)
                    last = turn_y(pe, s, par, k)
                elif k < 4:
                    last = nc.tensor.matmul(s.fill[0:D, :], w[:], s.hT[:, cols], start=True, stop=True)
                elif k < 6:
                    last = nc.tensor.matmul(s.fill[:], a_dst[:], whT[:, cols], start=True, stop=True)
                else:
                    for j in range(NB):
                        nodes = slice(j * P, (j + 1) * P)
                        if k == 6:
                            out_, lhs, rhs = s.fill[:, j:j + 1], whT[:, nodes], acol[:, 0:1]
                        else:
                            out_, lhs, rhs = s.fill[:, j * D:(j + 1) * D], s.hT[:, nodes], (w if k == 7 else wres)[:]
                        last = nc.tensor.matmul(out_, lhs, rhs, start=True, stop=True, skip_group_check=True)
                last.then_inc(sems["fill_ready"], 1)

            def graph(b, par, project):
                for n in range(NB):
                    u = b * NB + n
                    turn_probs(pe, s, sems, probs[:, n % 2, :], u)
                    if n > 0:
                        turn_out(pe, s, sems, u - 1, (b + 1) * K + (fills_before(n) if project else 0))
                    if project:
                        for k in range(fills_before(n), fills_before(n + 1)):
                            fill(b + 1, 1 - par, k, u)
                    probs_times_values(pe, s, sems, values[:, par, :, :], u)
                turn_out(pe, s, sems, b * NB + NB - 1, (b + 1) * K + (K if project else 0))

            pe.wait_ge(sems["weights_ready"], 2)
            for k in range(K):
                fill(0, 0, k, 0)
            with pe.Fori(0, B // 2 - 1) as t:
                for par in range(2):
                    graph(2 * t + par, par, True)
            graph(B - 2, 0, True)
            graph(B - 1, 1, False)

        @block.scalar
        def _(a):
            def dst_fill(b, par, k):
                if k in (4, 5):
                    a.wait_ge(sems["fill_ready"], b * K + k + 1)
                    nc.scalar.copy(dst[:, par, (k % 2) * BANK:(k % 2 + 1) * BANK], s.fill[:]).then_inc(sems["high_ready"], 1)

            def graph(b, par, project, last_graph):
                for n in range(NB):
                    u = b * NB + n
                    copy_half(a, nc.scalar.copy, s, sems, 0, u)
                    copy_half(a, nc.scalar.copy, s, sems, 1, u)
                    if not (last_graph and n + 1 == NB):
                        exponentials(a, s, sems, logits[:, (n + 1) % 2, :], probs[:, (n + 1) % 2, :], (n + 1) % 4, u + 1, 1.0)
                    if project:
                        for k in range(fills_before(n), fills_before(n + 1)):
                            dst_fill(b + 1, 1 - par, k)
                elu_exp(a, s, sems, low, b)

            for k in range(K):
                dst_fill(0, 0, k)
            exponentials(a, s, sems, logits[:, 0, :], probs[:, 0, :], 0, 0, 1.0)
            with a.Fori(0, B // 2 - 1) as t:
                for par in range(2):
                    graph(2 * t + par, par, True, False)
            graph(B - 2, 0, True, False)
            graph(B - 1, 1, False, True)

        @block.vector
        def _(v):
            def take_fill(b, par, k):
                cols = slice((k % 2) * BANK, (k % 2 + 1) * BANK)
                if k in (4, 5):
                    v.wait_ge(sems["high_ready"], b * 2 + k - 4 + 1)
                    last = nc.vector.tensor_scalar(dst_slope[:, par, cols], s.fill[:], SLOPE, None, ALU.mult)
                else:
                    v.wait_ge(sems["fill_ready"], b * K + k + 1)
                    if k < 2:
                        last = nc.vector.tensor_scalar(s.hT[0:D, cols], s.fill[0:D, :], 0.0, None, ALU.max)
                    elif k < 4:
                        last = nc.vector.tensor_copy(whT[0:D, cols], s.fill[0:D, :])
                    elif k == 6:
                        last = nc.vector.tensor_scalar(src[:, par, :], s.fill[:, 0:NB], 1.0 - SLOPE, None, ALU.mult)
                    else:
                        to = values if k == 7 else residual
                        last = nc.vector.tensor_copy(to[:, par, :, :].rearrange("p j d -> p (j d)"), s.fill[:])
                last.then_inc(sems["fill_copied"], 1)

            def logit(par, n, u):
                wait(v, sems["logits_ready"], u - 1)
                nc.vector.scalar_tensor_tensor(out=leaky[:, n % 2, :], in0=dst[:, par, :], scalar=src[:, par, n:n + 1],
                                               in1=dst_slope[:, par, :], op0=ALU.add, op1=ALU.max
                                               ).then_inc(sems["leaky_ready"], 1)
                v.wait_ge(sems["mask_ready"], u + 1)
                v.wait_ge(sems["leaky_ready"], u + 1)
                wait(v, sems["probs_ready"], u - 1)
                masked_max(v, s, sems, leaky[:, n % 2, :], n % 4, -1.0, logits[:, n % 2, :], s.mask[:, n % 2, :])

            def finish(par, n, u):
                slot = n % 4
                nc.vector.reciprocal(s.rinv[:, slot:slot + 1], s.rowsum[:, slot:slot + 1])
                v.drain()
                v.wait_ge(sems["out_turned"], u + 1)
                nc.vector.scalar_tensor_tensor(out=z[:, par, n, :], in0=s.fill[:, 0:D], scalar=s.rinv[:, slot:slot + 1],
                                               in1=residual[:, par, n, :], op0=ALU.mult, op1=ALU.add
                                               ).then_inc(sems["unit_done"], 1)

            def out_mean(b):
                wait(v, sems["x_done"], b)
                v.wait_ge(sems["elu_exp"], b + 1)
                nc.vector.tensor_tensor(work[:, 2, :, :], high[:], low[:], ALU.add)
                v.drain()
                nc.vector.tensor_reduce(total[:, 0, :], work[:, 2, :, :], AX.X, ALU.add)
                v.drain()
                nc.vector.tensor_scalar(total[:, 1, :], total[:, 0, :], 1.0 / D, None, ALU.mult).then_inc(sems["out_mean"], 1)

            def out_rstd(b):
                v.wait_ge(sems["out_square"], b + 1)
                nc.vector.tensor_reduce(total[:, 2, :], work[:, 1, :, :], AX.X, ALU.add)
                v.drain()
                rsqrt_of_variance(v, s, total[:, 2, :], total[:, 3, :]).then_inc(sems["out_rstd"], 1)

            def graph(b, par, project, last_graph, norm=True):
                for n in range(NB):
                    u = b * NB + n
                    if n > 0:
                        finish(par, n - 1, u - 1)
                    if n + 1 < NB:
                        logit(par, n + 1, u + 1)
                    elif not last_graph:
                        logit(1 - par, 0, u + 1)
                    if project:
                        for k in range(fills_before(n), fills_before(n + 1)):
                            take_fill(b + 1, 1 - par, k)
                    if norm and n == 0:
                        layer_norm_mean(v, s, sems, b + 2, b + 2)
                    if norm and n == 2:
                        layer_norm_scale(v, s, sems, b + 2, b + 2)
                    copy_out(v, s, sems, u)
                finish(par, NB - 1, b * NB + NB - 1)
                v.drain()
                wait(v, sems["x_done"], b)
                elu_parts(v, s, sems, z[:, par, :, :], low, high)
                out_mean(b)
                out_rstd(b)

            nc.vector.memset(w[D:P, :], 0.0)
            nc.vector.memset(wres[D:P, :], 0.0)
            nc.vector.memset(acol[:], 0.0)
            nc.vector.memset(ones[:], 1.0)
            nc.vector.memset(whT[D:P, :], 0.0).then_inc(sems["weights_ready"], 1)
            v.wait_ge(sems["weights_in"], 16 * 6)
            v.drain()
            nc.vector.tensor_scalar(a_dst[:], ones[:], acol[:, 1:2], None, ALU.mult).then_inc(sems["weights_ready"], 1)
            for b in range(2):
                layer_norm_mean(v, s, sems, b, b)
                layer_norm_scale(v, s, sems, b, b)
            for k in range(K):
                take_fill(0, 0, k)
            v.drain()
            logit(0, 0, 0)
            with v.Fori(0, B // 2 - 1) as t:
                for par in range(2):
                    graph(2 * t + par, par, True, False)
            graph(B - 2, 0, True, False, norm=False)
            graph(B - 1, 1, False, True, norm=False)



def gnn_stack(nc, x, adj, L0_gnn_W_q, L0_gnn_W_k, L0_gnn_W_v, L1_gnn_Wv, L1_gnn_bv, L1_gnn_Wq, L1_gnn_bq,
              L1_gnn_Wk, L1_gnn_bk, L2_gnn_lin_w, L2_gnn_lin_b, L2_gnn_W_w, L2_gnn_a, L3_gnn_W, L3_gnn_a,
              L3_gnn_W_res, L3_gnn_gamma, L3_gnn_beta, out):
    B, N, D = x.shape
    H = L1_gnn_Wq.shape[0]
    with ExitStack() as ctx:
        s = Shared(nc, ctx, B, N, D)
        constants(nc, s)
        dot_layer(nc, s, "l0", 1, [[L0_gnn_W_q], [L0_gnn_W_k], [L0_gnn_W_v]], None, adj, x)
        dot_layer(nc, s, "l1", H, [[w[h] for h in range(H)] for w in (L1_gnn_Wq, L1_gnn_Wk, L1_gnn_Wv)],
                  [[w[h:h + 1, :] for h in range(H)] for w in (L1_gnn_bq, L1_gnn_bk, L1_gnn_bv)])
        additive_layer(nc, s, L2_gnn_lin_w, L2_gnn_lin_b, L2_gnn_W_w, L2_gnn_a)
        gat_layer(nc, s, L3_gnn_W, L3_gnn_a, L3_gnn_W_res, L3_gnn_gamma, L3_gnn_beta, out)


def constants(nc, s):
    with nc.semaphore("zeroed") as zeroed, nc.semaphore("ones_ready") as ones_ready, nc.Block() as block:
        @block.vector
        def _(v):
            nc.vector.memset(s.ident[:], 0.0).then_inc(zeroed, 1)
            v.wait_ge(ones_ready, 2)
            nc.vector.tensor_copy(s.ident16[:], s.ident[:])
            nc.vector.tensor_tensor(s.add_halves[:], s.ident[:, 0:s.D], s.ident[:, s.D:2 * s.D], ALU.add)

        @block.gpsimd
        def _(g):
            g.wait_ge(zeroed, 1)
            nc.gpsimd.affine_select(out=s.ident[:], in_=s.ident[:], compare_op=ALU.not_equal, fill=1.0, base=0,
                                    pattern=[[-1, P]], channel_multiplier=1).then_inc(ones_ready, 2)


_INS = ["x", "adj", "L0_gnn_W_q", "L0_gnn_W_k", "L0_gnn_W_v", "L1_gnn_Wv", "L1_gnn_bv", "L1_gnn_Wq", "L1_gnn_bq",
        "L1_gnn_Wk", "L1_gnn_bk", "L2_gnn_lin_w", "L2_gnn_lin_b", "L2_gnn_W_w", "L2_gnn_a", "L3_gnn_W", "L3_gnn_a",
        "L3_gnn_W_res", "L3_gnn_gamma", "L3_gnn_beta"]


def kernel(**inputs):
    import numpy as np
    import concourse.bacc as bacc
    from concourse.bass_utils import run_bass_kernel_spmd

    nc = bacc.Bacc("TRN2", target_bir_lowering=False, num_devices=1)
    arrays = {name: np.ascontiguousarray(inputs[name]) for name in _INS}
    args = [nc.dram_tensor(name, a.shape, mybir.dt.from_np(a.dtype), kind="ExternalInput").ap()
            for name, a in arrays.items()]
    out = nc.dram_tensor("out", arrays["x"].shape, F32, kind="ExternalOutput").ap()
    gnn_stack(nc, *args, out)
    result = run_bass_kernel_spmd(nc, [arrays], core_ids=[0])
    return result.results[0]["out"]
```

```python
from contextlib import ExitStack

import concourse.bass as bass
from concourse import mybir

F32 = mybir.dt.float32
I32 = mybir.dt.int32
F16 = mybir.dt.float16
BF16 = mybir.dt.bfloat16
U8 = mybir.dt.uint8
ALU = mybir.AluOpType
ACT = mybir.ActivationFunctionType
AX = mybir.AxisListType

P = 128
BANK = 512
LN_EPS = 1e-05
MASKED = -float(2 ** 90)
SLOPE = 0.2
EXP_BITS = 0x7F800000
HIGH_BITS = -8192
RSQRT_MAGIC = float(0x5F3759DF)
F16_TOP = float(2 ** 14)
STARTS = 1
RING = 3


def wait(eng, sem, value):
    if not isinstance(value, int) or value > 0:
        eng.wait_ge(sem, value)


def hold_waits(eng, sems):
    eng.sem_inc(sems["passed"], 1)


class Shared:

    def __init__(self, nc, ctx, B, N, D):
        def sb(name, shape, dt):
            return ctx.enter_context(nc.sbuf_tensor(name, shape, dt))

        def ps(name, shape, dt):
            return ctx.enter_context(nc.psum_tensor(name, shape, dt))

        self.nc, self.B, self.N, self.D, self.NB = nc, B, N, D, N // P
        NB = self.NB
        self.x = sb("x_res", [P, B, NB, D], F32)
        self.adj8 = sb("adj8", [P, B * NB, N], U8)
        self.bytes = sb("bytes", [P, 2, N], U8)
        self.mask = sb("mask", [P, 2, N], BF16)
        self.probs_t = sb("probs_t", [P, NB, P], F32)
        self.y = sb("y", [P, 2, NB, D], F32)
        self.centred = sb("centred", [P, NB, D], F32)
        self.square = sb("square", [P, NB, D], F32)
        self.hT = sb("hT", [P, N], F32)
        self.stat = sb("stat", [P, 8, NB], F32)
        self.turned_out = sb("turned_out", [P, P], F32)
        self.ident = sb("ident", [P, P], F32)
        self.add_halves = sb("add_halves", [P, D], F32)
        self.rowmax = sb("rowmax", [P, 4], F32)
        self.negmax = sb("negmax", [P, 4], F32)
        self.rowsum = sb("rowsum", [P, 4], F32)
        self.rinv = sb("rinv", [P, 4], F32)
        self.scores = ps("scores", [P, 2, 2, BANK], F32)
        self.turned = ps("turned", [P, NB, P], F32)
        self.outT = ps("outT", [P, BANK], F32)
        self.fill = ps("fill", [P, BANK], F32)

    def graph(self, b):
        return self.x[:, bass.ds(b, 1), :, :].rearrange("p a t d -> p (a t) d")

    def block(self, b, i):
        return self.x[:, bass.ds(b, 1), i, :].rearrange("p a d -> p (a d)")

    def edges(self, m):
        return self.adj8[:, bass.ds(m, 1), :].rearrange("p a n -> p (a n)")



def layer_norm_mean(v, s, sems, b, done):
    nc = s.nc
    wait(v, sems["y_ready"], done)
    nc.vector.tensor_reduce(s.stat[:, 0, :], s.graph(b), AX.X, ALU.add)
    v.drain()
    nc.vector.tensor_scalar(s.stat[:, 1, :], s.stat[:, 0, :], 1.0 / s.D, None, ALU.mult).then_inc(sems["mean_ready"], 1)


def layer_norm_centre(g, s, sems, b, done):
    nc = s.nc
    shape = [P, s.NB, s.D]
    g.wait_ge(sems["mean_ready"], done + 1)
    wait(g, sems["y_ready"], done)
    nc.gpsimd.tensor_tensor(s.centred[:], s.graph(b), s.stat[:, 1, :].unsqueeze(2).to_broadcast(shape),
                            ALU.subtract).then_inc(sems["centred_ready"], 1)
    g.wait_ge(sems["centred_ready"], done + 1)
    nc.gpsimd.tensor_tensor(s.square[:], s.centred[:], s.centred[:], ALU.mult).then_inc(sems["square_ready"], 1)


def rsqrt_seed(v, s, stat, total):
    nc = s.nc
    half, guess, var = (stat[:, i, :] for i in (3, 4, 5))
    nc.vector.tensor_scalar(var, total, 1.0 / s.D, LN_EPS, ALU.mult, ALU.add)
    v.drain()
    nc.vector.tensor_scalar(half, var, -0.5, None, ALU.mult)
    nc.vector.tensor_scalar(var.bitcast(I32), var.bitcast(I32), 1, None, ALU.logical_shift_right)
    v.drain()
    return nc.vector.tensor_scalar(guess.bitcast(I32), var.bitcast(I32), -1.0, RSQRT_MAGIC, ALU.mult, ALU.add)


def rsqrt_newton(g, s, stat, out):
    nc = s.nc
    half, guess, square, product = (stat[:, i, :] for i in (3, 4, 5, 6))
    for step in range(3):
        nc.gpsimd.tensor_tensor(square, guess, guess, ALU.mult)
        g.drain()
        nc.gpsimd.tensor_tensor(product, square, half, ALU.mult)
        g.drain()
        nc.gpsimd.tensor_scalar(square, product, 1.0, 1.5, ALU.mult, ALU.add)
        g.drain()
        nc.gpsimd.tensor_tensor(out if step == 2 else guess, square, guess, ALU.mult)
        g.drain()


def layer_norm_scale(v, s, sems, b, done):
    nc = s.nc
    v.wait_ge(sems["square_ready"], done + 1)
    nc.vector.tensor_reduce(s.stat[:, 2, :], s.square[:], AX.X, ALU.add)
    v.drain()
    rsqrt_seed(v, s, s.stat, s.stat[:, 2, :]).then_inc(sems["seed_ready"], 1)


def layer_norm_apply(g, s, sems, b, par, done, y_free):
    g.wait_ge(sems["seed_ready"], done + 1)
    rsqrt_newton(g, s, s.stat, s.stat[:, 7, :])
    wait(g, sems["fill_ready"], y_free)
    s.nc.gpsimd.tensor_tensor(s.y[:, par, :, :], s.centred[:],
                              s.stat[:, 7, :].unsqueeze(2).to_broadcast([P, s.NB, s.D]),
                              ALU.mult).then_inc(sems["y_ready"], 1)


def turn_y(pe, s, par, half):
    for i in range(s.NB // 2):
        last = s.nc.tensor.matmul(s.fill[0:s.D, i * P:(i + 1) * P], s.y[:, par, half * s.NB // 2 + i, :], s.ident[:],
                                  start=True, stop=True, skip_group_check=True)
    return last


def turn_probs(pe, s, sems, probs, u):
    pe.wait_ge(sems["probs_ready"], u + 1)
    wait(pe, sems["half0_copied"], STARTS + u)
    wait(pe, sems["half1_copied"], STARTS + u)
    for j in range(s.NB):
        last = s.nc.tensor.transpose(s.turned[:, j, :], probs[:, j * P:(j + 1) * P], s.ident[:])
    last.then_inc(sems["turned_ready"], 1)


def probs_times_values(pe, s, sems, values, u):
    pe.wait_ge(sems["half0_copied"], STARTS + u + 1)
    pe.wait_ge(sems["half1_copied"], STARTS + u + 1)
    wait(pe, sems["out_copied"], STARTS + u)
    for j in range(s.NB):
        half = j % 2
        last = s.nc.tensor.matmul(s.outT[half * s.D:(half + 1) * s.D, 0:P], values[:, j, :], s.probs_t[:, j, :],
                                  start=(j < 2), stop=(j >= s.NB - 2))
    last.then_inc(sems["out_ready"], 1)


def turn_out(pe, s, sems, u, fills_done, to=None, buffers=1):
    pe.wait_ge(sems["out_copied"], STARTS + u + 1)
    if to is None:
        wait(pe, sems["fill_copied"], fills_done)
    wait(pe, sems["unit_done"], STARTS + u + 1 - buffers)
    s.nc.tensor.matmul((s.fill if to is None else to)[:, 0:s.D], s.turned_out[:], s.add_halves[:], start=True,
                       stop=True).then_inc(sems["out_turned"], 1)


def copy_half(eng, copy, s, sems, half, u):
    eng.wait_ge(sems["turned_ready"], STARTS + u + 1)
    n = s.NB // 2
    copy(s.probs_t[:, half * n:(half + 1) * n, :], s.turned[:, half * n:(half + 1) * n, :]
         ).then_inc(sems[f"half{half}_copied"], 1)


def copy_out(v, s, sems, u):
    v.wait_ge(sems["out_ready"], u + 1)
    s.nc.vector.tensor_copy(s.turned_out[:], s.outT[:, 0:P]).then_inc(sems["out_copied"], 1)


def load_bytes(sp, s, sems, m, slot):
    wait(sp, sems["mask_ready"], m - 1)
    sp.dma_start(s.bytes[:, slot, :], s.edges(m)).then_inc(sems[f"bytes_in{slot}"], 16)


def load_all_bytes(sp, s, sems):
    for i in range(2):
        load_bytes(sp, s, sems, i, i)
    with sp.Fori(1, s.B * s.NB // 2) as t:
        for i in range(2):
            load_bytes(sp, s, sems, 2 * t + i, i)


def mask_from(g, s, sems, bytes_, slot):
    hold_waits(g, sems)
    s.nc.gpsimd.tensor_scalar(s.mask[:, slot, :], bytes_, MASKED, 0.0, ALU.mult, ALU.add
                              ).then_inc(sems["mask_ready"], 1)


def masked_max(v, s, sems, logits, slot, bias_scale, out, mask):
    hold_waits(v, sems)
    s.nc.vector.tensor_tensor_reduce(out=out, in0=logits, in1=mask, scale=1.0, scalar=-3e38, op0=ALU.add,
                                     op1=ALU.max, accum_out=s.rowmax[:, slot:slot + 1])
    v.drain()
    s.nc.vector.tensor_scalar(s.negmax[:, slot:slot + 1], s.rowmax[:, slot:slot + 1], bias_scale, None,
                              ALU.mult).then_inc(sems["logits_ready"], 1)


def exponentials(a, s, sems, logits, probs, slot, u, scale, buffers=2):
    a.wait_ge(sems["logits_ready"], STARTS + u + 1)
    wait(a, sems["turned_ready"], STARTS + u + 1 - buffers)
    s.nc.scalar.activation(probs, logits, ACT.Exp, bias=s.negmax[:, slot:slot + 1], scale=scale,
                           accum_out=s.rowsum[:, slot:slot + 1]).then_inc(sems["probs_ready"], 1)


STARTED = ["half0_copied", "half1_copied", "out_copied", "unit_done", "turned_ready", "logits_ready", "x_added", "x_done"]
UNIT_SEMS = ["scores_ready", "logits_ready", "probs_ready", "turned_ready", "half0_copied", "half1_copied",
             "out_ready", "out_copied", "out_turned", "unit_done", "mask_ready", "bytes_in0", "bytes_in1",
             "mean_ready", "centred_ready", "square_ready", "seed_ready", "y_ready",
             "fill_ready", "high_ready", "fill_copied", "weights_in", "weights_ready", "passed"]


def start_sems(sp, sems):
    for name in STARTED:
        if name in sems:
            sp.sem_inc(sems[name], STARTS)


def make_sems(nc, ctx, layer, more=()):
    return {n: ctx.enter_context(nc.semaphore(f"{layer}_{n}")) for n in UNIT_SEMS + list(more)}



def dot_layer(nc, s, layer, heads, w_dram, b_dram, adj_dram=None, x_dram=None):
    B, N, D, NB, H = s.B, s.N, s.D, s.NB, heads
    U = NB * H
    leaky = H > 1
    QK = 2 * H
    K = 2 + 2 * QK + H
    LOADS = 2 if adj_dram is not None else 1
    with ExitStack() as ctx:
        def sb(name, shape, dt):
            return ctx.enter_context(nc.sbuf_tensor(f"{layer}_{name}", shape, dt))

        sems = make_sems(nc, ctx, layer, ["adj_packed", "bytes_stored0", "bytes_stored1", "x_in", "relu_ready", "masked_ready", "bound_ready", "zeros_ready"]
                         + [f"adj_in{i}" for i in range(LOADS)])
        wqk = sb("wqk", [P, QK, 2, D], F32)
        wv = sb("wv", [P, H, D], F32)
        wabs = sb("wabs", [P, QK, D], F32)
        ones = sb("ones", [P, P], F32)
        bound = sb("bound", [P, 12], F32)
        q2 = sb("q2", [P, 2, H, N], F16)
        kh = sb("kh", [P, 2, H, N], F16)
        kl = sb("kl", [P, 2, H, N], F16)
        values = sb("values", [P, 2, NB, H, D], F32)
        logits = sb("logits", [P, 2, N], F32)
        probs = sb("probs", [P, 2, N], F32)
        relu4 = sb("relu4", [P, 2, N], F32) if leaky else None
        masked = sb("masked", [P, 2, N], F32) if leaky else None
        acc = sb("acc", [P, D], F32)
        leaked = sb("leaked", [P, D], F32)
        adj32 = sb("adj32", [P, 2, N], I32) if adj_dram is not None else None
        exp_scale, neg_scale = bound[:, 6:7], bound[:, 7:8]
        scores = [s.scores[:, i, :, :].rearrange("p a b -> p (a b)") for i in range(2)]
        WEIGHT_LOADS = 3 * H * (2 if b_dram else 1) + QK * (2 if b_dram else 1)
        block = ctx.enter_context(nc.Block())

        def fills_before(n):
            return min(K, n if leaky else n + n // 5)

        @block.sync
        def _(sp):
            start_sems(sp, sems)
            sp.wait_ge(sems["zeros_ready"], 1)
            for o in range(2):
                for h in range(H):
                    p = 2 * h + o
                    for twice in range(2):
                        sp.dma_start(wqk[0:D, p, twice, :], w_dram[o][h]).then_inc(sems["weights_in"], 16)
                        if b_dram:
                            sp.dma_start(wqk[D:D + 1, p, twice, :], b_dram[o][h]).then_inc(sems["weights_in"], 16)
            for h in range(H):
                sp.dma_start(wv[0:D, h, :], w_dram[2][h]).then_inc(sems["weights_in"], 16)
                if b_dram:
                    sp.dma_start(wv[D:D + 1, h, :], b_dram[2][h]).then_inc(sems["weights_in"], 16)
            if adj_dram is not None:
                for b in range(B):
                    sp.dma_start(s.x[:, b, :, :], x_dram[b].rearrange("(t p) d -> p t d", p=P)
                                 ).then_inc(sems["x_in"], 16)
                rows = adj_dram.rearrange("b n m -> (b n) m")

                def load(m, i):
                    sp.dma_start(adj32[:, i, :], rows[bass.ds(m * P, P), :]).then_inc(sems[f"adj_in{i}"], 16)

                def store_bytes(m, i):
                    sp.wait_ge(sems["adj_packed"], m + 1)
                    sp.dma_start(s.edges(m), s.bytes[:, i, :]).then_inc(sems[f"bytes_stored{i}"], 16)

                for i in range(2):
                    load(i, i)
                with sp.Fori(1, B * NB // 2) as t:
                    for i in range(2):
                        store_bytes(2 * t + i - 2, i)
                        sp.wait_ge(sems["mask_ready"], 2 * t + i - 1)
                        load(2 * t + i, i)
                for i in range(2):
                    store_bytes(B * NB - 2 + i, i)
                for i in range(2):
                    sp.wait_ge(sems[f"bytes_stored{i}"], 16 * B * NB // 2)
            else:
                load_all_bytes(sp, s, sems)

        @block.gpsimd
        def _(g):
            def mask(pair, i):
                m = 2 * pair + i
                g.wait_ge(sems[f"adj_in{i}"], 16 * pair + 16)
                wait(g, sems[f"bytes_stored{i}"], 16 * pair)
                hold_waits(g, sems)
                nc.gpsimd.tensor_scalar(s.bytes[:, i, :], adj32[:, i, :], -1.0, 1.0, ALU.mult, ALU.add
                                        ).then_inc(sems["adj_packed"], 1)
                g.wait_ge(sems["adj_packed"], m + 1)
                wait(g, sems["logits_ready"], STARTS + m - 1)
                mask_from(g, s, sems, s.bytes[:, i, :], i)

            def mask_relu(pair, i, n, u):
                if n % H == 0:
                    g.wait_ge(sems[f"bytes_in{i}"], 16 * pair + 16)
                    wait(g, sems["masked_ready"], u)
                    mask_from(g, s, sems, s.bytes[:, i, :], 0)
                    g.wait_ge(sems["mask_ready"], 2 * pair + i + 1)
                g.wait_ge(sems["relu_ready"], u + 1)
                wait(g, sems["logits_ready"], STARTS + u - 1)
                nc.gpsimd.tensor_tensor(masked[:, n % 2, :], relu4[:, n % 2, :], s.mask[:, 0, :], ALU.add
                                        ).then_inc(sems["masked_ready"], 1)

            def graph(b, par, norm):
                for n in range(U):
                    if norm and n == 1:
                        layer_norm_centre(g, s, sems, b + 2, b + 2)
                    if norm and n == 3:
                        layer_norm_apply(g, s, sems, b + 2, par, b + 2, b * K + 2)
                    if leaky and (norm or par == 0 or n + 3 < U):
                        i = ((n + 3) // H) % NB
                        mask_relu((b + (n + 3) // U) * (NB // 2) + i // 2, i % 2, n + 3, b * U + n + 3)
                    if not leaky and (norm or par == 0 or n + 2 < NB):
                        mask(b * (NB // 2) + n // 2 + 1, n % 2)

            if adj_dram is not None:
                g.wait_ge(sems["x_in"], 16 * B)
            for b in range(2):
                layer_norm_centre(g, s, sems, b, b)
                layer_norm_apply(g, s, sems, b, b, b, 0)
            if leaky:
                for u in range(3):
                    mask_relu(0, 0, u, u)
            else:
                mask(0, 0)
                mask(0, 1)
            with g.Fori(0, B // 2 - 1) as t:
                for par in range(2):
                    graph(2 * t + par, par, True)
            graph(B - 2, 0, False)
            graph(B - 1, 1, False)

        @block.tensor
        def _(pe):
            def fill(b, par, k, units):
                wait(pe, sems["fill_copied"], b * K + k)
                wait(pe, sems["unit_done"], STARTS + units)
                if k < 2:
                    pe.wait_ge(sems["y_ready"], b + 1)
                    last = turn_y(pe, s, par, k)
                elif k < 2 + 2 * QK:
                    p, half = divmod(k - 2, 2)
                    last = nc.tensor.matmul(s.fill[:], wqk[:, p, :, :].rearrange("p a d -> p (a d)"),
                                            s.hT[:, half * BANK:(half + 1) * BANK], start=True, stop=True)
                else:
                    v = k - 2 - 2 * QK
                    each = NB // H
                    for i in range(each):
                        j = v * each + i
                        last = nc.tensor.matmul(s.fill[:, i * H * D:(i + 1) * H * D], s.hT[:, j * P:(j + 1) * P],
                                                wv[:].rearrange("p h d -> p (h d)"), start=True, stop=True,
                                                skip_group_check=True)
                last.then_inc(sems["fill_ready"], 1)

            def score(b, par, n, u):
                i, h = n // H, n % H
                wait(pe, sems["logits_ready"], STARTS + u - 1)
                lhs = q2[:, par, h, i * P:(i + 1) * P]
                for half in range(2):
                    cols = slice(half * BANK, (half + 1) * BANK)
                    out = s.scores[:, n % 2, half, :]
                    nc.tensor.matmul(out, lhs, kh[:, par, h, cols], start=True, stop=False)
                    last = nc.tensor.matmul(out, lhs, kl[:, par, h, cols], start=False, stop=True)
                last.then_inc(sems["scores_ready"], 1)

            def graph(b, par, project, last_graph):
                for n in range(U):
                    u = b * U + n
                    turn_probs(pe, s, sems, probs[:, n % 2, :], u)
                    if n > 0:
                        turn_out(pe, s, sems, u - 1, (b + 1) * K + (fills_before(n) if project else 0))
                    if n + 3 < U:
                        score(b, par, n + 3, u + 3)
                    elif not last_graph:
                        score(b + 1, 1 - par, n + 3 - U, u + 3)
                    if project:
                        for k in range(fills_before(n), fills_before(n + 1)):
                            fill(b + 1, 1 - par, k, u)
                    probs_times_values(pe, s, sems, values[:, par, :, n % H, :], u)
                turn_out(pe, s, sems, b * U + U - 1, (b + 1) * K + (K if project else 0))

            pe.wait_ge(sems["weights_ready"], 1)
            for p in range(2):
                nc.tensor.matmul(s.outT[:, p * H * D:(p + 1) * H * D], ones[:], wabs[:, p::2, :], start=True, stop=True,
                                 skip_group_check=True).then_inc(sems["bound_ready"], 1)
            pe.wait_ge(sems["weights_ready"], 2)
            for k in range(K):
                fill(0, 0, k, 0)
            wait(pe, sems["fill_copied"], K)
            for u in range(3):
                score(0, 0, u, u)
            with pe.Fori(0, B // 2 - 1) as t:
                for par in range(2):
                    graph(2 * t + par, par, True, False)
            graph(B - 2, 0, True, False)
            graph(B - 1, 1, False, True)

        @block.scalar
        def _(a):
            def high_part(b, par, k):
                if 2 <= k < 2 + 2 * QK:
                    p, half = divmod(k - 2, 2)
                    h, which = divmod(p, 2)
                    to = (q2, kh)[which]
                    a.wait_ge(sems["fill_ready"], b * K + k + 1)
                    nc.scalar.copy(to[:, par, h, half * BANK:(half + 1) * BANK], s.fill[:]
                                   ).then_inc(sems["high_ready"], 1)

            def relu(n, u):
                a.wait_ge(sems["scores_ready"], u + 1)
                wait(a, sems["masked_ready"], u - 1)
                nc.scalar.activation(relu4[:, n % 2, :], scores[n % 2], ACT.Relu, scale=1.0 / SLOPE - 1.0
                                     ).then_inc(sems["relu_ready"], 1)

            def graph(b, par, project, last_graph):
                for n in range(U):
                    u = b * U + n
                    copy_half(a, nc.scalar.copy, s, sems, 1, u)
                    if not (last_graph and n + 1 == U):
                        exponentials(a, s, sems, logits[:, (n + 1) % 2, :], probs[:, (n + 1) % 2, :],
                                     (n + 1) % 4, u + 1, exp_scale)
                    if project:
                        for k in range(fills_before(n), fills_before(n + 1)):
                            high_part(b + 1, 1 - par, k)
                    if leaky and not (last_graph and n + 3 >= U):
                        relu(n + 3, u + 3)

            for k in range(K):
                high_part(0, 0, k)
            if leaky:
                relu(0, 0)
                relu(1, 1)
            exponentials(a, s, sems, logits[:, 0, :], probs[:, 0, :], 0, 0, exp_scale)
            if leaky:
                relu(2, 2)
            with a.Fori(0, B // 2 - 1) as t:
                for par in range(2):
                    graph(2 * t + par, par, True, False)
            graph(B - 2, 0, True, False)
            graph(B - 1, 1, False, True)

        @block.vector
        def _(v):
            def take_fill(b, par, k):
                if k < 2:
                    v.wait_ge(sems["fill_ready"], b * K + k + 1)
                    last = nc.vector.tensor_scalar(s.hT[0:D, k * BANK:(k + 1) * BANK], s.fill[0:D, :], 0.0, None, ALU.max)
                elif k < 2 + 2 * QK:
                    p, half = divmod(k - 2, 2)
                    h, which = divmod(p, 2)
                    cols = slice(half * BANK, (half + 1) * BANK)
                    v.wait_ge(sems["high_ready"], b * 2 * QK + k - 2 + 1)
                    if which == 0:
                        low = q2[D:P, par, h, cols]
                        last = nc.vector.tensor_tensor(low, s.fill[D:P, :], low, ALU.subtract)
                    else:
                        last = nc.vector.tensor_tensor(kl[:, par, h, cols], s.fill[:], kh[:, par, h, cols], ALU.subtract)
                else:
                    v.wait_ge(sems["fill_ready"], b * K + k + 1)
                    each = NB // H
                    at = (k - 2 - 2 * QK) * each
                    last = nc.vector.tensor_copy(values[:, par, at:at + each, :, :].rearrange("p j h d -> p (j h d)"), s.fill[:])
                last.then_inc(sems["fill_copied"], 1)

            def logit(b, n, u):
                wait(v, sems["probs_ready"], u - 1)
                if leaky:
                    v.wait_ge(sems["masked_ready"], u + 1)
                    masked_max(v, s, sems, scores[n % 2], n % 4, neg_scale, logits[:, n % 2, :], masked[:, n % 2, :])
                else:
                    v.wait_ge(sems["scores_ready"], u + 1)
                    v.wait_ge(sems["mask_ready"], u + 1)
                    masked_max(v, s, sems, scores[n % 2], n % 4, neg_scale, logits[:, n % 2, :], s.mask[:, n % 2, :])

            def finish(b, n, u):
                i, h = n // H, n % H
                slot = n % 4
                nc.vector.reciprocal(s.rinv[:, slot:slot + 1], s.rowsum[:, slot:slot + 1])
                v.drain()
                v.wait_ge(sems["out_turned"], u + 1)
                xb = s.block(b, i)
                if not leaky:
                    nc.vector.scalar_tensor_tensor(out=xb, in0=s.fill[:, 0:D], scalar=s.rinv[:, slot:slot + 1], in1=xb,
                                                   op0=ALU.mult, op1=ALU.add).then_inc(sems["unit_done"], 1)
                    return
                if h == 0:
                    nc.vector.tensor_scalar(acc[:], s.fill[:, 0:D], s.rinv[:, slot:slot + 1], None, ALU.mult
                                            ).then_inc(sems["unit_done"], 1)
                else:
                    nc.vector.scalar_tensor_tensor(out=acc[:], in0=s.fill[:, 0:D], scalar=s.rinv[:, slot:slot + 1],
                                                   in1=acc[:], op0=ALU.mult, op1=ALU.add).then_inc(sems["unit_done"], 1)
                if h == H - 1:
                    v.drain()
                    nc.vector.scalar_tensor_tensor(out=leaked[:], in0=acc[:], scalar=SLOPE, in1=acc[:], op0=ALU.mult, op1=ALU.max)
                    v.drain()
                    nc.vector.scalar_tensor_tensor(out=xb, in0=leaked[:], scalar=1.0 / H, in1=xb, op0=ALU.mult, op1=ALU.add)

            def graph(b, par, project, last_graph, norm=True):
                for n in range(U):
                    u = b * U + n
                    copy_half(v, nc.vector.tensor_copy, s, sems, 0, u)
                    if n > 0:
                        finish(b, n - 1, u - 1)
                    if not last_graph or n + 2 < U:
                        logit(b, (n + 2) % U, u + 2)
                    if project:
                        for k in range(fills_before(n), fills_before(n + 1)):
                            take_fill(b + 1, 1 - par, k)
                    if norm and n == 0:
                        layer_norm_mean(v, s, sems, b + 2, b + 2)
                    if norm and n == 2:
                        layer_norm_scale(v, s, sems, b + 2, b + 2)
                    copy_out(v, s, sems, u)
                finish(b, U - 1, b * U + U - 1)

            nc.vector.memset(wqk[D:P, :, :, :], 0.0)
            nc.vector.memset(wv[D:P, :, :], 0.0).then_inc(sems["zeros_ready"], 1)
            if adj_dram is not None:
                v.wait_ge(sems["x_in"], 16 * B)
                nc.vector.memset(s.hT[D:P, :], 0.0)
                v.drain()
                nc.vector.memset(s.hT[D:D + 1, :], 1.0)
            nc.vector.memset(ones[:], 0.0)
            v.drain()
            nc.vector.memset(ones[0:D, :], float(D) ** 0.5)
            v.drain()
            nc.vector.memset(ones[D:D + 1, :], 1.0)
            v.wait_ge(sems["weights_in"], 16 * WEIGHT_LOADS)
            nc.vector.scalar_tensor_tensor(out=wabs[:], in0=wqk[:, :, 0, :], scalar=-1.0, in1=wqk[:, :, 0, :],
                                           op0=ALU.mult, op1=ALU.max).then_inc(sems["weights_ready"], 1)
            v.wait_ge(sems["bound_ready"], 2)
            for p in range(2):
                nc.vector.tensor_reduce(bound[:, p:p + 1], s.outT[:, p * H * D:(p + 1) * H * D], AX.X, ALU.max)
            v.drain()
            nc.vector.tensor_scalar(bound[:, 2:4], bound[:, 0:2], 1e-20, None, ALU.max)
            v.drain()
            nc.vector.tensor_scalar(bound[:, 0:2].bitcast(I32), bound[:, 2:4].bitcast(I32), EXP_BITS, None, ALU.bitwise_and)
            v.drain()
            nc.vector.reciprocal(bound[:, 2:4], bound[:, 0:2])
            v.drain()
            nc.vector.tensor_scalar(bound[:, 4:6], bound[:, 2:4], F16_TOP, None, ALU.mult)
            nc.vector.tensor_scalar(bound[:, 8:9], bound[:, 0:1], bound[:, 1:2],
                                    (SLOPE if leaky else 1.0) * float(D) ** -0.5 / F16_TOP ** 2, ALU.mult, ALU.mult)
            v.drain()
            nc.vector.tensor_copy(exp_scale, bound[:, 8:9])
            nc.vector.tensor_scalar(neg_scale, bound[:, 8:9], -1.0, None, ALU.mult)
            for o in range(2):
                last = nc.vector.tensor_scalar(wqk[:, o::2, :, :], wqk[:, o::2, :, :], bound[:, 4 + o:5 + o], None, ALU.mult)
            last.then_inc(sems["weights_ready"], 1)
            for b in range(2):
                layer_norm_mean(v, s, sems, b, b)
                layer_norm_scale(v, s, sems, b, b)
            for k in range(K):
                take_fill(0, 0, k)
            logit(0, 0, 0)
            logit(0, 1, 1)
            with v.Fori(0, B // 2 - 1) as t:
                for par in range(2):
                    graph(2 * t + par, par, True, False)
            graph(B - 2, 0, True, False, norm=False)
            graph(B - 1, 1, False, True, norm=False)



def elu_parts(v, s, sems, z, low, high):
    s.nc.vector.tensor_scalar(low[:], z, 0.0, None, ALU.min)
    s.nc.vector.tensor_scalar(high[:], z, 0.0, -1.0, ALU.max, ALU.add).then_inc(sems["elu_parts"], 1)


def elu_exp(a, s, sems, low, b):
    a.wait_ge(sems["elu_parts"], b + 1)
    s.nc.scalar.activation(low[:], low[:], ACT.Exp).then_inc(sems["elu_exp"], 1)



def additive_layer(nc, s, lin_w, lin_b, W_w, a_w):
    B, N, D, NB = s.B, s.N, s.D, s.NB
    K = 9
    G, ROWS = 4, 32
    SETS = ROWS // 2
    PAIRS = P // 2
    WIN = 2 * ROWS - 2
    with ExitStack() as ctx:
        def sb(name, shape, dt):
            return ctx.enter_context(nc.sbuf_tensor(f"l2_{name}", shape, dt))

        sems = make_sems(nc, ctx, "l2", ["vector_sets", "scalar_sets", "set_summed", "coded", "elu_parts", "elu_exp",
                                         "raw_turned", "x_added"])
        raw = sb("raw", [D, 3, D], F32)
        lwT = sb("lwT", [P, D], F32)
        w1 = sb("w1", [P, 2, D], F32)
        w2 = sb("w2", [P, 2, D], F32)
        acol = sb("acol", [P, 4], F32)
        ones = sb("ones", [P, P], F32)
        hpT = sb("hpT", [P, N], F32)
        w = sb("w", [P, 2, N], F32)
        r = sb("r", [P, 2, N // 2], F32)
        w_code = sb("w_code", [P, 2, N], F32)
        r_code = sb("r_code", [P, 2, N // 2], F32)
        rng = sb("rng", [P, 12], F32)
        signs = sb("signs", [P, WIN], F32)
        signs_code = sb("signs_code", [P, 2, WIN], BF16)
        quarter = sb("quarter", [P, 2, P], BF16)
        ring = sb("ring", [P, RING, G, N], F32)
        values = sb("values", [P, 2, NB, D], F32)
        logits = sb("logits", [P, N], F32)
        z = sb("z", [P, NB, D], F32)
        low = sb("low", [P, NB, D], F32)
        high = sb("high", [P, NB, D], F32)
        scores = [s.scores[:, i, :, :].rearrange("p a b -> p (a b)") for i in range(2)]
        block = ctx.enter_context(nc.Block())

        def parts(t):
            return t.bitcast(F16).rearrange("p (n two) -> p n two", two=2)

        flat = [t[:].rearrange("p j d -> p (j d)") for t in (low, high)]

        def on_scalar(k, n):
            if not isinstance(n, int):
                more = k in (6, 14)
            elif n < NB - 1:
                more = k in (2, 6, 10, 14)
            else:
                more = True
            return {(k // 2) % G, (k // 2 + 2) % G} if k % 2 or more else {(k // 2) % G}

        SLOT = [k % RING for k in range(SETS - 1)] + [1]
        BACK = [next(d for d in range(1, SETS) if SLOT[(k - d) % SETS] == SLOT[k]) for k in range(SETS)]

        TURN, MULTIPLY, TURN_OUT = 3, 6, 9
        MAX, COPY, COPY_OUT, FINISH = 1, 5, 8, 11
        EXP = 2
        FILL_AT = {0: 0, 2: 1, 4: 2, 6: 3, 11: 4, 13: 5}
        TAKE_AT = {k + 2: i for k, i in FILL_AT.items()}
        FILLS = {1: (0, 6), NB - 2: (6, K)}

        def fills_of(n, project):
            first, end = FILLS.get(n, (0, 0))
            return (first, end - first) if project else (0, 0)

        @block.sync
        def _(sp):
            start_sems(sp, sems)
            sp.wait_ge(sems["weights_ready"], 1)
            for dst, src in ((raw[:, 0, :], lin_w), (raw[:, 1, :], W_w[:, 0:D]), (raw[:, 2, :], W_w[:, D:2 * D]),
                             (acol[0:D, 0:1], a_w), (acol[D:P, 0:1], a_w),
                             (lwT[D:D + 1, :], lin_b.rearrange("(a d) -> a d", a=1))):
                sp.dma_start(dst, src).then_inc(sems["weights_in"], 16)
            load_all_bytes(sp, s, sems)

        @block.gpsimd
        def _(g):
            def mask(pair, i):
                g.wait_ge(sems[f"bytes_in{i}"], 16 * pair + 16)
                wait(g, sems["logits_ready"], STARTS + 2 * pair + i - 1)
                mask_from(g, s, sems, s.bytes[:, i, :], i)

            def elu_add(b):
                g.wait_ge(sems["elu_exp"], b + 1)
                nc.gpsimd.tensor_tensor(high[:], high[:], low[:], ALU.add).then_inc(sems["x_added"], 1)
                g.wait_ge(sems["x_added"], STARTS + 2 * b + 1)
                nc.gpsimd.tensor_tensor(s.graph(b), s.graph(b), high[:], ALU.add).then_inc(sems["x_added"], 1)

            def graph(b, par, norm, project):
                for n in range(2, NB):
                    mask(b * (NB // 2) + n // 2, n % 2)
                    if norm and n == NB - 1:
                        layer_norm_centre(g, s, sems, b + 2, b + 2)
                        layer_norm_apply(g, s, sems, b + 2, par, b + 2, b * K + 2)
                if project:
                    mask((b + 1) * (NB // 2), 0)
                    mask((b + 1) * (NB // 2), 1)
                elu_add(b)

            for b in range(2):
                layer_norm_centre(g, s, sems, b, b)
                layer_norm_apply(g, s, sems, b, b, b, 0)
            mask(0, 0)
            mask(0, 1)
            with g.Fori(0, B // 2 - 1) as t:
                for par in range(2):
                    graph(2 * t + par, par, True, True)
            graph(B - 2, 0, False, True)
            graph(B - 1, 1, False, False)

        @block.tensor
        def _(pe):
            def fill(b, par, k, units):
                wait(pe, sems["fill_copied"], b * K + k)
                wait(pe, sems["unit_done"], STARTS + units)
                both = [slice(h * BANK, (h + 1) * BANK) for h in range(2)]
                if k < 2:
                    pe.wait_ge(sems["y_ready"], b + 1)
                    last = turn_y(pe, s, par, k)
                elif k < 4:
                    last = nc.tensor.matmul(s.fill[0:D, :], lwT[:], s.hT[:, both[k - 2]], start=True, stop=True)
                elif k < 8:
                    lhs = (w2 if k < 6 else w1)[:].rearrange("p a d -> p (a d)")
                    last = nc.tensor.matmul(s.fill[:], lhs, hpT[:, both[k % 2]], start=True, stop=True)
                else:
                    for j in range(NB):
                        last = nc.tensor.matmul(s.fill[:, j * D:(j + 1) * D], s.hT[:, j * P:(j + 1) * P], lwT[:],
                                                start=True, stop=True, skip_group_check=True)
                last.then_inc(sems["fill_ready"], 1)

            def run(b, par, n, u, buf, fills, issued, before=True):
                first, count = fills
                wait(pe, sems["logits_ready"], STARTS + u - 1)
                pe.wait_ge(sems["coded"], b + 1)
                for half in range(2):
                    for part in range(2):
                        nc.tensor.matmul(s.scores[:, buf, half, :], quarter[:, par, :],
                                         parts(w_code[:, par, half * BANK:(half + 1) * BANK])[:, :, part],
                                         start=(part == 0), stop=False, skip_group_check=True)
                for k in range(SETS):
                    pe.wait_ge(sems["vector_sets"], SETS * u + k + 1)
                    pe.wait_ge(sems["scalar_sets"], SETS * u + k + 1)
                    window = slice(WIN - ROWS - 2 * k, WIN - 2 * k)
                    for half in range(2):
                        cols = slice(half * BANK, (half + 1) * BANK)
                        for part in range(2):
                            for g in range(G):
                                out = s.scores[g * ROWS:(g + 1) * ROWS, buf, half, :]
                                if g in on_scalar(k, n):
                                    if part == 0:
                                        last = nc.tensor.matmul(out, signs[:, window], ring[:, SLOT[k], g, cols],
                                                                start=False, stop=(k == SETS - 1), skip_group_check=True)
                                else:
                                    last = nc.tensor.matmul(out, signs_code[:, par, window],
                                                            parts(ring[:, SLOT[k], g, cols])[:, :, part], start=False,
                                                            stop=(k == SETS - 1 and part == 1), skip_group_check=True)
                    last.then_inc(sems["set_summed"], 1)
                    if k in FILL_AT and FILL_AT[k] < count:
                        fill(b + 1, 1 - par, first + FILL_AT[k], u if k > TURN_OUT else u - 1)
                        issued += 1
                    if not before:
                        continue
                    prev = par if not (isinstance(n, int) and n == 0) else 1 - par
                    if k == TURN:
                        turn_probs(pe, s, sems, logits, u - 1)
                    if k == MULTIPLY:
                        probs_times_values(pe, s, sems, values[:, prev, :, :], u - 1)
                    if k == TURN_OUT:
                        turn_out(pe, s, sems, u - 1, issued)
                return issued

            def graph(b, par, project, last_graph):
                done = (b + 1) * K
                done = run(b, par, 1, b * NB + 1, 1, fills_of(1, project), done)
                with pe.Fori(0, (NB - 4) // 2) as t:
                    for i in range(2):
                        run(b, par, 2 * t + 2 + i, b * NB + 2 * t + 2 + i, i, (0, 0), done)
                done = run(b, par, NB - 2, b * NB + NB - 2, 0, fills_of(NB - 2, project), done)
                done = run(b, par, NB - 1, b * NB + NB - 1, 1, (0, 0), done)
                if not last_graph:
                    run(b + 1, 1 - par, 0, (b + 1) * NB, 0, (0, 0), done)

            pe.wait_ge(sems["weights_ready"], 2)
            for i in range(3):
                last = nc.tensor.transpose(s.fill[0:D, i * D:(i + 1) * D], raw[:, i, :], s.ident[0:D, 0:D])
            last.then_inc(sems["raw_turned"], 1)
            pe.wait_ge(sems["weights_ready"], 3)
            for k in range(K):
                fill(0, 0, k, 0)
            run(0, 0, 0, 0, 0, (0, 0), K, before=False)
            with pe.Fori(0, B // 2 - 1) as t:
                for par in range(2):
                    graph(2 * t + par, par, True, False)
            graph(B - 2, 0, True, False)
            graph(B - 1, 1, False, True)
            last = B * NB - 1
            turn_probs(pe, s, sems, logits, last)
            probs_times_values(pe, s, sems, values[:, 1, :, :], last)
            turn_out(pe, s, sems, last, B * K)

        @block.scalar
        def _(a):
            def run(b, par, n, u, buf, before=True):
                slot = 1 - buf
                a.wait_ge(sems["fill_copied"], (b + 1) * K)
                for k in range(SETS):
                    wait(a, sems["set_summed"], SETS * u + k - BACK[k] + 1)
                    for g in sorted(on_scalar(k, n)):
                        last = nc.scalar.activation(ring[:, SLOT[k], g, :], w[:, par, :], ACT.Relu,
                                                    bias=r[:, par, bass.ds(n * PAIRS + g * SETS + k, 1)])
                    last.then_inc(sems["scalar_sets"], 1)
                    if not before:
                        continue
                    if k == EXP:
                        exponentials(a, s, sems, logits[:], logits[:], slot, u - 1, 1.0, buffers=1)
                    if k == COPY:
                        copy_half(a, nc.scalar.copy, s, sems, 1, u - 1)
                    if k == FINISH + 2 and isinstance(n, int) and n == 0:
                        elu_exp(a, s, sems, low, b - 1)

            def graph(b, par, last_graph):
                run(b, par, 1, b * NB + 1, 1)
                with a.Fori(0, (NB - 4) // 2) as t:
                    for i in range(2):
                        run(b, par, 2 * t + 2 + i, b * NB + 2 * t + 2 + i, i)
                for n in (NB - 2, NB - 1):
                    run(b, par, n, b * NB + n, n % 2)
                if not last_graph:
                    run(b + 1, 1 - par, 0, (b + 1) * NB, 0)

            run(0, 0, 0, 0, 0, before=False)
            with a.Fori(0, B // 2 - 1) as t:
                for par in range(2):
                    graph(2 * t + par, par, False)
            graph(B - 2, 0, False)
            graph(B - 1, 1, True)
            exponentials(a, s, sems, logits[:], logits[:], 1, B * NB - 1, 1.0, buffers=1)
            copy_half(a, nc.scalar.copy, s, sems, 1, B * NB - 1)
            elu_exp(a, s, sems, low, B - 1)

        @block.vector
        def _(v):
            def take_fill(b, par, k):
                v.wait_ge(sems["fill_ready"], b * K + k + 1)
                half = slice((k % 2) * BANK, (k % 2 + 1) * BANK)
                if k < 2:
                    last = nc.vector.tensor_scalar(s.hT[0:D, half], s.fill[0:D, :], 0.0, None, ALU.max)
                elif k < 4:
                    last = nc.vector.tensor_copy(hpT[0:D, half], s.fill[0:D, :])
                elif k < 6:
                    last = nc.vector.tensor_scalar(w[:, par, half], s.fill[:], acol[:, 2:3], None, ALU.mult)
                elif k < 8:
                    pairs = slice((k % 2) * BANK // 2, (k % 2 + 1) * BANK // 2)
                    for odd in range(2):
                        rows = slice(odd * D, (odd + 1) * D)
                        last = nc.vector.tensor_scalar(r[rows, par, pairs],
                                                       s.fill[rows, :].rearrange("p (n two) -> p n two", two=2)[:, :, odd],
                                                       acol[rows, 2:3], None, ALU.mult)
                else:
                    last = nc.vector.tensor_copy(values[:, par, :, :].rearrange("p j d -> p (j d)"), s.fill[:])
                last.then_inc(sems["fill_copied"], 1)

            def extremes(i, part, t):
                nc.vector.tensor_reduce(rng[:, 2 * i + part:2 * i + part + 1], t, AX.X, (ALU.max, ALU.min)[part])

            def find_range(par):
                v.drain()
                nc.vector.scalar_tensor_tensor(out=rng[:, 4:6], in0=rng[:, 1:4:2], scalar=-1.0, in1=rng[:, 0:4:2],
                                               op0=ALU.mult, op1=ALU.max)
                v.drain()
                nc.vector.tensor_scalar(rng[:, 6:7], rng[:, 4:5], rng[:, 5:6], 1e-30, ALU.max, ALU.max)
                v.drain()
                nc.vector.tensor_scalar(rng[:, 7:8].bitcast(I32), rng[:, 6:7].bitcast(I32), EXP_BITS, None, ALU.bitwise_and)
                v.drain()
                nc.vector.reciprocal(rng[:, 8:9], rng[:, 7:8])
                v.drain()
                nc.vector.tensor_scalar(rng[:, 9:10], rng[:, 8:9], F16_TOP, None, ALU.mult)
                nc.vector.tensor_scalar(rng[:, 10:11], rng[:, 8:9], -F16_TOP, None, ALU.mult)
                nc.vector.tensor_scalar(rng[:, 11:12], rng[:, 7:8], 1.0 / F16_TOP, None, ALU.mult)
                v.drain()

            def code(src, dst, scale):
                scaled, cut = flat
                nc.vector.tensor_scalar(scaled, src, scale, None, ALU.mult)
                v.drain()
                nc.vector.tensor_scalar(cut.bitcast(I32), scaled.bitcast(I32), HIGH_BITS, None, ALU.bitwise_and)
                v.drain()
                nc.vector.tensor_copy(parts(dst)[:, :, 1], cut)
                nc.vector.tensor_tensor(parts(dst)[:, :, 0], scaled, cut, ALU.subtract)
                v.drain()

            def code_half_w(par, half):
                cols = slice(half * BANK, (half + 1) * BANK)
                code(w[:, par, cols], w_code[:, par, cols], rng[:, 9:10])

            def code_signs(par):
                for odd in range(2):
                    rows = slice(odd * D, (odd + 1) * D)
                    nc.vector.tensor_scalar(signs_code[rows, par, ROWS - 2 + odd:ROWS - 1 + odd], acol[rows, 1:2],
                                            rng[rows, 11:12], None, ALU.mult)
                nc.vector.tensor_scalar(quarter[:, par, :], ones[:], acol[:, 3:4], rng[:, 11:12], ALU.mult, ALU.mult
                                        ).then_inc(sems["coded"], 1)

            def run(b, par, n, u, buf, fills, before=True, norm=False, encode=False, widen=False):
                first, count = fills
                for k in range(SETS):
                    wait(v, sems["set_summed"], SETS * u + k - BACK[k] + 1)
                    for g in range(G):
                        if g not in on_scalar(k, n):
                            last = nc.vector.tensor_scalar(ring[:, SLOT[k], g, :], w_code[:, par, :],
                                                           r_code[:, par, bass.ds(n * PAIRS + g * SETS + k, 1)], None,
                                                           ALU.max)
                    last.then_inc(sems["vector_sets"], 1)
                    if k in TAKE_AT and TAKE_AT[k] < count:
                        take_fill(b + 1, 1 - par, first + TAKE_AT[k])
                    if norm and k == 9:
                        layer_norm_mean(v, s, sems, b + 2, b + 2)
                    if norm and k == 14:
                        layer_norm_scale(v, s, sems, b + 2, b + 2)
                    if widen and k in (9, 12):
                        extremes(0, k // 12, w[:, 1 - par, :])
                    if encode and k in (0, 2):
                        extremes(1, k // 2, r[:, 1 - par, :])
                    if encode and k == 3:
                        find_range(1 - par)
                        wait(v, sems["x_added"], STARTS + 2 * b)
                    if encode and k in (4, 6):
                        code_half_w(1 - par, k // 6)
                    if encode and k == 10:
                        code(r[:, 1 - par, :], r_code[:, 1 - par, :], rng[:, 10:11])
                    if encode and k == 13:
                        code_signs(1 - par)
                    if not before:
                        continue
                    if k == MAX:
                        logit(1 - buf, u - 1)
                    if k == COPY:
                        copy_half(v, nc.vector.tensor_copy, s, sems, 0, u - 1)
                    if k == COPY_OUT:
                        copy_out(v, s, sems, u - 1)
                    if k == FINISH:
                        at_start = isinstance(n, int) and n == 0
                        finish(NB - 1 if at_start else n - 1, 1 - buf, u - 1)
                        if at_start:
                            batch_end(b - 1)

            def batch_end(b):
                v.drain()
                wait(v, sems["x_added"], STARTS + 2 * b)
                elu_parts(v, s, sems, z[:], low, high)

            def logit(buf, u):
                v.wait_ge(sems["set_summed"], SETS * (u + 1))
                v.wait_ge(sems["mask_ready"], u + 1)
                wait(v, sems["turned_ready"], STARTS + u)
                masked_max(v, s, sems, scores[buf], buf, -1.0, logits[:], s.mask[:, buf, :])

            def finish(n, slot, u):
                nc.vector.reciprocal(s.rinv[:, slot:slot + 1], s.rowsum[:, slot:slot + 1])
                v.drain()
                v.wait_ge(sems["out_turned"], u + 1)
                nc.vector.tensor_scalar(z[:, bass.ds(n, 1), :].rearrange("p a d -> p (a d)"), s.fill[:, 0:D],
                                        s.rinv[:, slot:slot + 1], None, ALU.mult).then_inc(sems["unit_done"], 1)

            def graph(b, par, project, last_graph, norm):
                run(b, par, 1, b * NB + 1, 1, fills_of(1, project))
                with v.Fori(0, (NB - 4) // 2) as t:
                    for i in range(2):
                        run(b, par, 2 * t + 2 + i, b * NB + 2 * t + 2 + i, i, (0, 0))
                run(b, par, NB - 2, b * NB + NB - 2, 0, fills_of(NB - 2, project), widen=project)
                run(b, par, NB - 1, b * NB + NB - 1, 1, (0, 0), norm=norm, encode=project)
                if not last_graph:
                    run(b + 1, 1 - par, 0, (b + 1) * NB, 0, (0, 0))

            nc.vector.memset(lwT[D:P, :], 0.0)
            nc.vector.memset(w1[D:P, :, :], 0.0)
            nc.vector.memset(w2[D:P, :, :], 0.0)
            nc.vector.memset(hpT[D:P, :], 0.0)
            nc.vector.memset(ones[:], 1.0)
            nc.vector.memset(signs[:], 0.0)
            nc.vector.memset(signs_code[:], 0.0).then_inc(sems["weights_ready"], 1)
            v.wait_ge(sems["weights_in"], 16 * 6)
            v.drain()
            nc.vector.tensor_scalar(acol[:, 1:2], acol[:, 0:1], 0.0, 2.0, ALU.is_ge, ALU.mult).then_inc(sems["weights_ready"], 1)
            v.drain()
            nc.vector.tensor_scalar(acol[:, 3:4], acol[:, 1:2], -1.0, None, ALU.add)
            v.drain()
            nc.vector.tensor_copy(acol[:, 1:2], acol[:, 3:4])
            nc.vector.scalar_tensor_tensor(out=acol[:, 2:3], in0=acol[:, 0:1], scalar=1.0 - SLOPE, in1=acol[:, 3:4],
                                           op0=ALU.mult, op1=ALU.mult)
            v.drain()
            nc.vector.tensor_scalar(acol[:, 3:4], acol[:, 1:2], SLOPE / (1.0 - SLOPE) / 2, None, ALU.mult)
            for odd in range(2):
                rows = slice(odd * D, (odd + 1) * D)
                nc.vector.tensor_copy(signs[rows, ROWS - 2 + odd:ROWS - 1 + odd], acol[rows, 1:2])
            v.wait_ge(sems["raw_turned"], 1)
            nc.vector.tensor_copy(lwT[0:D, :], s.fill[0:D, 0:D])
            for twice in range(2):
                nc.vector.tensor_copy(w1[0:D, twice, :], s.fill[0:D, D:2 * D])
                last = nc.vector.tensor_copy(w2[0:D, twice, :], s.fill[0:D, 2 * D:3 * D])
            last.then_inc(sems["weights_ready"], 1)
            for b in range(2):
                layer_norm_mean(v, s, sems, b, b)
                layer_norm_scale(v, s, sems, b, b)
            for k in range(K):
                take_fill(0, 0, k)
            v.drain()
            for i, t in enumerate((w, r)):
                for part in range(2):
                    extremes(i, part, t[:, 0, :])
            find_range(0)
            for half in range(2):
                code_half_w(0, half)
            code(r[:, 0, :], r_code[:, 0, :], rng[:, 10:11])
            code_signs(0)
            run(0, 0, 0, 0, 0, (0, 0), before=False)
            with v.Fori(0, B // 2 - 1) as t:
                for par in range(2):
                    graph(2 * t + par, par, True, False, True)
            graph(B - 2, 0, True, False, False)
            graph(B - 1, 1, False, True, False)
            u = B * NB - 1
            logit(1, u)
            copy_half(v, nc.vector.tensor_copy, s, sems, 0, u)
            copy_out(v, s, sems, u)
            finish(NB - 1, 1, u)
            batch_end(B - 1)



def gat_layer(nc, s, w_dram, a_dram, w_res, gamma_dram, beta_dram, out):
    B, N, D, NB = s.B, s.N, s.D, s.NB
    K = 9
    with ExitStack() as ctx:
        def sb(name, shape, dt):
            return ctx.enter_context(nc.sbuf_tensor(f"l3_{name}", shape, dt))

        sems = make_sems(nc, ctx, "l3", ["relu_ready", "base_ready", "elu_parts", "elu_exp", "elu_ready", "out_mean", "out_centred",
                                         "out_square", "out_seed", "out_steps", "x_done", "stored"])
        w = sb("w", [P, D], F32)
        wres = sb("wres", [P, D], F32)
        acol = sb("acol", [P, 2], F32)
        gamma = sb("gamma", [P, D], F32)
        beta = sb("beta", [P, D], F32)
        ones = sb("ones", [P, P], F32)
        a_dst = sb("a_dst", [P, P], F32)
        whT = sb("whT", [P, N], F32)
        dst = sb("dst", [P, 2, N], F32)
        dst_slope = sb("dst_slope", [P, 2, N], F32)
        src = sb("src", [P, 2, NB], F32)
        values = sb("values", [P, 2, NB, D], F32)
        residual = sb("residual", [P, 2, NB, D], F32)
        relu = sb("relu", [P, 2, N], F32)
        base = sb("base", [P, 2, N], F32)
        logits = sb("logits", [P, 2, N], F32)
        probs = sb("probs", [P, 2, N], F32)
        z = sb("z", [P, 2, NB, D], F32)
        low = sb("low", [P, NB, D], F32)
        high = sb("high", [P, NB, D], F32)
        work = sb("work", [P, 4, NB, D], F32)
        total = sb("total", [P, 8, NB], F32)
        unit_out = [s.scores[:, 1, i, :] for i in range(2)]
        block = ctx.enter_context(nc.Block())

        def fills_before(n):
            return min(K, (3 * n + 1) // 2)

        @block.sync
        def _(sp):
            start_sems(sp, sems)
            sp.wait_ge(sems["weights_ready"], 1)
            for to, at in ((w[0:D, :], w_dram), (wres[0:D, :], w_res),
                           (acol[0:D, 0:1], a_dram[0:D].rearrange("(d a) -> d a", a=1)),
                           (acol[0:D, 1:2], a_dram[D:2 * D].rearrange("(d a) -> d a", a=1)),
                           (gamma[:], gamma_dram.partition_broadcast(P)), (beta[:], beta_dram.partition_broadcast(P))):
                sp.dma_start(to, at).then_inc(sems["weights_in"], 16)

            def store(b):
                sp.wait_ge(sems["x_done"], STARTS + b + 1)
                sp.dma_start(out[bass.ds(b, 1)].rearrange("a (t p) d -> p (a t) d", p=P), s.graph(b)
                             ).then_inc(sems["stored"], 16)

            def loads(b, first):
                for n in range(first, NB):
                    load_bytes(sp, s, sems, b * NB + n, n % 2)

            load_bytes(sp, s, sems, 0, 0)
            load_bytes(sp, s, sems, 1, 1)
            loads(0, 2)
            loads(1, 0)
            with sp.Fori(2, B) as b:
                loads(b, 0)
                store(b - 2)
            store(B - 2)
            store(B - 1)
            sp.wait_ge(sems["stored"], 16 * B)

        @block.gpsimd
        def _(g):
            shape = [P, NB, D]

            def mask(b, par, n):
                u = b * NB + n
                g.wait_ge(sems[f"bytes_in{n % 2}"], 16 * (b * (NB // 2) + n // 2) + 16)
                wait(g, sems["base_ready"], u)
                mask_from(g, s, sems, s.bytes[:, n % 2, :], 0)
                g.wait_ge(sems["mask_ready"], u + 1)
                g.wait_ge(sems["fill_copied"], b * K + 6)
                wait(g, sems["logits_ready"], STARTS + u - 1)
                nc.gpsimd.tensor_tensor(base[:, n % 2, :], dst_slope[:, par, :], s.mask[:, 0, :], ALU.add
                                        ).then_inc(sems["base_ready"], 1)

            def out_centre(b):
                centred, square, elu = (work[:, i, :, :] for i in range(3))
                g.wait_ge(sems["out_mean"], b + 1)
                nc.gpsimd.tensor_tensor(centred, elu, total[:, 1, :].unsqueeze(2).to_broadcast(shape), ALU.subtract
                                        ).then_inc(sems["out_centred"], 1)
                g.wait_ge(sems["out_centred"], b + 1)
                nc.gpsimd.tensor_tensor(square, centred, centred, ALU.mult).then_inc(sems["out_square"], 1)

            step = [work[:, i, :, :] for i in range(4)]

            def out_scale(b):
                g.wait_ge(sems["out_seed"], b + 1)
                rsqrt_newton(g, s, total, total[:, 7, :])
                nc.gpsimd.tensor_tensor(step[3], step[0], total[:, 7, :].unsqueeze(2).to_broadcast(shape), ALU.mult
                                        ).then_inc(sems["out_steps"], 1)

            def out_add(b):
                g.wait_ge(sems["out_steps"], 3 * b + 1)
                nc.gpsimd.tensor_tensor(step[1], step[3], gamma[:].unsqueeze(1).to_broadcast(shape), ALU.mult
                                        ).then_inc(sems["out_steps"], 1)
                g.wait_ge(sems["out_steps"], 3 * b + 2)
                nc.gpsimd.tensor_tensor(step[3], step[1], beta[:].unsqueeze(1).to_broadcast(shape), ALU.add
                                        ).then_inc(sems["out_steps"], 1)
                g.wait_ge(sems["out_steps"], 3 * b + 3)
                nc.gpsimd.tensor_tensor(s.graph(b), s.graph(b), step[3], ALU.add).then_inc(sems["x_done"], 1)

            def graph(b, par, project, norm, first=False):
                for n in range(NB):
                    if n + 3 < NB:
                        mask(b, par, n + 3)
                    elif project:
                        mask(b + 1, 1 - par, n + 3 - NB)
                    if n == 1 and not first:
                        out_centre(b - 1)
                    if n == 2 and norm:
                        layer_norm_centre(g, s, sems, b + 2, b + 2)
                    if n == 4 and not first:
                        out_scale(b - 1)
                    if n == 5 and not first:
                        out_add(b - 1)
                    if n == 6 and norm:
                        layer_norm_apply(g, s, sems, b + 2, par, b + 2, b * K + 2)

            for b in range(2):
                layer_norm_centre(g, s, sems, b, b)
                layer_norm_apply(g, s, sems, b, b, b, 0)
            for n in range(3):
                mask(0, 0, n)
            graph(0, 0, True, True, first=True)
            with g.Fori(0, (B - 4) // 2) as t:
                for i in (1, 2):
                    graph(2 * t + i, i % 2, True, True)
            graph(B - 3, 1, True, True)
            graph(B - 2, 0, True, False)
            graph(B - 1, 1, False, False)
            out_centre(B - 1)
            out_scale(B - 1)
            out_add(B - 1)

        @block.tensor
        def _(pe):
            def fill(b, par, k):
                wait(pe, sems["fill_copied"], b * K + k)
                cols = slice((k % 2) * BANK, (k % 2 + 1) * BANK)
                if k < 2:
                    pe.wait_ge(sems["y_ready"], b + 1)
                    last = turn_y(pe, s, par, k)
                elif k < 4:
                    last = nc.tensor.matmul(s.fill[0:D, :], w[:], s.hT[:, cols], start=True, stop=True)
                elif k < 6:
                    last = nc.tensor.matmul(s.fill[:], a_dst[:], whT[:, cols], start=True, stop=True)
                else:
                    for j in range(NB):
                        nodes = slice(j * P, (j + 1) * P)
                        if k == 6:
                            out_, lhs, rhs = s.fill[:, j:j + 1], whT[:, nodes], acol[:, 0:1]
                        else:
                            out_, lhs, rhs = s.fill[:, j * D:(j + 1) * D], s.hT[:, nodes], (w if k == 7 else wres)[:]
                        last = nc.tensor.matmul(out_, lhs, rhs, start=True, stop=True, skip_group_check=True)
                last.then_inc(sems["fill_ready"], 1)

            def graph(b, par, project, first=False):
                for n in range(NB):
                    u = b * NB + n
                    fills = list(range(fills_before(n), fills_before(n + 1))) if project else []
                    turn_probs(pe, s, sems, probs[:, n % 2, :], u)
                    if not (first and n == 0):
                        turn_out(pe, s, sems, u - 1, 0, unit_out[(n - 1) % 2], buffers=2)
                    for k in fills[:1]:
                        fill(b + 1, 1 - par, k)
                    probs_times_values(pe, s, sems, values[:, par, :, :], u)
                    for k in fills[1:]:
                        fill(b + 1, 1 - par, k)

            pe.wait_ge(sems["weights_ready"], 2)
            for k in range(K):
                fill(0, 0, k)
            graph(0, 0, True, first=True)
            with pe.Fori(0, (B - 4) // 2) as t:
                for i in (1, 2):
                    graph(2 * t + i, i % 2, True)
            graph(B - 3, 1, True)
            graph(B - 2, 0, True)
            graph(B - 1, 1, False)
            turn_out(pe, s, sems, B * NB - 1, 0, unit_out[1], buffers=2)

        @block.scalar
        def _(a):
            def dst_fill(b, par, k):
                if k in (4, 5):
                    a.wait_ge(sems["fill_ready"], b * K + k + 1)
                    nc.scalar.activation(dst[:, par, (k % 2) * BANK:(k % 2 + 1) * BANK], s.fill[:], ACT.Copy,
                                         scale=1.0 - SLOPE).then_inc(sems["high_ready"], 1)

            def take_relu(b, par, n):
                a.wait_ge(sems["fill_copied"], b * K + 7)
                wait(a, sems["logits_ready"], STARTS + b * NB + n - 1)
                nc.scalar.activation(relu[:, n % 2, :], dst[:, par, :], ACT.Relu, bias=src[:, par, n:n + 1]
                                     ).then_inc(sems["relu_ready"], 1)

            def graph(b, par, project, first=False):
                for n in range(NB):
                    u = b * NB + n
                    copy_half(a, nc.scalar.copy, s, sems, 0, u)
                    copy_half(a, nc.scalar.copy, s, sems, 1, u)
                    if n + 1 < NB or project:
                        exponentials(a, s, sems, logits[:, (n + 1) % 2, :], probs[:, (n + 1) % 2, :], (n + 1) % 4, u + 1, 1.0)
                    if project:
                        for k in range(fills_before(n), fills_before(n + 1)):
                            dst_fill(b + 1, 1 - par, k)
                    if n + 3 < NB:
                        take_relu(b, par, n + 3)
                    elif project:
                        take_relu(b + 1, 1 - par, n + 3 - NB)
                    if n == 0 and not first:
                        elu_exp(a, s, sems, low, b - 1)

            for k in range(K):
                dst_fill(0, 0, k)
            take_relu(0, 0, 0)
            take_relu(0, 0, 1)
            exponentials(a, s, sems, logits[:, 0, :], probs[:, 0, :], 0, 0, 1.0)
            take_relu(0, 0, 2)
            graph(0, 0, True, first=True)
            with a.Fori(0, (B - 4) // 2) as t:
                for i in (1, 2):
                    graph(2 * t + i, i % 2, True)
            graph(B - 3, 1, True)
            graph(B - 2, 0, True)
            graph(B - 1, 1, False)
            elu_exp(a, s, sems, low, B - 1)

        @block.vector
        def _(v):
            def take_fill(b, par, k):
                cols = slice((k % 2) * BANK, (k % 2 + 1) * BANK)
                if k in (4, 5):
                    v.wait_ge(sems["high_ready"], b * 2 + k - 4 + 1)
                    last = nc.vector.tensor_scalar(dst_slope[:, par, cols], s.fill[:], SLOPE, None, ALU.mult)
                else:
                    v.wait_ge(sems["fill_ready"], b * K + k + 1)
                    if k < 2:
                        last = nc.vector.tensor_scalar(s.hT[0:D, cols], s.fill[0:D, :], 0.0, None, ALU.max)
                    elif k < 4:
                        last = nc.vector.tensor_copy(whT[0:D, cols], s.fill[0:D, :])
                    elif k == 6:
                        last = nc.vector.tensor_scalar(src[:, par, :], s.fill[:, 0:NB], 1.0 - SLOPE, None, ALU.mult)
                    else:
                        to = values if k == 7 else residual
                        last = nc.vector.tensor_copy(to[:, par, :, :].rearrange("p j d -> p (j d)"), s.fill[:])
                last.then_inc(sems["fill_copied"], 1)

            def logit(n, u):
                v.wait_ge(sems["base_ready"], u + 1)
                v.wait_ge(sems["relu_ready"], u + 1)
                wait(v, sems["probs_ready"], u - 1)
                masked_max(v, s, sems, relu[:, n % 2, :], n % 4, -1.0, logits[:, n % 2, :], base[:, n % 2, :])

            def finish(par, n, u):
                slot = n % 4
                nc.vector.reciprocal(s.rinv[:, slot:slot + 1], s.rowsum[:, slot:slot + 1])
                v.drain()
                v.wait_ge(sems["out_turned"], u + 1)
                nc.vector.scalar_tensor_tensor(out=z[:, par, n, :], in0=unit_out[n % 2][:, 0:D], scalar=s.rinv[:, slot:slot + 1],
                                               in1=residual[:, par, n, :], op0=ALU.mult, op1=ALU.add
                                               ).then_inc(sems["unit_done"], 1)

            def out_mean(b):
                wait(v, sems["x_done"], STARTS + b)
                v.wait_ge(sems["elu_exp"], b + 1)
                nc.vector.tensor_tensor(work[:, 2, :, :], high[:], low[:], ALU.add)
                v.drain()
                nc.vector.tensor_reduce(total[:, 0, :], work[:, 2, :, :], AX.X, ALU.add)
                v.drain()
                nc.vector.tensor_scalar(total[:, 1, :], total[:, 0, :], 1.0 / D, None, ALU.mult).then_inc(sems["out_mean"], 1)

            def out_seed(b):
                v.wait_ge(sems["out_square"], b + 1)
                nc.vector.tensor_reduce(total[:, 2, :], work[:, 1, :, :], AX.X, ALU.add)
                v.drain()
                rsqrt_seed(v, s, total, total[:, 2, :]).then_inc(sems["out_seed"], 1)

            def elu(b, par):
                v.drain()
                wait(v, sems["x_done"], STARTS + b)
                elu_parts(v, s, sems, z[:, par, :, :], low, high)

            def graph(b, par, project, norm, first=False):
                for n in range(NB):
                    u = b * NB + n
                    fills = list(range(fills_before(n), fills_before(n + 1))) if project else []
                    if n > 0:
                        finish(par, n - 1, u - 1)
                    elif not first:
                        finish(1 - par, NB - 1, u - 1)
                    if n + 2 < NB or project:
                        logit((n + 2) % NB, u + 2)
                    for k in fills[:1]:
                        take_fill(b + 1, 1 - par, k)
                    copy_out(v, s, sems, u)
                    for k in fills[1:]:
                        take_fill(b + 1, 1 - par, k)
                    if n == 0 and not first:
                        elu(b - 1, 1 - par)
                    if n == 1 and not first:
                        out_mean(b - 1)
                    if n == 1 and norm:
                        layer_norm_mean(v, s, sems, b + 2, b + 2)
                    if n == 3 and not first:
                        out_seed(b - 1)
                    if n == 4 and norm:
                        layer_norm_scale(v, s, sems, b + 2, b + 2)

            nc.vector.memset(w[D:P, :], 0.0)
            nc.vector.memset(wres[D:P, :], 0.0)
            nc.vector.memset(acol[:], 0.0)
            nc.vector.memset(ones[:], 1.0)
            nc.vector.memset(whT[D:P, :], 0.0).then_inc(sems["weights_ready"], 1)
            v.wait_ge(sems["weights_in"], 16 * 6)
            v.drain()
            nc.vector.tensor_scalar(a_dst[:], ones[:], acol[:, 1:2], None, ALU.mult).then_inc(sems["weights_ready"], 1)
            for b in range(2):
                layer_norm_mean(v, s, sems, b, b)
                layer_norm_scale(v, s, sems, b, b)
            for k in range(K):
                take_fill(0, 0, k)
            v.drain()
            logit(0, 0)
            logit(1, 1)
            graph(0, 0, True, True, first=True)
            with v.Fori(0, (B - 4) // 2) as t:
                for i in (1, 2):
                    graph(2 * t + i, i % 2, True, True)
            graph(B - 3, 1, True, True)
            graph(B - 2, 0, True, False)
            graph(B - 1, 1, False, False)
            finish(1, NB - 1, B * NB - 1)
            elu(B - 1, 1)
            out_mean(B - 1)
            out_seed(B - 1)



def gnn_stack(nc, x, adj, L0_gnn_W_q, L0_gnn_W_k, L0_gnn_W_v, L1_gnn_Wv, L1_gnn_bv, L1_gnn_Wq, L1_gnn_bq,
              L1_gnn_Wk, L1_gnn_bk, L2_gnn_lin_w, L2_gnn_lin_b, L2_gnn_W_w, L2_gnn_a, L3_gnn_W, L3_gnn_a,
              L3_gnn_W_res, L3_gnn_gamma, L3_gnn_beta, out):
    B, N, D = x.shape
    H = L1_gnn_Wq.shape[0]
    with ExitStack() as ctx:
        s = Shared(nc, ctx, B, N, D)
        constants(nc, s)
        dot_layer(nc, s, "l0", 1, [[L0_gnn_W_q], [L0_gnn_W_k], [L0_gnn_W_v]], None, adj, x)
        dot_layer(nc, s, "l1", H, [[w[h] for h in range(H)] for w in (L1_gnn_Wq, L1_gnn_Wk, L1_gnn_Wv)],
                  [[w[h:h + 1, :] for h in range(H)] for w in (L1_gnn_bq, L1_gnn_bk, L1_gnn_bv)])
        additive_layer(nc, s, L2_gnn_lin_w, L2_gnn_lin_b, L2_gnn_W_w, L2_gnn_a)
        gat_layer(nc, s, L3_gnn_W, L3_gnn_a, L3_gnn_W_res, L3_gnn_gamma, L3_gnn_beta, out)


def constants(nc, s):
    with nc.semaphore("zeroed") as zeroed, nc.semaphore("ones_ready") as ones_ready, nc.Block() as block:
        @block.vector
        def _(v):
            nc.vector.memset(s.ident[:], 0.0).then_inc(zeroed, 1)
            v.wait_ge(ones_ready, 2)
            nc.vector.tensor_tensor(s.add_halves[:], s.ident[:, 0:s.D], s.ident[:, s.D:2 * s.D], ALU.add)

        @block.gpsimd
        def _(g):
            g.wait_ge(zeroed, 1)
            nc.gpsimd.affine_select(out=s.ident[:], in_=s.ident[:], compare_op=ALU.not_equal, fill=1.0, base=0,
                                    pattern=[[-1, P]], channel_multiplier=1).then_inc(ones_ready, 2)


_INS = ["x", "adj", "L0_gnn_W_q", "L0_gnn_W_k", "L0_gnn_W_v", "L1_gnn_Wv", "L1_gnn_bv", "L1_gnn_Wq", "L1_gnn_bq",
        "L1_gnn_Wk", "L1_gnn_bk", "L2_gnn_lin_w", "L2_gnn_lin_b", "L2_gnn_W_w", "L2_gnn_a", "L3_gnn_W", "L3_gnn_a",
        "L3_gnn_W_res", "L3_gnn_gamma", "L3_gnn_beta"]


def kernel(**inputs):
    import numpy as np
    import concourse.bacc as bacc
    from concourse.bass_utils import run_bass_kernel_spmd

    nc = bacc.Bacc("TRN2", target_bir_lowering=False, num_devices=1)
    arrays = {name: np.ascontiguousarray(inputs[name]) for name in _INS}
    args = [nc.dram_tensor(name, a.shape, mybir.dt.from_np(a.dtype), kind="ExternalInput").ap()
            for name, a in arrays.items()]
    out = nc.dram_tensor("out", arrays["x"].shape, F32, kind="ExternalOutput").ap()
    gnn_stack(nc, *args, out)
    result = run_bass_kernel_spmd(nc, [arrays], core_ids=[0])
    return result.results[0]["out"]
```

```python
from contextlib import ExitStack

import concourse.bass as bass
from concourse import mybir

F32 = mybir.dt.float32
I32 = mybir.dt.int32
F16 = mybir.dt.float16
BF16 = mybir.dt.bfloat16
U8 = mybir.dt.uint8
ALU = mybir.AluOpType
ACT = mybir.ActivationFunctionType
AX = mybir.AxisListType

P = 128
BANK = 512
LN_EPS = 1e-05
MASKED = -float(2 ** 90)
SLOPE = 0.2
EXP_BITS = 0x7F800000
HIGH_BITS = -8192
RSQRT_MAGIC = float(0x5F3759DF)
F16_TOP = float(2 ** 14)
STARTS = 1
RING = 3


def wait(eng, sem, value):
    if not isinstance(value, int) or value > 0:
        eng.wait_ge(sem, value)


def hold_waits(eng, sems):
    eng.sem_inc(sems["passed"], 1)


class Shared:

    def __init__(self, nc, ctx, B, N, D):
        def sb(name, shape, dt):
            return ctx.enter_context(nc.sbuf_tensor(name, shape, dt))

        def ps(name, shape, dt):
            return ctx.enter_context(nc.psum_tensor(name, shape, dt))

        self.nc, self.B, self.N, self.D, self.NB = nc, B, N, D, N // P
        NB = self.NB
        self.x = sb("x_res", [P, B, NB, D], F32)
        self.adj8 = sb("adj8", [P, B * NB, N], U8)
        self.bytes = sb("bytes", [P, 2, N], U8)
        self.mask = sb("mask", [P, 2, N], BF16)
        self.probs_t = sb("probs_t", [P, NB, P], F32)
        self.y = sb("y", [P, 2, NB, D], F32)
        self.centred = sb("centred", [P, NB, D], F32)
        self.square = sb("square", [P, NB, D], F32)
        self.hT = sb("hT", [P, N], F32)
        self.stat = sb("stat", [P, 8, NB], F32)
        self.turned_out = sb("turned_out", [P, P], F32)
        self.ident = sb("ident", [P, P], F32)
        self.add_halves = sb("add_halves", [P, D], F32)
        self.rowmax = sb("rowmax", [P, 4], F32)
        self.negmax = sb("negmax", [P, 4], F32)
        self.rowsum = sb("rowsum", [P, 4], F32)
        self.rinv = sb("rinv", [P, 4], F32)
        self.scores = ps("scores", [P, 2, 2, BANK], F32)
        self.turned = ps("turned", [P, NB, P], F32)
        self.outT = ps("outT", [P, BANK], F32)
        self.fill = ps("fill", [P, BANK], F32)

    def graph(self, b):
        return self.x[:, bass.ds(b, 1), :, :].rearrange("p a t d -> p (a t) d")

    def block(self, b, i):
        return self.x[:, bass.ds(b, 1), i, :].rearrange("p a d -> p (a d)")

    def edges(self, m):
        return self.adj8[:, bass.ds(m, 1), :].rearrange("p a n -> p (a n)")


def fill_bank(s, b, k):
    return s.scores[:, k // 2 % 2, k % 2, :] if isinstance(b, int) and b == 0 else s.fill[:]


def wait_for_bank(pe, s, sems, b, K, k, needs):
    if isinstance(b, int) and b == 0:
        wait(pe, sems["fill_copied"], max(k - 3, needs))
    else:
        wait(pe, sems["fill_copied"], b * K + k)


def next_norm(s, b):
    return b + 2 - s.B if isinstance(b, int) and b + 2 >= s.B else b + 2



def layer_norm_mean(v, s, sems, b, done):
    nc = s.nc
    wait(v, sems["y_ready"], done)
    nc.vector.tensor_reduce(s.stat[:, 0, :], s.graph(b), AX.X, ALU.add)
    v.drain()
    nc.vector.tensor_scalar(s.stat[:, 1, :], s.stat[:, 0, :], 1.0 / s.D, None, ALU.mult).then_inc(sems["mean_ready"], 1)


def layer_norm_centre(g, s, sems, b, done):
    nc = s.nc
    shape = [P, s.NB, s.D]
    g.wait_ge(sems["mean_ready"], done + 1)
    wait(g, sems["y_ready"], done)
    nc.gpsimd.tensor_tensor(s.centred[:], s.graph(b), s.stat[:, 1, :].unsqueeze(2).to_broadcast(shape),
                            ALU.subtract).then_inc(sems["centred_ready"], 1)
    g.wait_ge(sems["centred_ready"], done + 1)
    nc.gpsimd.tensor_tensor(s.square[:], s.centred[:], s.centred[:], ALU.mult).then_inc(sems["square_ready"], 1)


def rsqrt_seed(v, s, stat, total):
    nc = s.nc
    half, guess, var = (stat[:, i, :] for i in (3, 4, 5))
    nc.vector.tensor_scalar(var, total, 1.0 / s.D, LN_EPS, ALU.mult, ALU.add)
    v.drain()
    nc.vector.tensor_scalar(half, var, -0.5, None, ALU.mult)
    nc.vector.tensor_scalar(var.bitcast(I32), var.bitcast(I32), 1, None, ALU.logical_shift_right)
    v.drain()
    return nc.vector.tensor_scalar(guess.bitcast(I32), var.bitcast(I32), -1.0, RSQRT_MAGIC, ALU.mult, ALU.add)


def rsqrt_newton(g, s, stat, out, steps=(0, 1, 2)):
    nc = s.nc
    half, guess, square, product = (stat[:, i, :] for i in (3, 4, 5, 6))
    for step in steps:
        nc.gpsimd.tensor_tensor(square, guess, guess, ALU.mult)
        g.drain()
        nc.gpsimd.tensor_tensor(product, square, half, ALU.mult)
        g.drain()
        nc.gpsimd.tensor_scalar(square, product, 1.0, 1.5, ALU.mult, ALU.add)
        g.drain()
        nc.gpsimd.tensor_tensor(out if step == 2 else guess, square, guess, ALU.mult)
        g.drain()


def layer_norm_scale(v, s, sems, b, done):
    nc = s.nc
    v.wait_ge(sems["square_ready"], done + 1)
    nc.vector.tensor_reduce(s.stat[:, 2, :], s.square[:], AX.X, ALU.add)
    v.drain()
    rsqrt_seed(v, s, s.stat, s.stat[:, 2, :]).then_inc(sems["seed_ready"], 1)


def layer_norm_root(g, s, sems, done, steps):
    if 0 in steps:
        g.wait_ge(sems["seed_ready"], done + 1)
    rsqrt_newton(g, s, s.stat, s.stat[:, 7, :], steps)


def layer_norm_apply(g, s, sems, b, par, done, y_free, steps=(0, 1, 2)):
    if steps:
        layer_norm_root(g, s, sems, done, steps)
    wait(g, sems["fill_ready"], y_free)
    s.nc.gpsimd.tensor_tensor(s.y[:, par, :, :], s.centred[:],
                              s.stat[:, 7, :].unsqueeze(2).to_broadcast([P, s.NB, s.D]),
                              ALU.mult).then_inc(sems["y_ready"], 1)


def turn_y(pe, s, par, half, bank):
    for i in range(s.NB // 2):
        last = s.nc.tensor.matmul(bank[0:s.D, i * P:(i + 1) * P], s.y[:, par, half * s.NB // 2 + i, :], s.ident[:],
                                  start=True, stop=True, skip_group_check=True)
    return last


def turn_probs(pe, s, sems, probs, u):
    pe.wait_ge(sems["probs_ready"], u + 1)
    wait(pe, sems["half0_copied"], STARTS + u)
    wait(pe, sems["half1_copied"], STARTS + u)
    for j in range(s.NB):
        last = s.nc.tensor.transpose(s.turned[:, j, :], probs[:, j * P:(j + 1) * P], s.ident[:])
    last.then_inc(sems["turned_ready"], 1)


def probs_times_values(pe, s, sems, values, u):
    pe.wait_ge(sems["half0_copied"], STARTS + u + 1)
    pe.wait_ge(sems["half1_copied"], STARTS + u + 1)
    wait(pe, sems["out_copied"], STARTS + u)
    for j in range(s.NB):
        half = j % 2
        last = s.nc.tensor.matmul(s.outT[half * s.D:(half + 1) * s.D, 0:P], values[:, j, :], s.probs_t[:, j, :],
                                  start=(j < 2), stop=(j >= s.NB - 2))
    last.then_inc(sems["out_ready"], 1)


def turn_out(pe, s, sems, u, fills_done, to=None, buffers=1):
    pe.wait_ge(sems["out_copied"], STARTS + u + 1)
    if to is None:
        wait(pe, sems["fill_copied"], fills_done)
    wait(pe, sems["unit_done"], STARTS + u + 1 - buffers)
    s.nc.tensor.matmul((s.fill if to is None else to)[:, 0:s.D], s.turned_out[:], s.add_halves[:], start=True,
                       stop=True).then_inc(sems["out_turned"], 1)


def copy_half(eng, copy, s, sems, half, u):
    eng.wait_ge(sems["turned_ready"], STARTS + u + 1)
    n = s.NB // 2
    copy(s.probs_t[:, half * n:(half + 1) * n, :], s.turned[:, half * n:(half + 1) * n, :]
         ).then_inc(sems[f"half{half}_copied"], 1)


def copy_out(v, s, sems, u):
    v.wait_ge(sems["out_ready"], u + 1)
    s.nc.vector.tensor_copy(s.turned_out[:], s.outT[:, 0:P]).then_inc(sems["out_copied"], 1)


def load_bytes(sp, s, sems, m, slot):
    wait(sp, sems["mask_ready"], m - 1)
    sp.dma_start(s.bytes[:, slot, :], s.edges(m)).then_inc(sems[f"bytes_in{slot}"], 16)


def load_all_bytes(sp, s, sems):
    for i in range(2):
        load_bytes(sp, s, sems, i, i)
    with sp.Fori(1, s.B * s.NB // 2) as t:
        for i in range(2):
            load_bytes(sp, s, sems, 2 * t + i, i)


def mask_from(g, s, sems, bytes_, slot):
    hold_waits(g, sems)
    s.nc.gpsimd.tensor_scalar(s.mask[:, slot, :], bytes_, MASKED, 0.0, ALU.mult, ALU.add
                              ).then_inc(sems["mask_ready"], 1)


def masked_max(v, s, sems, logits, slot, bias_scale, out, mask):
    hold_waits(v, sems)
    s.nc.vector.tensor_tensor_reduce(out=out, in0=logits, in1=mask, scale=1.0, scalar=-3e38, op0=ALU.add,
                                     op1=ALU.max, accum_out=s.rowmax[:, slot:slot + 1])
    v.drain()
    s.nc.vector.tensor_scalar(s.negmax[:, slot:slot + 1], s.rowmax[:, slot:slot + 1], bias_scale, None,
                              ALU.mult).then_inc(sems["logits_ready"], 1)


def exponentials(a, s, sems, logits, probs, slot, u, scale, buffers=2):
    a.wait_ge(sems["logits_ready"], STARTS + u + 1)
    wait(a, sems["turned_ready"], STARTS + u + 1 - buffers)
    s.nc.scalar.activation(probs, logits, ACT.Exp, bias=s.negmax[:, slot:slot + 1], scale=scale,
                           accum_out=s.rowsum[:, slot:slot + 1]).then_inc(sems["probs_ready"], 1)


STARTED = ["half0_copied", "half1_copied", "out_copied", "unit_done", "turned_ready", "logits_ready", "x_added", "x_done"]
NORM_SEMS = ["mean_ready", "centred_ready", "square_ready", "seed_ready", "y_ready"]
UNIT_SEMS = ["scores_ready", "logits_ready", "probs_ready", "turned_ready", "half0_copied", "half1_copied",
             "out_ready", "out_copied", "out_turned", "unit_done", "mask_ready", "bytes_in0", "bytes_in1",
             "mean_ready", "centred_ready", "square_ready", "seed_ready", "y_ready",
             "fill_ready", "high_ready", "fill_copied", "weights_in", "weights_ready", "passed"]


def start_sems(sp, sems, normed):
    for name in NORM_SEMS if normed else []:
        sp.sem_inc(sems[name], 2)
    for name in STARTED:
        if name in sems:
            sp.sem_inc(sems[name], STARTS)


def make_sems(nc, ctx, layer, more=()):
    return {n: ctx.enter_context(nc.semaphore(f"{layer}_{n}")) for n in UNIT_SEMS + list(more)}



def dot_layer(nc, s, layer, heads, w_dram, b_dram, adj_dram=None, x_dram=None):
    B, N, D, NB, H = s.B, s.N, s.D, s.NB, heads
    U = NB * H
    leaky = H > 1
    QK = 2 * H
    PIECES = 2
    WIDTH = s.N // PIECES
    K = 2 + PIECES * QK + H
    LOADS = 2 if adj_dram is not None else 1
    with ExitStack() as ctx:
        def sb(name, shape, dt):
            return ctx.enter_context(nc.sbuf_tensor(f"{layer}_{name}", shape, dt))

        sems = make_sems(nc, ctx, layer, ["adj_packed", "bytes_stored0", "bytes_stored1", "x_in0", "x_in1", "x_in", "relu_ready", "masked_ready", "bound_ready", "zeros_ready"]
                         + [f"adj_in{i}" for i in range(LOADS)])
        wqk = sb("wqk", [P, QK, 2, D], F32)
        wv = sb("wv", [P, H, D], F32)
        wabs = sb("wabs", [P, QK, D], F32)
        ones = sb("ones", [P, P], F32)
        bound = sb("bound", [P, 12], F32)
        q2 = sb("q2", [P, 2, H, N], F16)
        kh = sb("kh", [P, 2, H, N], F16)
        kl = sb("kl", [P, 2, H, N], F16)
        values = sb("values", [P, 2, NB, H, D], F32)
        logits = sb("logits", [P, 2, N], F32)
        probs = sb("probs", [P, 2, N], F32)
        relu4 = sb("relu4", [P, 2, N], F32) if leaky else None
        masked = sb("masked", [P, 2, N], F32) if leaky else None
        acc = sb("acc", [P, D], F32)
        leaked = sb("leaked", [P, D], F32)
        adj32 = sb("adj32", [P, 2, N], I32) if adj_dram is not None else None
        exp_scale, neg_scale = bound[:, 6:7], bound[:, 7:8]
        unit_out = s.outT[:, P:P + D]
        scores = [s.scores[:, i, :, :].rearrange("p a b -> p (a b)") for i in range(2)]
        WEIGHT_LOADS = 5 * (2 if b_dram else 1)
        block = ctx.enter_context(nc.Block())

        def fills_before(n):
            return min(K, n if leaky else n + n // 5)

        def steps_fills(n, project):
            return list(range(fills_before(n), fills_before(n + 1))) if project else []

        @block.sync
        def _(sp):
            start_sems(sp, sems, normed=adj_dram is None)
            def load_x(b, arrived):
                sp.dma_start(s.x[:, b, :, :], x_dram[b].rearrange("(t p) d -> p t d", p=P)).then_inc(sems[arrived], 16)

            if adj_dram is not None:
                for b in range(2):
                    load_x(b, f"x_in{b}")
            sp.wait_ge(sems["zeros_ready"], 1)
            for o in range(2):
                for twice in range(2):
                    sp.dma_start(wqk[0:D, o::2, twice, :], w_dram[o].rearrange("h i o -> i h o")
                                 ).then_inc(sems["weights_in"], 16)
                    if b_dram:
                        sp.dma_start(wqk[D:D + 1, o::2, twice, :], b_dram[o].rearrange("(a h) o -> a h o", a=1)
                                     ).then_inc(sems["weights_in"], 16)
            sp.dma_start(wv[0:D, :, :], w_dram[2].rearrange("h i o -> i h o")).then_inc(sems["weights_in"], 16)
            if b_dram:
                sp.dma_start(wv[D:D + 1, :, :], b_dram[2].rearrange("(a h) o -> a h o", a=1)
                             ).then_inc(sems["weights_in"], 16)
            if adj_dram is not None:
                rows = adj_dram.rearrange("b n m -> (b n) m")

                def load(m, i):
                    sp.dma_start(adj32[:, i, :], rows[bass.ds(m * P, P), :]).then_inc(sems[f"adj_in{i}"], 16)

                def store_bytes(m, i):
                    sp.wait_ge(sems["adj_packed"], m + 1)
                    sp.dma_start(s.edges(m), s.bytes[:, i, :]).then_inc(sems[f"bytes_stored{i}"], 16)

                for i in range(2):
                    load(i, i)
                for b in range(2, B):
                    load_x(b, "x_in")
                with sp.Fori(1, B * NB // 2) as t:
                    for i in range(2):
                        store_bytes(2 * t + i - 2, i)
                        sp.wait_ge(sems["mask_ready"], 2 * t + i - 1)
                        load(2 * t + i, i)
                for i in range(2):
                    store_bytes(B * NB - 2 + i, i)
                for i in range(2):
                    sp.wait_ge(sems[f"bytes_stored{i}"], 16 * B * NB // 2)
            else:
                load_all_bytes(sp, s, sems)

        @block.gpsimd
        def _(g):
            def mask(pair, i):
                m = 2 * pair + i
                g.wait_ge(sems[f"adj_in{i}"], 16 * pair + 16)
                wait(g, sems[f"bytes_stored{i}"], 16 * pair)
                hold_waits(g, sems)
                nc.gpsimd.tensor_scalar(s.bytes[:, i, :], adj32[:, i, :], -1.0, 1.0, ALU.mult, ALU.add
                                        ).then_inc(sems["adj_packed"], 1)
                g.wait_ge(sems["adj_packed"], m + 1)
                wait(g, sems["logits_ready"], STARTS + m - 1)
                mask_from(g, s, sems, s.bytes[:, i, :], i)

            def mask_relu(pair, i, n, u):
                if n % H == 0:
                    g.wait_ge(sems[f"bytes_in{i}"], 16 * pair + 16)
                    wait(g, sems["masked_ready"], u)
                    mask_from(g, s, sems, s.bytes[:, i, :], 0)
                    g.wait_ge(sems["mask_ready"], 2 * pair + i + 1)
                g.wait_ge(sems["relu_ready"], u + 1)
                wait(g, sems["logits_ready"], STARTS + u - 1)
                nc.gpsimd.tensor_tensor(masked[:, n % 2, :], relu4[:, n % 2, :], s.mask[:, 0, :], ALU.add
                                        ).then_inc(sems["masked_ready"], 1)

            def graph(b, par, last_graph):
                for n in range(U):
                    if n == 1:
                        layer_norm_centre(g, s, sems, next_norm(s, b), b + 2)
                    if 3 <= n < 6:
                        layer_norm_root(g, s, sems, b + 2, (n - 3,))
                    if n == 6:
                        layer_norm_apply(g, s, sems, next_norm(s, b), par, b + 2, b * K + 2, steps=())
                    if leaky and not (last_graph and n + 3 >= U):
                        i = ((n + 3) // H) % NB
                        mask_relu((b + (n + 3) // U) * (NB // 2) + i // 2, i % 2, n + 3, b * U + n + 3)
                    if not leaky and not (last_graph and n + 2 >= NB):
                        mask(b * (NB // 2) + n // 2 + 1, n % 2)

            if leaky:
                for u in range(3):
                    mask_relu(0, 0, u, u)
            else:
                layer_norm_centre(g, s, sems, 0, 0)
                layer_norm_apply(g, s, sems, 0, 0, 0, 0)
                layer_norm_centre(g, s, sems, 1, 1)
                mask(0, 0)
                layer_norm_apply(g, s, sems, 1, 1, 1, 0)
                mask(0, 1)
            with g.Fori(0, B // 2 - 1) as t:
                for par in range(2):
                    graph(2 * t + par, par, False)
            graph(B - 2, 0, False)
            graph(B - 1, 1, True)

        @block.tensor
        def _(pe):
            def fill(b, par, k):
                bank = fill_bank(s, b, k)
                wait_for_bank(pe, s, sems, b, K, k, 0 if k < 2 else 2)
                if k < 2:
                    pe.wait_ge(sems["y_ready"], b + 1)
                    last = turn_y(pe, s, par, k, bank)
                elif k < 2 + PIECES * QK:
                    p, piece = divmod(k - 2, PIECES)
                    last = nc.tensor.matmul(bank[:, 0:WIDTH], wqk[:, p, :, :].rearrange("p a d -> p (a d)"),
                                            s.hT[:, piece * WIDTH:(piece + 1) * WIDTH], start=True, stop=True)
                else:
                    v = k - 2 - PIECES * QK
                    each = NB // H
                    for i in range(each):
                        j = v * each + i
                        last = nc.tensor.matmul(bank[:, i * H * D:(i + 1) * H * D], s.hT[:, j * P:(j + 1) * P],
                                                wv[:].rearrange("p h d -> p (h d)"), start=True, stop=True,
                                                skip_group_check=True)
                last.then_inc(sems["fill_ready"], 1)

            def score(b, par, n, u):
                i, h = n // H, n % H
                wait(pe, sems["logits_ready"], STARTS + u - 1)
                if n < 3:
                    pe.wait_ge(sems["fill_copied"], b * K + 2 + PIECES * QK)
                lhs = q2[:, par, h, i * P:(i + 1) * P]
                for half in range(2):
                    cols = slice(half * BANK, (half + 1) * BANK)
                    out = s.scores[:, n % 2, half, :]
                    nc.tensor.matmul(out, lhs, kh[:, par, h, cols], start=True, stop=False)
                    last = nc.tensor.matmul(out, lhs, kl[:, par, h, cols], start=False, stop=True)
                last.then_inc(sems["scores_ready"], 1)

            def graph(b, par, project, last_graph):
                for n in range(U):
                    u = b * U + n
                    turn_probs(pe, s, sems, probs[:, n % 2, :], u)
                    if n > 0:
                        turn_out(pe, s, sems, u - 1, 0, unit_out)
                    if n + 3 < U:
                        score(b, par, n + 3, u + 3)
                    elif not last_graph:
                        score(b + 1, 1 - par, n + 3 - U, u + 3)
                    fills = steps_fills(n, project)
                    for k in fills[:1]:
                        fill(b + 1, 1 - par, k)
                    wait(pe, sems["unit_done"], STARTS + u)
                    if n == 0:
                        pe.wait_ge(sems["fill_copied"], (b + 1) * K)
                    probs_times_values(pe, s, sems, values[:, par, :, n % H, :], u)
                    for k in fills[1:]:
                        fill(b + 1, 1 - par, k)
                turn_out(pe, s, sems, b * U + U - 1, 0, unit_out)

            pe.wait_ge(sems["weights_ready"], 1)
            for p in range(2):
                nc.tensor.matmul(s.outT[:, p * H * D:(p + 1) * H * D], ones[:], wabs[:, p::2, :], start=True, stop=True,
                                 skip_group_check=True).then_inc(sems["bound_ready"], 1)
            pe.wait_ge(sems["weights_ready"], 2)
            for k in range(K):
                fill(0, 0, k)
            wait(pe, sems["fill_copied"], K)
            for u in range(3):
                score(0, 0, u, u)
            with pe.Fori(0, B // 2 - 1) as t:
                for par in range(2):
                    graph(2 * t + par, par, True, False)
            graph(B - 2, 0, True, False)
            graph(B - 1, 1, False, True)

        @block.scalar
        def _(a):
            def high_part(b, par, k):
                if 2 <= k < 2 + PIECES * QK:
                    p, piece = divmod(k - 2, PIECES)
                    h, which = divmod(p, 2)
                    to = (q2, kh)[which]
                    a.wait_ge(sems["fill_ready"], b * K + k + 1)
                    nc.scalar.copy(to[:, par, h, piece * WIDTH:(piece + 1) * WIDTH], fill_bank(s, b, k)[:, 0:WIDTH]
                                   ).then_inc(sems["high_ready"], 1)

            def relu(n, u):
                a.wait_ge(sems["scores_ready"], u + 1)
                wait(a, sems["masked_ready"], u - 1)
                nc.scalar.activation(relu4[:, n % 2, :], scores[n % 2], ACT.Relu, scale=1.0 / SLOPE - 1.0
                                     ).then_inc(sems["relu_ready"], 1)

            def graph(b, par, project, last_graph):
                for n in range(U):
                    u = b * U + n
                    copy_half(a, nc.scalar.copy, s, sems, 1, u)
                    if not (last_graph and n + 1 == U):
                        exponentials(a, s, sems, logits[:, (n + 1) % 2, :], probs[:, (n + 1) % 2, :],
                                     (n + 1) % 4, u + 1, exp_scale)
                    fills = steps_fills(n, project)
                    for k in fills[:1]:
                        high_part(b + 1, 1 - par, k)
                    if leaky and not (last_graph and n + 3 >= U):
                        relu(n + 3, u + 3)
                    for k in fills[1:]:
                        high_part(b + 1, 1 - par, k)

            for k in range(K):
                high_part(0, 0, k)
            if leaky:
                relu(0, 0)
                relu(1, 1)
            exponentials(a, s, sems, logits[:, 0, :], probs[:, 0, :], 0, 0, exp_scale)
            if leaky:
                relu(2, 2)
            with a.Fori(0, B // 2 - 1) as t:
                for par in range(2):
                    graph(2 * t + par, par, True, False)
            graph(B - 2, 0, True, False)
            graph(B - 1, 1, False, True)

        @block.vector
        def _(v):
            def take_fill(b, par, k):
                bank = fill_bank(s, b, k)
                if k < 2:
                    v.wait_ge(sems["fill_ready"], b * K + k + 1)
                    last = nc.vector.tensor_scalar(s.hT[0:D, k * BANK:(k + 1) * BANK], bank[0:D, :], 0.0, None, ALU.max)
                elif k < 2 + PIECES * QK:
                    p, piece = divmod(k - 2, PIECES)
                    h, which = divmod(p, 2)
                    cols = slice(piece * WIDTH, (piece + 1) * WIDTH)
                    v.wait_ge(sems["high_ready"], b * PIECES * QK + k - 2 + 1)
                    if which == 0:
                        low = q2[D:P, par, h, cols]
                        last = nc.vector.tensor_tensor(low, bank[D:P, 0:WIDTH], low, ALU.subtract)
                    else:
                        last = nc.vector.tensor_tensor(kl[:, par, h, cols], bank[:, 0:WIDTH], kh[:, par, h, cols], ALU.subtract)
                else:
                    v.wait_ge(sems["fill_ready"], b * K + k + 1)
                    each = NB // H
                    at = (k - 2 - PIECES * QK) * each
                    last = nc.vector.tensor_copy(values[:, par, at:at + each, :, :].rearrange("p j h d -> p (j h d)"), bank[:])
                last.then_inc(sems["fill_copied"], 1)

            def logit(b, n, u):
                wait(v, sems["probs_ready"], u - 1)
                if leaky:
                    v.wait_ge(sems["masked_ready"], u + 1)
                    masked_max(v, s, sems, scores[n % 2], n % 4, neg_scale, logits[:, n % 2, :], masked[:, n % 2, :])
                else:
                    v.wait_ge(sems["scores_ready"], u + 1)
                    v.wait_ge(sems["mask_ready"], u + 1)
                    masked_max(v, s, sems, scores[n % 2], n % 4, neg_scale, logits[:, n % 2, :], s.mask[:, n % 2, :])

            def finish(b, n, u):
                i, h = n // H, n % H
                slot = n % 4
                nc.vector.reciprocal(s.rinv[:, slot:slot + 1], s.rowsum[:, slot:slot + 1])
                v.drain()
                v.wait_ge(sems["out_turned"], u + 1)
                xb = s.block(b, i)
                if not leaky:
                    nc.vector.scalar_tensor_tensor(out=xb, in0=unit_out[:, 0:D], scalar=s.rinv[:, slot:slot + 1], in1=xb,
                                                   op0=ALU.mult, op1=ALU.add).then_inc(sems["unit_done"], 1)
                    return
                if h == 0:
                    nc.vector.tensor_scalar(acc[:], unit_out[:, 0:D], s.rinv[:, slot:slot + 1], None, ALU.mult
                                            ).then_inc(sems["unit_done"], 1)
                else:
                    nc.vector.scalar_tensor_tensor(out=acc[:], in0=unit_out[:, 0:D], scalar=s.rinv[:, slot:slot + 1],
                                                   in1=acc[:], op0=ALU.mult, op1=ALU.add).then_inc(sems["unit_done"], 1)
                if h == H - 1:
                    v.drain()
                    nc.vector.scalar_tensor_tensor(out=leaked[:], in0=acc[:], scalar=SLOPE, in1=acc[:], op0=ALU.mult, op1=ALU.max)
                    v.drain()
                    nc.vector.scalar_tensor_tensor(out=xb, in0=leaked[:], scalar=1.0 / H, in1=xb, op0=ALU.mult, op1=ALU.add)

            def graph(b, par, project, last_graph):
                for n in range(U):
                    u = b * U + n
                    copy_half(v, nc.vector.tensor_copy, s, sems, 0, u)
                    if n > 0:
                        finish(b, n - 1, u - 1)
                    if not last_graph or n + 2 < U:
                        logit(b, (n + 2) % U, u + 2)
                    fills = steps_fills(n, project)
                    if n == 0:
                        layer_norm_mean(v, s, sems, next_norm(s, b), b + 2)
                    if n == 2:
                        layer_norm_scale(v, s, sems, next_norm(s, b), b + 2)
                    copy_out(v, s, sems, u)
                    for k in fills:
                        take_fill(b + 1, 1 - par, k)
                finish(b, U - 1, b * U + U - 1)

            nc.vector.memset(wqk[D:P, :, :, :], 0.0)
            nc.vector.memset(wv[D:P, :, :], 0.0).then_inc(sems["zeros_ready"], 1)
            if adj_dram is not None:
                v.wait_ge(sems["x_in0"], 16)
                layer_norm_mean(v, s, sems, 0, 0)
                nc.vector.memset(s.hT[D:P, :], 0.0)
                v.drain()
                nc.vector.memset(s.hT[D:D + 1, :], 1.0)
            nc.vector.memset(ones[:], 0.0)
            v.drain()
            nc.vector.memset(ones[0:D, :], float(D) ** 0.5)
            v.drain()
            nc.vector.memset(ones[D:D + 1, :], 1.0)
            v.wait_ge(sems["weights_in"], 16 * WEIGHT_LOADS)
            nc.vector.scalar_tensor_tensor(out=wabs[:], in0=wqk[:, :, 0, :], scalar=-1.0, in1=wqk[:, :, 0, :],
                                           op0=ALU.mult, op1=ALU.max).then_inc(sems["weights_ready"], 1)
            if adj_dram is not None:
                layer_norm_scale(v, s, sems, 0, 0)
            v.wait_ge(sems["bound_ready"], 2)
            for p in range(2):
                nc.vector.tensor_reduce(bound[:, p:p + 1], s.outT[:, p * H * D:(p + 1) * H * D], AX.X, ALU.max)
            v.drain()
            nc.vector.tensor_scalar(bound[:, 2:4], bound[:, 0:2], 1e-20, None, ALU.max)
            v.drain()
            nc.vector.tensor_scalar(bound[:, 0:2].bitcast(I32), bound[:, 2:4].bitcast(I32), EXP_BITS, None, ALU.bitwise_and)
            v.drain()
            nc.vector.reciprocal(bound[:, 2:4], bound[:, 0:2])
            v.drain()
            nc.vector.tensor_scalar(bound[:, 4:6], bound[:, 2:4], F16_TOP, None, ALU.mult)
            nc.vector.tensor_scalar(bound[:, 8:9], bound[:, 0:1], bound[:, 1:2],
                                    (SLOPE if leaky else 1.0) * float(D) ** -0.5 / F16_TOP ** 2, ALU.mult, ALU.mult)
            v.drain()
            nc.vector.tensor_copy(exp_scale, bound[:, 8:9])
            nc.vector.tensor_scalar(neg_scale, bound[:, 8:9], -1.0, None, ALU.mult)
            for o in range(2):
                last = nc.vector.tensor_scalar(wqk[:, o::2, :, :], wqk[:, o::2, :, :], bound[:, 4 + o:5 + o], None, ALU.mult)
            last.then_inc(sems["weights_ready"], 1)
            for k in range(K):
                take_fill(0, 0, k)
                if adj_dram is not None and k == 1:
                    v.wait_ge(sems["x_in1"], 16)
                    layer_norm_mean(v, s, sems, 1, 1)
                if adj_dram is not None and k == 4:
                    layer_norm_scale(v, s, sems, 1, 1)
            logit(0, 0, 0)
            logit(0, 1, 1)
            if adj_dram is not None:
                v.wait_ge(sems["x_in"], 16 * (B - 2))
            with v.Fori(0, B // 2 - 1) as t:
                for par in range(2):
                    graph(2 * t + par, par, True, False)
            graph(B - 2, 0, True, False)
            graph(B - 1, 1, False, True)



def elu_parts(v, s, sems, z, low, high):
    s.nc.vector.tensor_scalar(low[:], z, 0.0, None, ALU.min)
    s.nc.vector.tensor_scalar(high[:], z, 0.0, -1.0, ALU.max, ALU.add).then_inc(sems["elu_parts"], 1)


def elu_exp(a, s, sems, low, b):
    a.wait_ge(sems["elu_parts"], b + 1)
    s.nc.scalar.activation(low[:], low[:], ACT.Exp).then_inc(sems["elu_exp"], 1)



def additive_layer(nc, s, lin_w, lin_b, W_w, a_w):
    B, N, D, NB = s.B, s.N, s.D, s.NB
    K = 9
    G, ROWS = 4, 32
    SETS = ROWS // 2
    PAIRS = P // 2
    WIN = 2 * ROWS - 2
    with ExitStack() as ctx:
        def sb(name, shape, dt):
            return ctx.enter_context(nc.sbuf_tensor(f"l2_{name}", shape, dt))

        sems = make_sems(nc, ctx, "l2", ["vector_sets", "scalar_sets", "set_summed", "coded", "elu_parts", "elu_exp",
                                         "raw_turned", "x_added"])
        raw = sb("raw", [D, 3, D], F32)
        lwT = sb("lwT", [P, D], F32)
        w1 = sb("w1", [P, 2, D], F32)
        w2 = sb("w2", [P, 2, D], F32)
        acol = sb("acol", [P, 4], F32)
        ones = sb("ones", [P, P], F32)
        hpT = sb("hpT", [P, N], F32)
        w = sb("w", [P, 2, N], F32)
        r = sb("r", [P, 2, N // 2], F32)
        w_code = sb("w_code", [P, 2, N], F32)
        r_code = sb("r_code", [P, 2, N // 2], F32)
        rng = sb("rng", [P, 12], F32)
        signs = sb("signs", [P, WIN], F32)
        signs_code = sb("signs_code", [P, 2, WIN], BF16)
        quarter = sb("quarter", [P, 2, P], BF16)
        ring = sb("ring", [P, RING, G, N], F32)
        values = sb("values", [P, 2, NB, D], F32)
        logits = sb("logits", [P, N], F32)
        z = sb("z", [P, NB, D], F32)
        low = sb("low", [P, NB, D], F32)
        high = sb("high", [P, NB, D], F32)
        scores = [s.scores[:, i, :, :].rearrange("p a b -> p (a b)") for i in range(2)]
        block = ctx.enter_context(nc.Block())

        def parts(t):
            return t.bitcast(F16).rearrange("p (n two) -> p n two", two=2)

        flat = [t[:].rearrange("p j d -> p (j d)") for t in (low, high)]

        def on_scalar(k, n):
            if not isinstance(n, int):
                more = k in (6, 14)
            elif n < NB - 1:
                more = k in (10,)
            else:
                more = k != 12
            return {(k // 2) % G, (k // 2 + 2) % G} if k % 2 or more else {(k // 2) % G}

        SLOT = [k % RING for k in range(SETS - 1)] + [1]
        BACK = [next(d for d in range(1, SETS) if SLOT[(k - d) % SETS] == SLOT[k]) for k in range(SETS)]

        TURN, MULTIPLY, TURN_OUT = 3, 6, 9
        MAX, COPY, COPY_OUT, FINISH = 1, 5, 8, 11
        EXP = 2
        FILL_AT = {0: 0, 2: 1, 4: 2, 6: 3, 11: 4, 13: 5}
        TAKE_AT = {k + 2: i for k, i in FILL_AT.items()}
        FILLS = {1: (0, 6), NB - 2: (6, K)}

        def fills_of(n, project):
            first, end = FILLS.get(n, (0, 0))
            return (first, end - first) if project else (0, 0)

        @block.sync
        def _(sp):
            start_sems(sp, sems, normed=True)
            sp.wait_ge(sems["weights_ready"], 1)
            for dst, src in ((raw[:, 0, :], lin_w), (raw[:, 1, :], W_w[:, 0:D]), (raw[:, 2, :], W_w[:, D:2 * D]),
                             (acol[0:D, 0:1], a_w), (acol[D:P, 0:1], a_w),
                             (lwT[D:D + 1, :], lin_b.rearrange("(a d) -> a d", a=1))):
                sp.dma_start(dst, src).then_inc(sems["weights_in"], 16)
            load_all_bytes(sp, s, sems)

        @block.gpsimd
        def _(g):
            def mask(pair, i):
                g.wait_ge(sems[f"bytes_in{i}"], 16 * pair + 16)
                wait(g, sems["logits_ready"], STARTS + 2 * pair + i - 1)
                mask_from(g, s, sems, s.bytes[:, i, :], i)

            def elu_add(b):
                g.wait_ge(sems["elu_exp"], b + 1)
                nc.gpsimd.tensor_tensor(high[:], high[:], low[:], ALU.add).then_inc(sems["x_added"], 1)
                g.wait_ge(sems["x_added"], STARTS + 2 * b + 1)
                nc.gpsimd.tensor_tensor(s.graph(b), s.graph(b), high[:], ALU.add).then_inc(sems["x_added"], 1)

            def graph(b, par, project):
                for n in range(2, NB):
                    mask(b * (NB // 2) + n // 2, n % 2)
                    if n == NB - 1:
                        layer_norm_centre(g, s, sems, next_norm(s, b), b + 2)
                        layer_norm_apply(g, s, sems, next_norm(s, b), par, b + 2, b * K + 2)
                if project:
                    mask((b + 1) * (NB // 2), 0)
                    mask((b + 1) * (NB // 2), 1)
                elu_add(b)

            mask(0, 0)
            mask(0, 1)
            with g.Fori(0, B // 2 - 1) as t:
                for par in range(2):
                    graph(2 * t + par, par, True)
            graph(B - 2, 0, True)
            graph(B - 1, 1, False)

        @block.tensor
        def _(pe):
            def fill(b, par, k, units):
                bank = fill_bank(s, b, k)
                wait_for_bank(pe, s, sems, b, K, k, 0 if k < 2 else 4 if 4 <= k < 8 else 2)
                wait(pe, sems["unit_done"], STARTS + units)
                both = [slice(h * BANK, (h + 1) * BANK) for h in range(2)]
                if k < 2:
                    pe.wait_ge(sems["y_ready"], b + 1)
                    last = turn_y(pe, s, par, k, bank)
                elif k < 4:
                    last = nc.tensor.matmul(bank[0:D, :], lwT[:], s.hT[:, both[k - 2]], start=True, stop=True)
                elif k < 8:
                    lhs = (w2 if k < 6 else w1)[:].rearrange("p a d -> p (a d)")
                    last = nc.tensor.matmul(bank[:], lhs, hpT[:, both[k % 2]], start=True, stop=True)
                else:
                    for j in range(NB):
                        last = nc.tensor.matmul(bank[:, j * D:(j + 1) * D], s.hT[:, j * P:(j + 1) * P], lwT[:],
                                                start=True, stop=True, skip_group_check=True)
                last.then_inc(sems["fill_ready"], 1)

            def run(b, par, n, u, buf, fills, issued, before=True):
                first, count = fills
                wait(pe, sems["logits_ready"], STARTS + u - 1)
                pe.wait_ge(sems["coded"], b + 1)
                for half in range(2):
                    for part in range(2):
                        nc.tensor.matmul(s.scores[:, buf, half, :], quarter[:, par, :],
                                         parts(w_code[:, par, half * BANK:(half + 1) * BANK])[:, :, part],
                                         start=(part == 0), stop=False, skip_group_check=True)
                for k in range(SETS):
                    pe.wait_ge(sems["vector_sets"], SETS * u + k + 1)
                    pe.wait_ge(sems["scalar_sets"], SETS * u + k + 1)
                    window = slice(WIN - ROWS - 2 * k, WIN - 2 * k)
                    for half in range(2):
                        cols = slice(half * BANK, (half + 1) * BANK)
                        for part in range(2):
                            for g in range(G):
                                out = s.scores[g * ROWS:(g + 1) * ROWS, buf, half, :]
                                if g in on_scalar(k, n):
                                    if part == 0:
                                        last = nc.tensor.matmul(out, signs[:, window], ring[:, SLOT[k], g, cols],
                                                                start=False, stop=(k == SETS - 1), skip_group_check=True)
                                else:
                                    last = nc.tensor.matmul(out, signs_code[:, par, window],
                                                            parts(ring[:, SLOT[k], g, cols])[:, :, part], start=False,
                                                            stop=(k == SETS - 1 and part == 1), skip_group_check=True)
                    last.then_inc(sems["set_summed"], 1)
                    if k in FILL_AT and FILL_AT[k] < count:
                        fill(b + 1, 1 - par, first + FILL_AT[k], u if k > TURN_OUT else u - 1)
                        issued += 1
                    if not before:
                        continue
                    prev = par if not (isinstance(n, int) and n == 0) else 1 - par
                    if k == TURN:
                        turn_probs(pe, s, sems, logits, u - 1)
                    if k == MULTIPLY:
                        probs_times_values(pe, s, sems, values[:, prev, :, :], u - 1)
                    if k == TURN_OUT:
                        turn_out(pe, s, sems, u - 1, issued)
                return issued

            def graph(b, par, project, last_graph):
                done = (b + 1) * K
                done = run(b, par, 1, b * NB + 1, 1, fills_of(1, project), done)
                with pe.Fori(0, (NB - 4) // 2) as t:
                    for i in range(2):
                        run(b, par, 2 * t + 2 + i, b * NB + 2 * t + 2 + i, i, (0, 0), done)
                done = run(b, par, NB - 2, b * NB + NB - 2, 0, fills_of(NB - 2, project), done)
                done = run(b, par, NB - 1, b * NB + NB - 1, 1, (0, 0), done)
                if not last_graph:
                    run(b + 1, 1 - par, 0, (b + 1) * NB, 0, (0, 0), done)

            pe.wait_ge(sems["weights_ready"], 2)
            for i in range(3):
                last = nc.tensor.transpose(s.fill[0:D, i * D:(i + 1) * D], raw[:, i, :], s.ident[0:D, 0:D])
            last.then_inc(sems["raw_turned"], 1)
            pe.wait_ge(sems["weights_ready"], 3)
            for k in range(K):
                fill(0, 0, k, 0)
            run(0, 0, 0, 0, 0, (0, 0), K, before=False)
            with pe.Fori(0, B // 2 - 1) as t:
                for par in range(2):
                    graph(2 * t + par, par, True, False)
            graph(B - 2, 0, True, False)
            graph(B - 1, 1, False, True)
            last = B * NB - 1
            turn_probs(pe, s, sems, logits, last)
            probs_times_values(pe, s, sems, values[:, 1, :, :], last)
            turn_out(pe, s, sems, last, B * K)

        @block.scalar
        def _(a):
            def run(b, par, n, u, buf, before=True):
                slot = 1 - buf
                a.wait_ge(sems["fill_copied"], (b + 1) * K)
                for k in range(SETS):
                    wait(a, sems["set_summed"], SETS * u + k - BACK[k] + 1)
                    for g in sorted(on_scalar(k, n)):
                        last = nc.scalar.activation(ring[:, SLOT[k], g, :], w[:, par, :], ACT.Relu,
                                                    bias=r[:, par, bass.ds(n * PAIRS + g * SETS + k, 1)])
                    last.then_inc(sems["scalar_sets"], 1)
                    if not before:
                        continue
                    if k == EXP:
                        exponentials(a, s, sems, logits[:], logits[:], slot, u - 1, 1.0, buffers=1)
                    if k == COPY:
                        copy_half(a, nc.scalar.copy, s, sems, 1, u - 1)
                    if k == FINISH + 2 and isinstance(n, int) and n == 0:
                        elu_exp(a, s, sems, low, b - 1)

            def graph(b, par, last_graph):
                run(b, par, 1, b * NB + 1, 1)
                with a.Fori(0, (NB - 4) // 2) as t:
                    for i in range(2):
                        run(b, par, 2 * t + 2 + i, b * NB + 2 * t + 2 + i, i)
                for n in (NB - 2, NB - 1):
                    run(b, par, n, b * NB + n, n % 2)
                if not last_graph:
                    run(b + 1, 1 - par, 0, (b + 1) * NB, 0)

            run(0, 0, 0, 0, 0, before=False)
            with a.Fori(0, B // 2 - 1) as t:
                for par in range(2):
                    graph(2 * t + par, par, False)
            graph(B - 2, 0, False)
            graph(B - 1, 1, True)
            exponentials(a, s, sems, logits[:], logits[:], 1, B * NB - 1, 1.0, buffers=1)
            copy_half(a, nc.scalar.copy, s, sems, 1, B * NB - 1)
            elu_exp(a, s, sems, low, B - 1)

        @block.vector
        def _(v):
            def take_fill(b, par, k):
                bank = fill_bank(s, b, k)
                v.wait_ge(sems["fill_ready"], b * K + k + 1)
                half = slice((k % 2) * BANK, (k % 2 + 1) * BANK)
                if k < 2:
                    last = nc.vector.tensor_scalar(s.hT[0:D, half], bank[0:D, :], 0.0, None, ALU.max)
                elif k < 4:
                    last = nc.vector.tensor_copy(hpT[0:D, half], bank[0:D, :])
                elif k < 6:
                    last = nc.vector.tensor_scalar(w[:, par, half], bank[:], acol[:, 2:3], None, ALU.mult)
                elif k < 8:
                    pairs = slice((k % 2) * BANK // 2, (k % 2 + 1) * BANK // 2)
                    for odd in range(2):
                        rows = slice(odd * D, (odd + 1) * D)
                        last = nc.vector.tensor_scalar(r[rows, par, pairs],
                                                       bank[rows, :].rearrange("p (n two) -> p n two", two=2)[:, :, odd],
                                                       acol[rows, 2:3], None, ALU.mult)
                else:
                    last = nc.vector.tensor_copy(values[:, par, :, :].rearrange("p j d -> p (j d)"), bank[:])
                last.then_inc(sems["fill_copied"], 1)

            def extremes(i, part, t):
                nc.vector.tensor_reduce(rng[:, 2 * i + part:2 * i + part + 1], t, AX.X, (ALU.max, ALU.min)[part])

            def find_range(par):
                v.drain()
                nc.vector.scalar_tensor_tensor(out=rng[:, 4:6], in0=rng[:, 1:4:2], scalar=-1.0, in1=rng[:, 0:4:2],
                                               op0=ALU.mult, op1=ALU.max)
                v.drain()
                nc.vector.tensor_scalar(rng[:, 6:7], rng[:, 4:5], rng[:, 5:6], 1e-30, ALU.max, ALU.max)
                v.drain()
                nc.vector.tensor_scalar(rng[:, 7:8].bitcast(I32), rng[:, 6:7].bitcast(I32), EXP_BITS, None, ALU.bitwise_and)
                v.drain()
                nc.vector.reciprocal(rng[:, 8:9], rng[:, 7:8])
                v.drain()
                nc.vector.tensor_scalar(rng[:, 9:10], rng[:, 8:9], F16_TOP, None, ALU.mult)
                nc.vector.tensor_scalar(rng[:, 10:11], rng[:, 8:9], -F16_TOP, None, ALU.mult)
                nc.vector.tensor_scalar(rng[:, 11:12], rng[:, 7:8], 1.0 / F16_TOP, None, ALU.mult)
                v.drain()

            def code(src, dst, scale):
                scaled, cut = flat
                nc.vector.tensor_scalar(scaled, src, scale, None, ALU.mult)
                v.drain()
                nc.vector.tensor_scalar(cut.bitcast(I32), scaled.bitcast(I32), HIGH_BITS, None, ALU.bitwise_and)
                v.drain()
                nc.vector.tensor_copy(parts(dst)[:, :, 1], cut)
                nc.vector.tensor_tensor(parts(dst)[:, :, 0], scaled, cut, ALU.subtract)
                v.drain()

            def code_half_w(par, half):
                cols = slice(half * BANK, (half + 1) * BANK)
                code(w[:, par, cols], w_code[:, par, cols], rng[:, 9:10])

            def code_signs(par):
                for odd in range(2):
                    rows = slice(odd * D, (odd + 1) * D)
                    nc.vector.tensor_scalar(signs_code[rows, par, ROWS - 2 + odd:ROWS - 1 + odd], acol[rows, 1:2],
                                            rng[rows, 11:12], None, ALU.mult)
                nc.vector.tensor_scalar(quarter[:, par, :], ones[:], acol[:, 3:4], rng[:, 11:12], ALU.mult, ALU.mult
                                        ).then_inc(sems["coded"], 1)

            def run(b, par, n, u, buf, fills, before=True, norm=False, encode=False, widen=False):
                first, count = fills
                for k in range(SETS):
                    wait(v, sems["set_summed"], SETS * u + k - BACK[k] + 1)
                    for g in range(G):
                        if g not in on_scalar(k, n):
                            last = nc.vector.tensor_scalar(ring[:, SLOT[k], g, :], w_code[:, par, :],
                                                           r_code[:, par, bass.ds(n * PAIRS + g * SETS + k, 1)], None,
                                                           ALU.max)
                    last.then_inc(sems["vector_sets"], 1)
                    if k in TAKE_AT and TAKE_AT[k] < count:
                        take_fill(b + 1, 1 - par, first + TAKE_AT[k])
                    if norm and k == 9:
                        layer_norm_mean(v, s, sems, next_norm(s, b), b + 2)
                    if norm and k == 14:
                        layer_norm_scale(v, s, sems, next_norm(s, b), b + 2)
                    if widen and k in (9, 12):
                        extremes(0, k // 12, w[:, 1 - par, :])
                    if encode and k in (0, 2):
                        extremes(1, k // 2, r[:, 1 - par, :])
                    if encode and k == 3:
                        find_range(1 - par)
                        wait(v, sems["x_added"], STARTS + 2 * b)
                    if encode and k in (4, 6):
                        code_half_w(1 - par, k // 6)
                    if encode and k == 10:
                        code(r[:, 1 - par, :], r_code[:, 1 - par, :], rng[:, 10:11])
                    if encode and k == 13:
                        code_signs(1 - par)
                    if not before:
                        continue
                    if k == MAX:
                        logit(1 - buf, u - 1)
                    if k == COPY:
                        copy_half(v, nc.vector.tensor_copy, s, sems, 0, u - 1)
                    if k == COPY_OUT:
                        copy_out(v, s, sems, u - 1)
                    if k == FINISH:
                        at_start = isinstance(n, int) and n == 0
                        finish(NB - 1 if at_start else n - 1, 1 - buf, u - 1)
                        if at_start:
                            batch_end(b - 1)

            def batch_end(b):
                v.drain()
                wait(v, sems["x_added"], STARTS + 2 * b)
                elu_parts(v, s, sems, z[:], low, high)

            def logit(buf, u):
                v.wait_ge(sems["set_summed"], SETS * (u + 1))
                v.wait_ge(sems["mask_ready"], u + 1)
                wait(v, sems["turned_ready"], STARTS + u)
                masked_max(v, s, sems, scores[buf], buf, -1.0, logits[:], s.mask[:, buf, :])

            def finish(n, slot, u):
                nc.vector.reciprocal(s.rinv[:, slot:slot + 1], s.rowsum[:, slot:slot + 1])
                v.drain()
                v.wait_ge(sems["out_turned"], u + 1)
                nc.vector.tensor_scalar(z[:, bass.ds(n, 1), :].rearrange("p a d -> p (a d)"), s.fill[:, 0:D],
                                        s.rinv[:, slot:slot + 1], None, ALU.mult).then_inc(sems["unit_done"], 1)

            def graph(b, par, project, last_graph):
                run(b, par, 1, b * NB + 1, 1, fills_of(1, project))
                with v.Fori(0, (NB - 4) // 2) as t:
                    for i in range(2):
                        run(b, par, 2 * t + 2 + i, b * NB + 2 * t + 2 + i, i, (0, 0))
                run(b, par, NB - 2, b * NB + NB - 2, 0, fills_of(NB - 2, project), widen=project)
                run(b, par, NB - 1, b * NB + NB - 1, 1, (0, 0), norm=True, encode=project)
                if not last_graph:
                    run(b + 1, 1 - par, 0, (b + 1) * NB, 0, (0, 0))

            nc.vector.memset(lwT[D:P, :], 0.0)
            nc.vector.memset(w1[D:P, :, :], 0.0)
            nc.vector.memset(w2[D:P, :, :], 0.0)
            nc.vector.memset(hpT[D:P, :], 0.0)
            nc.vector.memset(ones[:], 1.0)
            nc.vector.memset(signs[:], 0.0)
            nc.vector.memset(signs_code[:], 0.0).then_inc(sems["weights_ready"], 1)
            v.wait_ge(sems["weights_in"], 16 * 6)
            v.drain()
            nc.vector.tensor_scalar(acol[:, 1:2], acol[:, 0:1], 0.0, 2.0, ALU.is_ge, ALU.mult).then_inc(sems["weights_ready"], 1)
            v.drain()
            nc.vector.tensor_scalar(acol[:, 3:4], acol[:, 1:2], -1.0, None, ALU.add)
            v.drain()
            nc.vector.tensor_copy(acol[:, 1:2], acol[:, 3:4])
            nc.vector.scalar_tensor_tensor(out=acol[:, 2:3], in0=acol[:, 0:1], scalar=1.0 - SLOPE, in1=acol[:, 3:4],
                                           op0=ALU.mult, op1=ALU.mult)
            v.drain()
            nc.vector.tensor_scalar(acol[:, 3:4], acol[:, 1:2], SLOPE / (1.0 - SLOPE) / 2, None, ALU.mult)
            for odd in range(2):
                rows = slice(odd * D, (odd + 1) * D)
                nc.vector.tensor_copy(signs[rows, ROWS - 2 + odd:ROWS - 1 + odd], acol[rows, 1:2])
            v.wait_ge(sems["raw_turned"], 1)
            nc.vector.tensor_copy(lwT[0:D, :], s.fill[0:D, 0:D])
            for twice in range(2):
                nc.vector.tensor_copy(w1[0:D, twice, :], s.fill[0:D, D:2 * D])
                last = nc.vector.tensor_copy(w2[0:D, twice, :], s.fill[0:D, 2 * D:3 * D])
            last.then_inc(sems["weights_ready"], 1)
            for k in range(K):
                take_fill(0, 0, k)
            v.drain()
            for i, t in enumerate((w, r)):
                for part in range(2):
                    extremes(i, part, t[:, 0, :])
            find_range(0)
            for half in range(2):
                code_half_w(0, half)
            code(r[:, 0, :], r_code[:, 0, :], rng[:, 10:11])
            code_signs(0)
            run(0, 0, 0, 0, 0, (0, 0), before=False)
            with v.Fori(0, B // 2 - 1) as t:
                for par in range(2):
                    graph(2 * t + par, par, True, False)
            graph(B - 2, 0, True, False)
            graph(B - 1, 1, False, True)
            u = B * NB - 1
            logit(1, u)
            copy_half(v, nc.vector.tensor_copy, s, sems, 0, u)
            copy_out(v, s, sems, u)
            finish(NB - 1, 1, u)
            batch_end(B - 1)



def gat_layer(nc, s, w_dram, a_dram, w_res, gamma_dram, beta_dram, out):
    B, N, D, NB = s.B, s.N, s.D, s.NB
    K = 9
    with ExitStack() as ctx:
        def sb(name, shape, dt):
            return ctx.enter_context(nc.sbuf_tensor(f"l3_{name}", shape, dt))

        sems = make_sems(nc, ctx, "l3", ["relu_ready", "base_ready", "elu_parts", "elu_exp", "elu_ready", "out_mean", "out_centred",
                                         "out_square", "out_seed", "out_scaled", "x_done", "stored"])
        w = sb("w", [P, D], F32)
        wres = sb("wres", [P, D], F32)
        acol = sb("acol", [P, 2], F32)
        gamma = sb("gamma", [P, D], F32)
        beta = sb("beta", [P, D], F32)
        ones = sb("ones", [P, P], F32)
        a_dst = sb("a_dst", [P, P], F32)
        whT = sb("whT", [P, N], F32)
        dst = sb("dst", [P, 2, N], F32)
        dst_slope = sb("dst_slope", [P, 2, N], F32)
        src = sb("src", [P, 2, NB], F32)
        values = sb("values", [P, 2, NB, D], F32)
        residual = sb("residual", [P, 2, NB, D], F32)
        relu = sb("relu", [P, 2, N], F32)
        base = sb("base", [P, 2, N], F32)
        logits = sb("logits", [P, 2, N], F32)
        probs = sb("probs", [P, 2, N], F32)
        z = sb("z", [P, 2, NB, D], F32)
        low = sb("low", [P, NB, D], F32)
        high = sb("high", [P, NB, D], F32)
        work = sb("work", [P, 4, NB, D], F32)
        total = sb("total", [P, 8, NB], F32)
        unit_out = [s.scores[:, 1, i, :] for i in range(2)]
        block = ctx.enter_context(nc.Block())

        def fills_before(n):
            return min(K, (3 * n + 1) // 2)

        @block.sync
        def _(sp):
            start_sems(sp, sems, normed=True)
            sp.wait_ge(sems["weights_ready"], 1)
            for to, at in ((w[0:D, :], w_dram), (wres[0:D, :], w_res),
                           (acol[0:D, 0:1], a_dram[0:D].rearrange("(d a) -> d a", a=1)),
                           (acol[0:D, 1:2], a_dram[D:2 * D].rearrange("(d a) -> d a", a=1)),
                           (gamma[:], gamma_dram.partition_broadcast(P)), (beta[:], beta_dram.partition_broadcast(P))):
                sp.dma_start(to, at).then_inc(sems["weights_in"], 16)

            def store(b):
                sp.wait_ge(sems["x_done"], STARTS + b + 1)
                sp.dma_start(out[bass.ds(b, 1)].rearrange("a (t p) d -> p (a t) d", p=P), s.graph(b)
                             ).then_inc(sems["stored"], 16)

            def loads(b, first):
                for n in range(first, NB):
                    load_bytes(sp, s, sems, b * NB + n, n % 2)

            load_bytes(sp, s, sems, 0, 0)
            load_bytes(sp, s, sems, 1, 1)
            loads(0, 2)
            loads(1, 0)
            with sp.Fori(2, B) as b:
                loads(b, 0)
                store(b - 2)
            store(B - 2)
            store(B - 1)
            sp.wait_ge(sems["stored"], 16 * B)

        @block.gpsimd
        def _(g):
            shape = [P, NB, D]

            def mask(b, par, n):
                u = b * NB + n
                g.wait_ge(sems[f"bytes_in{n % 2}"], 16 * (b * (NB // 2) + n // 2) + 16)
                wait(g, sems["base_ready"], u)
                mask_from(g, s, sems, s.bytes[:, n % 2, :], 0)
                g.wait_ge(sems["mask_ready"], u + 1)
                g.wait_ge(sems["fill_copied"], b * K + 6)
                wait(g, sems["logits_ready"], STARTS + u - 1)
                nc.gpsimd.tensor_tensor(base[:, n % 2, :], dst_slope[:, par, :], s.mask[:, 0, :], ALU.add
                                        ).then_inc(sems["base_ready"], 1)

            def out_centre(b):
                centred, square, elu = (work[:, i, :, :] for i in range(3))
                g.wait_ge(sems["out_mean"], b + 1)
                nc.gpsimd.tensor_tensor(centred, elu, total[:, 1, :].unsqueeze(2).to_broadcast(shape), ALU.subtract
                                        ).then_inc(sems["out_centred"], 1)
                g.wait_ge(sems["out_centred"], b + 1)
                nc.gpsimd.tensor_tensor(square, centred, centred, ALU.mult).then_inc(sems["out_square"], 1)

            def out_scale(b):
                g.wait_ge(sems["out_seed"], b + 1)
                rsqrt_newton(g, s, total, total[:, 7, :])
                nc.gpsimd.tensor_tensor(work[:, 3, :, :], work[:, 0, :, :], total[:, 7, :].unsqueeze(2).to_broadcast(shape), ALU.mult
                                        ).then_inc(sems["out_scaled"], 1)

            def graph(b, par, project, norm, first=False):
                for n in range(NB):
                    if n + 3 < NB:
                        mask(b, par, n + 3)
                    elif project:
                        mask(b + 1, 1 - par, n + 3 - NB)
                    if n == 1 and not first:
                        out_centre(b - 1)
                    if n == 2 and norm:
                        layer_norm_centre(g, s, sems, next_norm(s, b), b + 2)
                    if n == 4 and not first:
                        out_scale(b - 1)
                    if n == 6 and norm:
                        layer_norm_apply(g, s, sems, next_norm(s, b), par, b + 2, b * K + 2)

            for n in range(3):
                mask(0, 0, n)
            graph(0, 0, True, True, first=True)
            with g.Fori(0, (B - 4) // 2) as t:
                for i in (1, 2):
                    graph(2 * t + i, i % 2, True, True)
            graph(B - 3, 1, True, True)
            graph(B - 2, 0, True, False)
            graph(B - 1, 1, False, False)
            out_centre(B - 1)
            out_scale(B - 1)

        @block.tensor
        def _(pe):
            def fill(b, par, k):
                bank = fill_bank(s, b, k)
                wait_for_bank(pe, s, sems, b, K, k, 0 if k < 2 else 4 if 4 <= k < 7 else 2)
                cols = slice((k % 2) * BANK, (k % 2 + 1) * BANK)
                if k < 2:
                    pe.wait_ge(sems["y_ready"], b + 1)
                    last = turn_y(pe, s, par, k, bank)
                elif k < 4:
                    last = nc.tensor.matmul(bank[0:D, :], w[:], s.hT[:, cols], start=True, stop=True)
                elif k < 6:
                    last = nc.tensor.matmul(bank[:], a_dst[:], whT[:, cols], start=True, stop=True)
                else:
                    for j in range(NB):
                        nodes = slice(j * P, (j + 1) * P)
                        if k == 6:
                            out_, lhs, rhs = bank[:, j:j + 1], whT[:, nodes], acol[:, 0:1]
                        else:
                            out_, lhs, rhs = bank[:, j * D:(j + 1) * D], s.hT[:, nodes], (w if k == 7 else wres)[:]
                        last = nc.tensor.matmul(out_, lhs, rhs, start=True, stop=True, skip_group_check=True)
                last.then_inc(sems["fill_ready"], 1)

            def graph(b, par, project, first=False):
                for n in range(NB):
                    u = b * NB + n
                    fills = list(range(fills_before(n), fills_before(n + 1))) if project else []
                    turn_probs(pe, s, sems, probs[:, n % 2, :], u)
                    if not (first and n == 0):
                        turn_out(pe, s, sems, u - 1, 0, unit_out[(n - 1) % 2], buffers=2)
                    for k in fills[:1]:
                        fill(b + 1, 1 - par, k)
                    probs_times_values(pe, s, sems, values[:, par, :, :], u)
                    for k in fills[1:]:
                        fill(b + 1, 1 - par, k)

            pe.wait_ge(sems["weights_ready"], 2)
            for k in range(K):
                fill(0, 0, k)
            graph(0, 0, True, first=True)
            with pe.Fori(0, (B - 4) // 2) as t:
                for i in (1, 2):
                    graph(2 * t + i, i % 2, True)
            graph(B - 3, 1, True)
            graph(B - 2, 0, True)
            graph(B - 1, 1, False)
            turn_out(pe, s, sems, B * NB - 1, 0, unit_out[1], buffers=2)

        @block.scalar
        def _(a):
            def dst_fill(b, par, k):
                if k in (4, 5):
                    a.wait_ge(sems["fill_ready"], b * K + k + 1)
                    nc.scalar.activation(dst[:, par, (k % 2) * BANK:(k % 2 + 1) * BANK], fill_bank(s, b, k), ACT.Copy,
                                         scale=1.0 - SLOPE).then_inc(sems["high_ready"], 1)

            def take_relu(b, par, n):
                a.wait_ge(sems["fill_copied"], b * K + 7)
                wait(a, sems["logits_ready"], STARTS + b * NB + n - 1)
                nc.scalar.activation(relu[:, n % 2, :], dst[:, par, :], ACT.Relu, bias=src[:, par, n:n + 1]
                                     ).then_inc(sems["relu_ready"], 1)

            def graph(b, par, project, first=False):
                for n in range(NB):
                    u = b * NB + n
                    copy_half(a, nc.scalar.copy, s, sems, 0, u)
                    copy_half(a, nc.scalar.copy, s, sems, 1, u)
                    if n + 1 < NB or project:
                        exponentials(a, s, sems, logits[:, (n + 1) % 2, :], probs[:, (n + 1) % 2, :], (n + 1) % 4, u + 1, 1.0)
                    if project:
                        for k in range(fills_before(n), fills_before(n + 1)):
                            dst_fill(b + 1, 1 - par, k)
                    if n + 3 < NB:
                        take_relu(b, par, n + 3)
                    elif project:
                        take_relu(b + 1, 1 - par, n + 3 - NB)
                    if n == 0 and not first:
                        elu_exp(a, s, sems, low, b - 1)

            for k in range(K):
                dst_fill(0, 0, k)
            take_relu(0, 0, 0)
            take_relu(0, 0, 1)
            exponentials(a, s, sems, logits[:, 0, :], probs[:, 0, :], 0, 0, 1.0)
            take_relu(0, 0, 2)
            graph(0, 0, True, first=True)
            with a.Fori(0, (B - 4) // 2) as t:
                for i in (1, 2):
                    graph(2 * t + i, i % 2, True)
            graph(B - 3, 1, True)
            graph(B - 2, 0, True)
            graph(B - 1, 1, False)
            elu_exp(a, s, sems, low, B - 1)

        @block.vector
        def _(v):
            def take_fill(b, par, k):
                bank = fill_bank(s, b, k)
                cols = slice((k % 2) * BANK, (k % 2 + 1) * BANK)
                if k in (4, 5):
                    v.wait_ge(sems["high_ready"], b * 2 + k - 4 + 1)
                    last = nc.vector.tensor_scalar(dst_slope[:, par, cols], bank[:], SLOPE, None, ALU.mult)
                else:
                    v.wait_ge(sems["fill_ready"], b * K + k + 1)
                    if k < 2:
                        last = nc.vector.tensor_scalar(s.hT[0:D, cols], bank[0:D, :], 0.0, None, ALU.max)
                    elif k < 4:
                        last = nc.vector.tensor_copy(whT[0:D, cols], bank[0:D, :])
                    elif k == 6:
                        last = nc.vector.tensor_scalar(src[:, par, :], bank[:, 0:NB], 1.0 - SLOPE, None, ALU.mult)
                    else:
                        to = values if k == 7 else residual
                        last = nc.vector.tensor_copy(to[:, par, :, :].rearrange("p j d -> p (j d)"), bank[:])
                last.then_inc(sems["fill_copied"], 1)

            def logit(n, u):
                v.wait_ge(sems["base_ready"], u + 1)
                v.wait_ge(sems["relu_ready"], u + 1)
                wait(v, sems["probs_ready"], u - 1)
                masked_max(v, s, sems, relu[:, n % 2, :], n % 4, -1.0, logits[:, n % 2, :], base[:, n % 2, :])

            def finish(par, n, u):
                slot = n % 4
                nc.vector.reciprocal(s.rinv[:, slot:slot + 1], s.rowsum[:, slot:slot + 1])
                v.drain()
                v.wait_ge(sems["out_turned"], u + 1)
                nc.vector.scalar_tensor_tensor(out=z[:, par, n, :], in0=unit_out[n % 2][:, 0:D], scalar=s.rinv[:, slot:slot + 1],
                                               in1=residual[:, par, n, :], op0=ALU.mult, op1=ALU.add
                                               ).then_inc(sems["unit_done"], 1)

            def out_mean(b):
                wait(v, sems["x_done"], STARTS + b)
                v.wait_ge(sems["elu_exp"], b + 1)
                nc.vector.tensor_tensor(work[:, 2, :, :], high[:], low[:], ALU.add)
                v.drain()
                nc.vector.tensor_reduce(total[:, 0, :], work[:, 2, :, :], AX.X, ALU.add)
                v.drain()
                nc.vector.tensor_scalar(total[:, 1, :], total[:, 0, :], 1.0 / D, None, ALU.mult).then_inc(sems["out_mean"], 1)

            def out_seed(b):
                v.wait_ge(sems["out_square"], b + 1)
                nc.vector.tensor_reduce(total[:, 2, :], work[:, 1, :, :], AX.X, ALU.add)
                v.drain()
                rsqrt_seed(v, s, total, total[:, 2, :]).then_inc(sems["out_seed"], 1)

            def out_add(b):
                scaled, product, total_ = (work[:, i, :, :] for i in (3, 1, 2))
                shape = [P, NB, D]
                v.wait_ge(sems["out_scaled"], b + 1)
                nc.vector.tensor_tensor(product, scaled, gamma[:].unsqueeze(1).to_broadcast(shape), ALU.mult)
                v.drain()
                nc.vector.tensor_tensor(total_, product, beta[:].unsqueeze(1).to_broadcast(shape), ALU.add)
                v.drain()
                nc.vector.tensor_tensor(s.graph(b), s.graph(b), total_, ALU.add).then_inc(sems["x_done"], 1)

            def elu(b, par):
                v.drain()
                wait(v, sems["x_done"], STARTS + b)
                elu_parts(v, s, sems, z[:, par, :, :], low, high)

            def graph(b, par, project, norm, first=False):
                for n in range(NB):
                    u = b * NB + n
                    fills = list(range(fills_before(n), fills_before(n + 1))) if project else []
                    if n > 0:
                        finish(par, n - 1, u - 1)
                    elif not first:
                        finish(1 - par, NB - 1, u - 1)
                    if n + 2 < NB or project:
                        logit((n + 2) % NB, u + 2)
                    for k in fills[:1]:
                        take_fill(b + 1, 1 - par, k)
                    copy_out(v, s, sems, u)
                    for k in fills[1:]:
                        take_fill(b + 1, 1 - par, k)
                    if n == 0 and not first:
                        elu(b - 1, 1 - par)
                    if n == 1 and not first:
                        out_mean(b - 1)
                    if n == 1 and norm:
                        layer_norm_mean(v, s, sems, next_norm(s, b), b + 2)
                    if n == 3 and not first:
                        out_seed(b - 1)
                    if n == 6 and not first:
                        out_add(b - 1)
                    if n == 4 and norm:
                        layer_norm_scale(v, s, sems, next_norm(s, b), b + 2)

            nc.vector.memset(w[D:P, :], 0.0)
            nc.vector.memset(wres[D:P, :], 0.0)
            nc.vector.memset(acol[:], 0.0)
            nc.vector.memset(ones[:], 1.0)
            nc.vector.memset(whT[D:P, :], 0.0).then_inc(sems["weights_ready"], 1)
            v.wait_ge(sems["weights_in"], 16 * 6)
            v.drain()
            nc.vector.tensor_scalar(a_dst[:], ones[:], acol[:, 1:2], None, ALU.mult).then_inc(sems["weights_ready"], 1)
            for k in range(K):
                take_fill(0, 0, k)
            v.drain()
            logit(0, 0)
            logit(1, 1)
            graph(0, 0, True, True, first=True)
            with v.Fori(0, (B - 4) // 2) as t:
                for i in (1, 2):
                    graph(2 * t + i, i % 2, True, True)
            graph(B - 3, 1, True, True)
            graph(B - 2, 0, True, False)
            graph(B - 1, 1, False, False)
            finish(1, NB - 1, B * NB - 1)
            elu(B - 1, 1)
            out_mean(B - 1)
            out_seed(B - 1)
            out_add(B - 1)



def gnn_stack(nc, x, adj, L0_gnn_W_q, L0_gnn_W_k, L0_gnn_W_v, L1_gnn_Wv, L1_gnn_bv, L1_gnn_Wq, L1_gnn_bq,
              L1_gnn_Wk, L1_gnn_bk, L2_gnn_lin_w, L2_gnn_lin_b, L2_gnn_W_w, L2_gnn_a, L3_gnn_W, L3_gnn_a,
              L3_gnn_W_res, L3_gnn_gamma, L3_gnn_beta, out):
    B, N, D = x.shape
    H = L1_gnn_Wq.shape[0]
    with ExitStack() as ctx:
        s = Shared(nc, ctx, B, N, D)
        constants(nc, s)
        dot_layer(nc, s, "l0", 1, [w.rearrange("(h i) o -> h i o", h=1) for w in (L0_gnn_W_q, L0_gnn_W_k, L0_gnn_W_v)],
                  None, adj, x)
        dot_layer(nc, s, "l1", H, [L1_gnn_Wq, L1_gnn_Wk, L1_gnn_Wv],
                  [L1_gnn_bq, L1_gnn_bk, L1_gnn_bv])
        additive_layer(nc, s, L2_gnn_lin_w, L2_gnn_lin_b, L2_gnn_W_w, L2_gnn_a)
        gat_layer(nc, s, L3_gnn_W, L3_gnn_a, L3_gnn_W_res, L3_gnn_gamma, L3_gnn_beta, out)


def constants(nc, s):
    with nc.semaphore("zeroed") as zeroed, nc.semaphore("ones_ready") as ones_ready, nc.Block() as block:
        @block.vector
        def _(v):
            nc.vector.memset(s.ident[:], 0.0).then_inc(zeroed, 1)
            v.wait_ge(ones_ready, 2)
            nc.vector.tensor_tensor(s.add_halves[:], s.ident[:, 0:s.D], s.ident[:, s.D:2 * s.D], ALU.add)

        @block.gpsimd
        def _(g):
            g.wait_ge(zeroed, 1)
            nc.gpsimd.affine_select(out=s.ident[:], in_=s.ident[:], compare_op=ALU.not_equal, fill=1.0, base=0,
                                    pattern=[[-1, P]], channel_multiplier=1).then_inc(ones_ready, 2)


_INS = ["x", "adj", "L0_gnn_W_q", "L0_gnn_W_k", "L0_gnn_W_v", "L1_gnn_Wv", "L1_gnn_bv", "L1_gnn_Wq", "L1_gnn_bq",
        "L1_gnn_Wk", "L1_gnn_bk", "L2_gnn_lin_w", "L2_gnn_lin_b", "L2_gnn_W_w", "L2_gnn_a", "L3_gnn_W", "L3_gnn_a",
        "L3_gnn_W_res", "L3_gnn_gamma", "L3_gnn_beta"]


def kernel(**inputs):
    import numpy as np
    import concourse.bacc as bacc
    from concourse.bass_utils import run_bass_kernel_spmd

    nc = bacc.Bacc("TRN2", target_bir_lowering=False, num_devices=1)
    arrays = {name: np.ascontiguousarray(inputs[name]) for name in _INS}
    args = [nc.dram_tensor(name, a.shape, mybir.dt.from_np(a.dtype), kind="ExternalInput").ap()
            for name, a in arrays.items()]
    out = nc.dram_tensor("out", arrays["x"].shape, F32, kind="ExternalOutput").ap()
    gnn_stack(nc, *args, out)
    result = run_bass_kernel_spmd(nc, [arrays], core_ids=[0])
    return result.results[0]["out"]
```
